# Optimizing a Trainium2 kernel written in Bass

```python
import numpy as np
import jax
import jax.numpy as jnp

def _softmax(x, axis=-1):
    return jax.nn.softmax(x, axis=axis)

def _gelu(x):
    return jax.nn.gelu(x, approximate=True)

def _silu(x):
    return jax.nn.silu(x)

def _sigmoid(x):
    return jax.nn.sigmoid(x)

def _layernorm(x, axis=-1, eps=1e-05):
    m = jnp.mean(x, axis=axis, keepdims=True)
    v = jnp.var(x, axis=axis, keepdims=True)
    return (x - m) / jnp.sqrt(v + eps)

def _scatter_add(tgt, idx, src, axis=0):
    return tgt.at[idx].add(src)

def _segment_sum(src, seg, n):
    return jax.ops.segment_sum(src, seg, n)
kernel_name = 'mk_decoder_preln_d2_seqx_r8_4ebad8'

def setup_inputs(seed: int=0):
    np.random.seed(seed)
    _w = jnp.asarray

    def _rec_inputs():
        import jax
        import jax.numpy as jnp
        _rk = jax.random.key(seed)
        x = -0.0003929 + 0.9999 * jax.random.normal(jax.random.fold_in(_rk, 1), (2, 512, 128), jnp.float32)
        _lenS = 512 - jax.random.randint(jax.random.fold_in(_rk, 7), (2,), 0, max(1, 512 // 4) + 1, jnp.int32)
        _lenS2 = 154 - jax.random.randint(jax.random.fold_in(_rk, 8), (2,), 0, max(1, 154 // 4) + 1, jnp.int32)
        _ctx_1024P = jax.random.normal(jax.random.fold_in(_rk, 11), (2, 16, 128), jnp.float32)
        _ctx_1024c = jax.random.dirichlet(jax.random.fold_in(_rk, 511), 0.3 * jnp.ones((16,), jnp.float32), (2, 154))
        _ctx_1024t = jnp.einsum('bsk,bkd->bsd', _ctx_1024c, _ctx_1024P)
        _ctx_1024t = _ctx_1024t * jax.lax.rsqrt(jnp.mean(jnp.square(_ctx_1024t)) + 1e-12) * 0.953939
        ctx_1024 = 4.13588e-05 + 0.999923 * (_ctx_1024t + 0.3 * jax.random.normal(jax.random.fold_in(_rk, 611), (2, 154, 128), jnp.float32))
        _validS = jnp.arange(512)[None, :] < _lenS[:, None]
        _validS2 = jnp.arange(154)[None, :] < _lenS2[:, None]
        _causal = jnp.tril(jnp.ones((512, 512), dtype=bool))
        mask_BxS_bf1 = jnp.ones((2, 512), dtype=bool)
        mask_1x1xSxS2_bk1 = jnp.broadcast_to(_validS2[0:1, None, None, :], (1, 1, 512, 154))
        return (x, ctx_1024, mask_BxS_bf1, mask_1x1xSxS2_bk1)
    x, ctx_1024, mask_BxS_bf1, mask_1x1xSxS2_bk1 = _rec_inputs()

    def _L0_attn_setup():
        import jax, jax.numpy as jnp
        import numpy as np
        N, S, D_IN, ATTN_DIM, OUT_DIM = (4, 1024, 128, 128, 128)
        key = jax.random.key(seed)
        ks = jax.random.split(key, 6)
        scale_in = 1.0 / np.sqrt(D_IN)
        scale_attn = 1.0 / np.sqrt(ATTN_DIM)
        return {'x': jax.random.normal(ks[0], (N, S, D_IN), dtype=jnp.float32), 'wq': jax.random.normal(ks[1], (D_IN, ATTN_DIM), dtype=jnp.float32) * scale_in, 'bq': jnp.zeros((ATTN_DIM,), dtype=jnp.float32), 'wk': jax.random.normal(ks[2], (D_IN, ATTN_DIM), dtype=jnp.float32) * scale_in, 'bk': jnp.zeros((ATTN_DIM,), dtype=jnp.float32), 'wv': jax.random.normal(ks[3], (D_IN, ATTN_DIM), dtype=jnp.float32) * scale_in, 'bv': jnp.zeros((ATTN_DIM,), dtype=jnp.float32), 'wo': jax.random.normal(ks[4], (ATTN_DIM, OUT_DIM), dtype=jnp.float32) * scale_attn, 'bo': jnp.zeros((OUT_DIM,), dtype=jnp.float32)}
    _L0_attn_all = _L0_attn_setup()
    _L0_attn_in = {k: v for k, v in _L0_attn_all.items() if k in ('wq', 'bq', 'wk', 'bk', 'wv', 'bv', 'wo', 'bo')}
    del _L0_attn_all

    def _L0_xattn_setup():
        import jax, jax.numpy as jnp
        import numpy as np
        DIM = 128
        DEPTH = 4
        HEADS = 8
        DH = 64
        INNER = HEADS * DH
        FF = 4 * DIM
        ROT = 32
        B, CHUNK, SEQ = (128, 128, 64)

        def rope_freqs(n, rot_dim):
            inv = 1.0 / 10000.0 ** (jnp.arange(0, rot_dim, 2, dtype=jnp.float32) / rot_dim)
            freqs = jnp.arange(n, dtype=jnp.float32)[:, None] * inv[None, :]
            return jnp.concatenate([freqs, freqs], axis=-1)

        def apply_rope(t, freqs):
            rot = freqs.shape[-1]
            t1, tp = (t[..., :rot], t[..., rot:])
            d2 = rot // 2
            rh = jnp.concatenate([-t1[..., d2:], t1[..., :d2]], axis=-1)
            t1 = t1 * jnp.cos(freqs) + rh * jnp.sin(freqs)
            return jnp.concatenate([t1, tp], axis=-1)

        def rmsnorm(x, gamma, eps=1e-08):
            n = jnp.sqrt(jnp.sum(x * x, axis=-1, keepdims=True)) * x.shape[-1] ** (-0.5)
            return x / jnp.maximum(n, eps) * gamma

        def attn_block(xq, ctx, Wq, Wk, Wv, Wo, bo, pe_q, pe_k, mask):
            b, n, _ = xq.shape
            j = ctx.shape[1]
            q = (xq @ Wq).reshape(b, n, HEADS, DH).transpose(0, 2, 1, 3)
            k = (ctx @ Wk).reshape(b, j, HEADS, DH).transpose(0, 2, 1, 3)
            v = (ctx @ Wv).reshape(b, j, HEADS, DH).transpose(0, 2, 1, 3)
            q = q * DH ** (-0.5)
            q = apply_rope(q, pe_q)
            k = apply_rope(k, pe_k)
            sim = jnp.einsum('bhid,bhjd->bhij', q, k)
            if mask is not None:
                sim = jnp.where(mask[:, None, None, :], sim, -jnp.finfo(sim.dtype).max)
            a = jax.nn.softmax(sim, axis=-1)
            out = jnp.einsum('bhij,bhjd->bhid', a, v)
            out = out.transpose(0, 2, 1, 3).reshape(b, n, INNER)
            return out @ Wo + bo
        key = jax.random.key(seed)
        ks = jax.random.split(key, 16)
        g = lambda k, shape: 0.02 * jax.random.normal(k, shape, dtype=jnp.float32)
        inp = {'x': jax.random.normal(ks[0], (B, CHUNK, DIM), dtype=jnp.float32), 'chunked_seq': jax.random.normal(ks[1], (B, SEQ, DIM), dtype=jnp.float32), 'mask': jnp.ones((B, CHUNK), dtype=bool), 'sWq': g(ks[2], (DEPTH, DIM, INNER)), 'sWk': g(ks[3], (DEPTH, DIM, INNER)), 'sWv': g(ks[4], (DEPTH, DIM, INNER)), 'sWo': g(ks[5], (DEPTH, INNER, DIM)), 'sbo': jnp.zeros((DEPTH, DIM), jnp.float32), 'sg': jnp.ones((DEPTH, DIM), jnp.float32), 'cWq': g(ks[6], (DEPTH, DIM, INNER)), 'cWk': g(ks[7], (DEPTH, DIM, INNER)), 'cWv': g(ks[8], (DEPTH, DIM, INNER)), 'cWo': g(ks[9], (DEPTH, INNER, DIM)), 'cbo': jnp.zeros((DEPTH, DIM), jnp.float32), 'cg': jnp.ones((DEPTH, DIM), jnp.float32), 'fW1': g(ks[10], (DEPTH, DIM, FF)), 'fb1': jnp.zeros((DEPTH, FF), jnp.float32), 'fW2': g(ks[11], (DEPTH, FF, DIM)), 'fb2': jnp.zeros((DEPTH, DIM), jnp.float32), 'fg': jnp.ones((DEPTH, DIM), jnp.float32), 'g_out': jnp.ones((DIM,), jnp.float32)}
        return inp
    _L0_xattn_all = _L0_xattn_setup()
    _L0_xattn_in = {k: v for k, v in _L0_xattn_all.items() if k in ('sWq', 'sWk', 'sWv', 'sWo', 'sbo', 'sg', 'cWq', 'cWk', 'cWv', 'cWo', 'cbo', 'cg', 'fW1', 'fb1', 'fW2', 'fb2', 'fg', 'g_out')}
    del _L0_xattn_all

    def _L0_ffn_setup():
        import jax, jax.numpy as jnp
        import numpy as np
        TOP_P = 0.8
        B, T, H, F, E = (2, 256, 128, 512, 8)
        key = jax.random.key(seed)
        k0, k1, k2, k3 = jax.random.split(key, 4)
        x = jax.random.normal(k0, (B, T, H), jnp.float32)
        Wr = jax.random.normal(k1, (H, E), jnp.float32) * 0.02
        br = jnp.zeros((E,), jnp.float32)
        W1 = jax.random.normal(k2, (E, H, F), jnp.float32) * 0.02
        b1 = jnp.zeros((E, F), jnp.float32)
        W2 = jax.random.normal(k3, (E, F, H), jnp.float32) * 0.02
        b2 = jnp.zeros((E, H), jnp.float32)
        return {'x': x, 'Wr': Wr, 'br': br, 'W1': W1, 'b1': b1, 'W2': W2, 'b2': b2}
    _L0_ffn_all = _L0_ffn_setup()
    _L0_ffn_in = {k: v for k, v in _L0_ffn_all.items() if k in ('Wr', 'br', 'W1', 'b1', 'W2', 'b2')}
    del _L0_ffn_all

    def _L1_attn_setup():
        import jax, jax.numpy as jnp
        import numpy as np
        B, T, D = (4, 512, 128)
        EPS = 1e-06
        key = jax.random.key(seed)
        ks = jax.random.split(key, 9)
        s = 0.02
        f32 = jnp.float32
        return {'x_seq': jax.random.normal(ks[0], (B, T, D), f32), 'W_q': jax.random.normal(ks[1], (D, D), f32) * s, 'b_q': jax.random.normal(ks[2], (D,), f32) * s, 'W_k': jax.random.normal(ks[3], (D, D), f32) * s, 'b_k': jax.random.normal(ks[4], (D,), f32) * s, 'W_v': jax.random.normal(ks[5], (D, D), f32) * s, 'b_v': jax.random.normal(ks[6], (D,), f32) * s, 'W_a': jax.random.normal(ks[7], (D, D), f32) * s, 'b_a': jax.random.normal(ks[8], (D,), f32) * s}
    _L1_attn_all = _L1_attn_setup()
    _L1_attn_in = {k: v for k, v in _L1_attn_all.items() if k in ('W_q', 'b_q', 'W_k', 'b_k', 'W_v', 'b_v', 'W_a', 'b_a')}
    del _L1_attn_all

    def _L1_xattn_setup():
        import jax, jax.numpy as jnp
        import numpy as np
        D_MODEL = 128
        NUM_HEADS = 16
        D_K = D_MODEL // NUM_HEADS
        B, S = (4, 256)
        key = jax.random.key(seed)
        ks = jax.random.split(key, 12)
        sd = 1.0 / np.sqrt(D_MODEL)
        inp = {'query': jax.random.normal(ks[0], (B, S, D_MODEL), jnp.float32), 'key': jax.random.normal(ks[1], (B, S, D_MODEL), jnp.float32), 'value': jax.random.normal(ks[2], (B, S, D_MODEL), jnp.float32), 'mask': jnp.triu(jnp.ones((S, S), jnp.bool_), k=1)[None, None], 'Wq': jax.random.normal(ks[3], (D_MODEL, D_MODEL), jnp.float32) * sd, 'bq': jnp.zeros((D_MODEL,), jnp.float32), 'Wk': jax.random.normal(ks[4], (D_MODEL, D_MODEL), jnp.float32) * sd, 'bk': jnp.zeros((D_MODEL,), jnp.float32), 'Wv': jax.random.normal(ks[5], (D_MODEL, D_MODEL), jnp.float32) * sd, 'bv': jnp.zeros((D_MODEL,), jnp.float32), 'Wo': jax.random.normal(ks[6], (D_MODEL, D_MODEL), jnp.float32) * sd, 'bo': jnp.zeros((D_MODEL,), jnp.float32)}
        return inp
    _L1_xattn_all = _L1_xattn_setup()
    _L1_xattn_in = {k: v for k, v in _L1_xattn_all.items() if k in ('Wq', 'bq', 'Wk', 'bk', 'Wv', 'bv', 'Wo', 'bo')}
    del _L1_xattn_all

    def _L1_ffn_setup():
        import jax, jax.numpy as jnp
        import numpy as np
        B, T, D = (4, 512, 128)
        E = 8
        TOP_K = 2
        FFN = 384
        HALF = FFN // 2

        def _kaiming_uniform(key, shape, fan_in):
            bound = 1.0 / np.sqrt(fan_in)
            return jax.random.uniform(key, shape, jnp.float32, -bound, bound)
        key = jax.random.key(seed)
        ks = jax.random.split(key, 7)
        x = jax.random.normal(ks[0], (B, T, D), jnp.float32)
        gate_w = _kaiming_uniform(ks[1], (E, D), D) * 0.01
        w_up = _kaiming_uniform(ks[2], (E, FFN, D), D)
        w_down = _kaiming_uniform(ks[3], (E, D, HALF), HALF)
        sg_gate = _kaiming_uniform(ks[4], (HALF, D), D)
        sg_up = _kaiming_uniform(ks[5], (HALF, D), D)
        sg_down = _kaiming_uniform(ks[6], (D, HALF), HALF)
        return {'x': x, 'gate_w': gate_w, 'w_up': w_up, 'w_down': w_down, 'sg_gate': sg_gate, 'sg_up': sg_up, 'sg_down': sg_down}
    _L1_ffn_all = _L1_ffn_setup()
    _L1_ffn_in = {k: v for k, v in _L1_ffn_all.items() if k in ('gate_w', 'w_up', 'w_down', 'sg_gate', 'sg_up', 'sg_down')}
    del _L1_ffn_all
    return {'x': x, 'ctx_1024': ctx_1024, 'mask_BxS_bf1': mask_BxS_bf1, 'mask_1x1xSxS2_bk1': mask_1x1xSxS2_bk1, 'L0_attn_wq': _L0_attn_in['wq'], 'L0_attn_bq': _L0_attn_in['bq'], 'L0_attn_wk': _L0_attn_in['wk'], 'L0_attn_bk': _L0_attn_in['bk'], 'L0_attn_wv': _L0_attn_in['wv'], 'L0_attn_bv': _L0_attn_in['bv'], 'L0_attn_wo': _L0_attn_in['wo'], 'L0_attn_bo': _L0_attn_in['bo'], 'L0_xattn_sWq': _L0_xattn_in['sWq'], 'L0_xattn_sWk': _L0_xattn_in['sWk'], 'L0_xattn_sWv': _L0_xattn_in['sWv'], 'L0_xattn_sWo': _L0_xattn_in['sWo'], 'L0_xattn_sbo': _L0_xattn_in['sbo'], 'L0_xattn_sg': _L0_xattn_in['sg'], 'L0_xattn_cWq': _L0_xattn_in['cWq'], 'L0_xattn_cWk': _L0_xattn_in['cWk'], 'L0_xattn_cWv': _L0_xattn_in['cWv'], 'L0_xattn_cWo': _L0_xattn_in['cWo'], 'L0_xattn_cbo': _L0_xattn_in['cbo'], 'L0_xattn_cg': _L0_xattn_in['cg'], 'L0_xattn_fW1': _L0_xattn_in['fW1'], 'L0_xattn_fb1': _L0_xattn_in['fb1'], 'L0_xattn_fW2': _L0_xattn_in['fW2'], 'L0_xattn_fb2': _L0_xattn_in['fb2'], 'L0_xattn_fg': _L0_xattn_in['fg'], 'L0_xattn_g_out': _L0_xattn_in['g_out'], 'L0_ffn_Wr': _L0_ffn_in['Wr'], 'L0_ffn_br': _L0_ffn_in['br'], 'L0_ffn_W1': _L0_ffn_in['W1'], 'L0_ffn_b1': _L0_ffn_in['b1'], 'L0_ffn_W2': _L0_ffn_in['W2'], 'L0_ffn_b2': _L0_ffn_in['b2'], 'L1_attn_W_q': _L1_attn_in['W_q'], 'L1_attn_b_q': _L1_attn_in['b_q'], 'L1_attn_W_k': _L1_attn_in['W_k'], 'L1_attn_b_k': _L1_attn_in['b_k'], 'L1_attn_W_v': _L1_attn_in['W_v'], 'L1_attn_b_v': _L1_attn_in['b_v'], 'L1_attn_W_a': _L1_attn_in['W_a'], 'L1_attn_b_a': _L1_attn_in['b_a'], 'L1_xattn_Wq': _L1_xattn_in['Wq'], 'L1_xattn_bq': _L1_xattn_in['bq'], 'L1_xattn_Wk': _L1_xattn_in['Wk'], 'L1_xattn_bk': _L1_xattn_in['bk'], 'L1_xattn_Wv': _L1_xattn_in['Wv'], 'L1_xattn_bv': _L1_xattn_in['bv'], 'L1_xattn_Wo': _L1_xattn_in['Wo'], 'L1_xattn_bo': _L1_xattn_in['bo'], 'L1_ffn_gate_w': _L1_ffn_in['gate_w'], 'L1_ffn_w_up': _L1_ffn_in['w_up'], 'L1_ffn_w_down': _L1_ffn_in['w_down'], 'L1_ffn_sg_gate': _L1_ffn_in['sg_gate'], 'L1_ffn_sg_up': _L1_ffn_in['sg_up'], 'L1_ffn_sg_down': _L1_ffn_in['sg_down']}

def reference(x, ctx_1024, mask_BxS_bf1, mask_1x1xSxS2_bk1, L0_attn_wq, L0_attn_bq, L0_attn_wk, L0_attn_bk, L0_attn_wv, L0_attn_bv, L0_attn_wo, L0_attn_bo, L0_xattn_sWq, L0_xattn_sWk, L0_xattn_sWv, L0_xattn_sWo, L0_xattn_sbo, L0_xattn_sg, L0_xattn_cWq, L0_xattn_cWk, L0_xattn_cWv, L0_xattn_cWo, L0_xattn_cbo, L0_xattn_cg, L0_xattn_fW1, L0_xattn_fb1, L0_xattn_fW2, L0_xattn_fb2, L0_xattn_fg, L0_xattn_g_out, L0_ffn_Wr, L0_ffn_br, L0_ffn_W1, L0_ffn_b1, L0_ffn_W2, L0_ffn_b2, L1_attn_W_q, L1_attn_b_q, L1_attn_W_k, L1_attn_b_k, L1_attn_W_v, L1_attn_b_v, L1_attn_W_a, L1_attn_b_a, L1_xattn_Wq, L1_xattn_bq, L1_xattn_Wk, L1_xattn_bk, L1_xattn_Wv, L1_xattn_bv, L1_xattn_Wo, L1_xattn_bo, L1_ffn_gate_w, L1_ffn_w_up, L1_ffn_w_down, L1_ffn_sg_gate, L1_ffn_sg_up, L1_ffn_sg_down):
    import jax
    import jax.numpy as jnp

    def _L0_attn_ref(x, wq, bq, wk, bk, wv, bv, wo, bo):
        import jax, jax.numpy as jnp
        import numpy as np
        N, S, D_IN, ATTN_DIM, OUT_DIM = (4, 1024, 128, 128, 128)
        query = x @ wq + bq
        key_ = x @ wk + bk
        value = x @ wv + bv
        Q = jax.nn.elu(query) + 1.0
        K = jax.nn.elu(key_) + 1.0
        KV = jnp.einsum('nsh,nsh->nh', K, value, precision='highest')
        Ksum = jnp.sum(K, axis=1)
        Z = 1.0 / (Q * Ksum[:, None, :] + 1e-06)
        V = Q * KV[:, None, :] * Z
        out = V @ wo + bo
        return jax.nn.gelu(out, approximate=True)

    def _L0_xattn_ref(x, chunked_seq, mask, sWq, sWk, sWv, sWo, sbo, sg, cWq, cWk, cWv, cWo, cbo, cg, fW1, fb1, fW2, fb2, fg, g_out):
        import jax, jax.numpy as jnp
        import numpy as np
        DIM = 128
        DEPTH = 4
        HEADS = 8
        DH = 64
        INNER = HEADS * DH
        FF = 4 * DIM
        ROT = 32
        B, CHUNK, SEQ = (128, 128, 64)

        def rope_freqs(n, rot_dim):
            inv = 1.0 / 10000.0 ** (jnp.arange(0, rot_dim, 2, dtype=jnp.float32) / rot_dim)
            freqs = jnp.arange(n, dtype=jnp.float32)[:, None] * inv[None, :]
            return jnp.concatenate([freqs, freqs], axis=-1)

        def apply_rope(t, freqs):
            rot = freqs.shape[-1]
            t1, tp = (t[..., :rot], t[..., rot:])
            d2 = rot // 2
            rh = jnp.concatenate([-t1[..., d2:], t1[..., :d2]], axis=-1)
            t1 = t1 * jnp.cos(freqs) + rh * jnp.sin(freqs)
            return jnp.concatenate([t1, tp], axis=-1)

        def rmsnorm(x, gamma, eps=1e-08):
            n = jnp.sqrt(jnp.sum(x * x, axis=-1, keepdims=True)) * x.shape[-1] ** (-0.5)
            return x / jnp.maximum(n, eps) * gamma

        def attn_block(xq, ctx, Wq, Wk, Wv, Wo, bo, pe_q, pe_k, mask):
            b, n, _ = xq.shape
            j = ctx.shape[1]
            q = (xq @ Wq).reshape(b, n, HEADS, DH).transpose(0, 2, 1, 3)
            k = (ctx @ Wk).reshape(b, j, HEADS, DH).transpose(0, 2, 1, 3)
            v = (ctx @ Wv).reshape(b, j, HEADS, DH).transpose(0, 2, 1, 3)
            q = q * DH ** (-0.5)
            q = apply_rope(q, pe_q)
            k = apply_rope(k, pe_k)
            sim = jnp.einsum('bhid,bhjd->bhij', q, k)
            if mask is not None:
                sim = jnp.where(mask[:, None, None, :], sim, -jnp.finfo(sim.dtype).max)
            a = jax.nn.softmax(sim, axis=-1)
            out = jnp.einsum('bhij,bhjd->bhid', a, v)
            out = out.transpose(0, 2, 1, 3).reshape(b, n, INNER)
            return out @ Wo + bo
        pe_q = rope_freqs(x.shape[1], ROT)
        pe_k = rope_freqs(chunked_seq.shape[1], ROT)
        for l in range(DEPTH):
            h = rmsnorm(x, sg[l])
            x = attn_block(h, h, sWq[l], sWk[l], sWv[l], sWo[l], sbo[l], pe_q, pe_q, mask) + x
            h = rmsnorm(x, cg[l])
            x = attn_block(h, chunked_seq, cWq[l], cWk[l], cWv[l], cWo[l], cbo[l], pe_q, pe_k, None) + x
            h = rmsnorm(x, fg[l])
            x = jax.nn.gelu(h @ fW1[l] + fb1[l], approximate=False) @ fW2[l] + fb2[l] + x
        return rmsnorm(x, g_out)

    def _L0_ffn_ref(x, Wr, br, W1, b1, W2, b2):
        import jax, jax.numpy as jnp
        import numpy as np
        TOP_P = 0.8
        B, T, H, F, E = (2, 256, 128, 512, 8)
        probs = jax.nn.softmax(x @ Wr + br, axis=-1)
        sorted_idx = jnp.argsort(-probs, axis=-1)
        sorted_probs = jnp.take_along_axis(probs, sorted_idx, axis=-1)
        cum = jnp.cumsum(sorted_probs, axis=-1)
        mask = cum < TOP_P
        mask = mask.at[..., 0].set(True)
        inv = jnp.argsort(sorted_idx, axis=-1)
        keep = jnp.take_along_axis(mask, inv, axis=-1)
        gate = probs * keep
        h = jax.nn.relu(jnp.einsum('bth,ehf->betf', x, W1) + b1[None, :, None, :])
        y = jnp.einsum('betf,efh->beth', h, W2) + b2[None, :, None, :]
        return jnp.einsum('bte,beth->bth', gate, y)

    def _L1_attn_ref(x_seq, W_q, b_q, W_k, b_k, W_v, b_v, W_a, b_a):
        import jax, jax.numpy as jnp
        import numpy as np
        B, T, D = (4, 512, 128)
        EPS = 1e-06
        q = jax.nn.relu(x_seq @ W_q.T + b_q)
        k = jax.nn.relu(x_seq @ W_k.T + b_k)
        v = x_seq @ W_v.T + b_v
        A = jax.nn.sigmoid(x_seq @ W_a.T + b_a)
        log_g = jax.lax.cumsum(jnp.log(A + 1e-06), axis=1, reverse=True)
        wk = k * jnp.exp(log_g)
        scores = jnp.einsum('btd,bsd->bts', q, wk)
        Tn = x_seq.shape[1]
        mask = jnp.tril(jnp.ones((Tn, Tn), bool))
        scores = jnp.where(mask, scores, 0.0)
        num = jnp.einsum('bts,bsd->btd', scores, v)
        denom = scores.sum(-1, keepdims=True) + EPS
        return num / denom

    def _L1_xattn_ref(query, key, value, mask, Wq, bq, Wk, bk, Wv, bv, Wo, bo):
        import jax, jax.numpy as jnp
        import numpy as np
        D_MODEL = 128
        NUM_HEADS = 16
        D_K = D_MODEL // NUM_HEADS
        B, S = (4, 256)
        b = query.shape[0]
        Q = query @ Wq.T + bq
        K = key @ Wk.T + bk
        V = value @ Wv.T + bv

        def split(x):
            return x.reshape(b, -1, NUM_HEADS, D_K).transpose(0, 2, 1, 3)
        Q, K, V = (split(Q), split(K), split(V))
        scores = jnp.einsum('bhqd,bhkd->bhqk', Q, K) / jnp.sqrt(jnp.float32(D_K))
        scores = jnp.where(mask, -jnp.inf, scores)
        attn_w = jax.nn.softmax(scores, axis=-1)
        attn_w = jnp.where(jnp.isnan(attn_w), 0.0, attn_w)
        out = jnp.einsum('bhqk,bhkd->bhqd', attn_w, V)
        out = out.transpose(0, 2, 1, 3).reshape(b, -1, D_MODEL)
        return out @ Wo.T + bo

    def _L1_ffn_ref(x, gate_w, w_up, w_down, sg_gate, sg_up, sg_down):
        import jax, jax.numpy as jnp
        import numpy as np
        B, T, D = (4, 512, 128)
        E = 8
        TOP_K = 2
        FFN = 384
        HALF = FFN // 2

        def _kaiming_uniform(key, shape, fan_in):
            bound = 1.0 / np.sqrt(fan_in)
            return jax.random.uniform(key, shape, jnp.float32, -bound, bound)
        b, t, d = x.shape
        xf = x.reshape(b * t, d)
        N = xf.shape[0]
        logits = xf @ gate_w.T
        topk_logits, topk_idx = jax.lax.top_k(logits, TOP_K)
        topk_w = jax.nn.softmax(topk_logits.astype(jnp.float32), axis=-1).astype(x.dtype)
        comb = jnp.zeros((N, E), x.dtype).at[jnp.arange(N)[:, None], topk_idx].add(topk_w)
        wg = w_up[:, :HALF, :]
        wu = w_up[:, HALF:, :]
        out = jnp.zeros_like(xf)
        for e in range(E):
            g = xf @ wg[e].T
            u = xf @ wu[e].T
            y = jax.nn.silu(g) * u @ w_down[e].T
            out = out + comb[:, e:e + 1] * y
        shared = jax.nn.silu(xf @ sg_gate.T) * (xf @ sg_up.T) @ sg_down.T
        return (shared + out).reshape(b, t, d)
    x = x + _L0_attn_ref(_layernorm(x, axis=-1), L0_attn_wq, L0_attn_bq, L0_attn_wk, L0_attn_bk, L0_attn_wv, L0_attn_bv, L0_attn_wo, L0_attn_bo)
    x = x + _L0_xattn_ref(_layernorm(x, axis=-1), ctx_1024, mask_BxS_bf1, L0_xattn_sWq, L0_xattn_sWk, L0_xattn_sWv, L0_xattn_sWo, L0_xattn_sbo, L0_xattn_sg, L0_xattn_cWq, L0_xattn_cWk, L0_xattn_cWv, L0_xattn_cWo, L0_xattn_cbo, L0_xattn_cg, L0_xattn_fW1, L0_xattn_fb1, L0_xattn_fW2, L0_xattn_fb2, L0_xattn_fg, L0_xattn_g_out)
    x = x + _L0_ffn_ref(_layernorm(x, axis=-1), L0_ffn_Wr, L0_ffn_br, L0_ffn_W1, L0_ffn_b1, L0_ffn_W2, L0_ffn_b2)
    x = x + _L1_attn_ref(_layernorm(x, axis=-1), L1_attn_W_q, L1_attn_b_q, L1_attn_W_k, L1_attn_b_k, L1_attn_W_v, L1_attn_b_v, L1_attn_W_a, L1_attn_b_a)
    x = x + _L1_xattn_ref(_layernorm(x, axis=-1), ctx_1024, ctx_1024, mask_1x1xSxS2_bk1, L1_xattn_Wq, L1_xattn_bq, L1_xattn_Wk, L1_xattn_bk, L1_xattn_Wv, L1_xattn_bv, L1_xattn_Wo, L1_xattn_bo)
    x = x + _L1_ffn_ref(_layernorm(x, axis=-1), L1_ffn_gate_w, L1_ffn_w_up, L1_ffn_w_down, L1_ffn_sg_gate, L1_ffn_sg_up, L1_ffn_sg_down)
    return x

_drawn_inputs = setup_inputs


def setup_inputs(seed=0):
    import zlib

    import numpy as np

    out = dict(_drawn_inputs(seed))
    spreads = {'L0_attn_bq': (0.0, 2.0),
     'L0_attn_bk': (0.0, 0.8),
     'L0_attn_bv': (0.0, 0.1),
     'L0_attn_bo': (0.0, 0.1),
     'L0_xattn_sbo': (0.0, 0.1),
     'L0_xattn_sg': (1.0, 0.6),
     'L0_xattn_cbo': (0.0, 0.1),
     'L0_xattn_cg': (1.0, 0.6),
     'L0_xattn_fb1': (0.0, 0.379),
     'L0_xattn_fb2': (0.0, 0.1),
     'L0_xattn_fg': (1.0, 0.6),
     'L0_xattn_g_out': (1.0, 0.2),
     'L0_ffn_br': (0.0, 0.74),
     'L0_ffn_b1': (0.0, 0.8),
     'L0_ffn_b2': (0.0, 0.52),
     'L1_xattn_bq': (0.0, 0.494),
     'L1_xattn_bk': (0.0, 2.0),
     'L1_xattn_bv': (0.0, 0.1),
     'L1_xattn_bo': (0.0, 0.1)}
    factors = {'L0_attn_wq': 8.0,
     'L0_xattn_sWq': 8.0,
     'L0_xattn_sWk': 8.0,
     'L0_xattn_cWq': 8.0,
     'L0_xattn_cWk': 8.0,
     'L0_ffn_Wr': 5.011,
     'L0_ffn_W1': 5.298,
     'L0_ffn_W2': 4.232,
     'L1_attn_W_q': 8.0,
     'L1_attn_b_q': 64.0,
     'L1_attn_W_k': 8.0,
     'L1_attn_b_k': 64.0,
     'L1_attn_W_v': 4.303,
     'L1_attn_b_v': 25.116,
     'L1_attn_W_a': 8.0,
     'L1_attn_b_a': 8.0}
    for name, (base, spread) in spreads.items():
        noise = np.random.default_rng([zlib.crc32(name.encode()), seed]).standard_normal(out[name].shape)
        drawn = base * np.exp(spread * noise) if base else spread * noise
        out[name] = jnp.asarray(drawn.astype(out[name].dtype))
    for name, factor in factors.items():
        out[name] = (out[name] * factor).astype(out[name].dtype)
    return out
```

```python
import concourse.bass as bass
from concourse import mybir
from contextlib import ExitStack

F32 = mybir.dt.float32
BF16 = mybir.dt.bfloat16
U8 = mybir.dt.uint8
ALU = mybir.AluOpType
ACT = mybir.ActivationFunctionType
AX = mybir.AxisListType

P = 128
B, S, D = 2, 512, 128
NT = B * S
TB = S // P
TILES = B * TB
C = 154
CH = C // 2
LAYERS, HEADS, DH = 4, 8, 64
PAIRS = HEADS // 2
INNER = HEADS * DH
FF, FCH = 512, 512 // P
E = 8
F0, F0CH = 512, 512 // P
HALF = 192
HP = HALF // 2
H1, DK = 16, 8
SPLITS = 6
SCALE = DH ** -0.5
NEG = -float(2.0 ** 100)
GUARD = 1.0e29

LAYER = dict(
    var_ready=6, rstd_ready=6, normed=6, hT_full=6, hT_ready=6, y_free=6,
    proj_full=28, roped=28, rope_ready=28, qk_low_ready=28,
    v_full=12, v_ready=12,
    max_full=64 + 32, max_done=64 + 32, shift_ready=4, shiftT_full=4, shiftT_ready=4,
    scores_full=64 + 32, probs_ready=64 + 32, pv_full=32, heads_ready=32,
    out_full=6, y_ready=6, up_full=8, up_ready=8,
    w_self=80, w_sout=16, w_cross=80, w_cout=16, w_ff1=16, w_ff2=16, w_small=32, dve_step=64,
)
EXPERTS0 = dict(moe_up_full=16, moe_up_ready=16, moe_down_full=4, moe_x_ready=4, w_expert0=48, w_expert1=48)
EXPERTS1 = dict(glu_gate_full=8, glu_up_full=8, glu_act=8, glu_ready=8, glu_down_full=4, glu_x_ready=4,
                w_glu0=32, w_glu1=32)


class Seen:

    def __init__(self):
        self.n, self.turn, self.per = {}, None, {}

    def at(self, sem, n):
        per = self.per.get(sem.name, 0) if self.turn is not None else 0
        return n + self.turn * per if per else n

    def now(self, sem):
        return self.at(sem, self.n[sem.name])

    def expect(self, sem, k=1):
        self.n[sem.name] = self.n.get(sem.name, 0) + k
        return self.n[sem.name]

    def next(self, sem, k=1):
        return self.at(sem, self.expect(sem, k))

    def enter(self, turn, per):
        self.turn, self.per, self.start = turn, per, dict(self.n)

    def leave(self, turns):
        for name, n in self.n.items():
            more = n - self.start.get(name, 0)
            if more:
                assert more == self.per.get(name), (name, more)
                self.n[name] = self.start.get(name, 0) + more * turns
        self.turn, self.per = None, {}


def decoder(nc, a, out):
    ctx = ExitStack()
    with ctx:
        def sb(name, shape, dt=F32):
            return ctx.enter_context(nc.sbuf_tensor(name, shape, dt))

        def sem(name):
            return ctx.enter_context(nc.semaphore(name))

        bank = [ctx.enter_context(nc.psum_tensor(f"bank{i}", [P, 512], F32)) for i in range(8)]

        x = sb("x", [P, TILES, D])
        y = sb("y", [P, TILES, D])
        nx = sb("nx", [P, TILES, D])
        stats = sb("stats", [P, TILES, 6])
        mv = sb("mv", [P, TILES, 2])
        var = sb("var", [P, TILES])
        rstd = sb("rstd", [P, TILES])
        neghalf = sb("neghalf", [P, TILES])
        hT = sb("hT", [P, NT])
        QT = sb("QT", [P, PAIRS, NT])
        KT = sb("KT", [P, PAIRS, NT])
        Qb = sb("Qb", [P, PAIRS, NT], BF16)
        Kb = sb("Kb", [P, PAIRS, NT], BF16)
        KTc = sb("KTc", [P, PAIRS, B * C])
        Kbc = sb("Kbc", [P, PAIRS, B * C], BF16)
        Vs = sb("Vs", [P, TILES, HEADS, P])
        Vc = Vs[0:CH, 0:2 * B]
        probs = sb("probs", [P, 2, 4, 512])
        AT = sb("AT", [P, PAIRS, NT])
        rot = sb("rot", [P, 2, 2, 512])
        rec = sb("rec", [P, 512])

        mx = sb("mx", [P, TB, H1])
        shift = sb("shift", [P, TB, H1])
        shl = sb("shl", [P, TB, 2 * H1], BF16)
        shiftT = sb("shiftT", [2 * H1, B, S], BF16)
        sel = sb("sel", [2 * HEADS, HEADS, P], BF16)
        wq = sb("wq", [P, INNER]); wqr = sb("wqr", [P, INNER])
        wk = sb("wk", [P, INNER]); wkr = sb("wkr", [P, INNER])
        wv = sb("wv", [P, INNER]); wo = sb("wo", [P, PAIRS, D])
        cq = sb("cq", [P, INNER]); cqr = sb("cqr", [P, INNER])
        ck = sb("ck", [P, INNER]); ckr = sb("ckr", [P, INNER])
        cv = sb("cv", [P, INNER]); co = sb("co", [P, PAIRS, D])
        f1 = sb("f1", [P, FF]); f2 = sb("f2", [P, FCH, D])
        lcol = sb("lcol", [P, 3 + FCH])
        lrow = sb("lrow", [P, 3, D])
        ident = sb("ident", [P, P]); identb = sb("identb", [P, P], BF16)
        triu = sb("triu", [P, P])
        cos = sb("cos", [P, S]); sin = sb("sin", [P, S])
        maskrow = sb("maskrow", [P, NT], BF16)
        maskc8 = sb("maskc8", [P, TILES], U8); maskcol = sb("maskcol", [P, TILES])
        maskq = sb("maskq", [P, TB, C], BF16); maskT = sb("maskT", [CH, 2, S], BF16)
        ctxT = sb("ctxT", [P, B * C])
        ones = sb("ones", [1, P])
        cols = sb("cols", [P, 8])
        rows = sb("rows", [1, 3, D])
        brow = sb("brow", [P, 3, D])
        lrow8 = sb("lrow8", [1, E])
        wa = sb("wa", [P, 4, D])
        wr = sb("wr", [P, 2, E])
        tri8 = sb("tri8", [P, E, E])

        gates = sb("gates", [P, 2, TILES, E])
        b2e = sb("b2e", [E, D])

        cin = probs[0:CH, 0, :, 0:D]
        maskr8 = probs[:, 1, 0, 0:NT // 4].bitcast(U8)
        m1u8 = probs[:, 1, 1, 0:TB * C // 4].bitcast(U8).rearrange("p (t c) -> p t c", t=TB)
        elu = rot
        q0T, k0T, v0T = QT[:, 0, :], QT[:, 1, :], QT[:, 2, :]
        o0T, z0T, g0 = QT[:, 3, :], KT[:, 0, :], KT[:, 1, :]
        kv = mx[:, 0, :]
        ew1, ew2, eb1 = [wq, wqr], [wk, wkr], [wv[:, 0:F0CH], wv[:, F0CH:2 * F0CH]]
        gate0, gate1 = gates[:, 0], gates[:, 1]
        gateT = rot[0:E, 0, :, :].rearrange("p a c -> p (a c)")
        cmp1 = KT[:, 0, 0:512].rearrange("p (t e j) -> p t e j", e=E, j=E)
        cmp2 = KT[:, 1, 0:512].rearrange("p (t e j) -> p t e j", e=E, j=E)

        def small(i):
            return KT[:, 2, 64 * i:64 * i + 64].rearrange("p (t e) -> p t e", e=E)
        cnt, csum, ex, keep, centred, logits = (small(i) for i in range(6))
        row = KT[:, 2, 512:512 + TILES]
        rcx = KT[:, 2, 576:592]
        w1a = cq[:, :].rearrange("p (a n) -> p a n", a=4)
        AG, LG, CS, EX = (QT[:, i, :] for i in range(4))
        q1T, k1T = KT[:, 0, :], KT[:, 1, :]
        VsF = Vs[:, :, :, :].rearrange("p t h c -> p (t h c)")
        V1 = VsF[:, 0:TILES * 130].rearrange("p (t c) -> p t c", c=130)
        SC = VsF[:, 2048:4096].rearrange("p (t c) -> p t c", t=TB)
        ones_row = VsF[:, 4096:4096 + S]
        w1x = ck[:, :].rearrange("p (a n) -> p a n", a=4)
        Qst = VsF.bitcast(BF16).rearrange("p (h t) -> p h t", h=H1)
        Kst = AT[:, :, :].rearrange("p a c -> p (a c)").bitcast(BF16)[:, 0:H1 * B * C].rearrange("p (h t) -> p h t", h=H1)
        Vx = KT[0:CH, :, :].rearrange("p a c -> p (a c)")[:, 2048:4096].rearrange("p (i h c) -> p i h c", i=2 * B, h=H1)
        qparts = [Qb[:, i, :] for i in range(3)]
        kparts = [Kb[:, i, 0:B * C] for i in range(3)]
        SPL = QT[:, 0, 0:512]
        OX = QT[:, 1, 0:512].rearrange("p (t c) -> p t c", t=TB)
        OXT = QT[:, 2, 0:512]
        O4 = [QT[:, 3, 0:512], QT[:, 3, 512:1024]]
        gup = [cqr, ckr, f1]
        gdn = [w.rearrange("p (c n) -> p c n", c=2) for w in (cv[0:HP, 0:2 * D], cv[0:HP, 2 * D:4 * D])]
        gdn.append(co[0:HP, 0:2, :])
        GS = probs[0:HP, 0, :, :].rearrange("p (b c) n -> p b c n", b=B)
        GA = probs[0:HP, 1, :, :].rearrange("p (b c) n -> p b c n", b=B)

        class q:
            const = sem("const")
            x_in = sem("x_in")
            w_early = sem("w_early")
            small_in = sem("small_in")
            ctx_in = sem("ctx_in")
            mask_in = sem("mask_in")
            w_self = sem("w_self")
            w_sout = sem("w_sout")
            w_cross = sem("w_cross")
            w_cout = sem("w_cout")
            w_ff1 = sem("w_ff1")
            w_ff2 = sem("w_ff2")
            w_small = sem("w_small")
            w_expert0 = sem("w_expert0")
            w_expert1 = sem("w_expert1")
            w_l1 = sem("w_l1")
            w_glu0 = sem("w_glu0")
            w_glu1 = sem("w_glu1")
            var_ready = sem("var_ready")
            rstd_ready = sem("rstd_ready")
            normed = sem("normed")
            hT_full = sem("hT_full")
            hT_ready = sem("hT_ready")
            y_free = sem("y_free")
            ctx_full = sem("ctx_full")
            ctx_ready = sem("ctx_ready")
            mask_ready = sem("mask_ready")
            maskT_full = sem("maskT_full")
            maskT_ready = sem("maskT_ready")
            lin_full = sem("lin_full")
            lin_min = sem("lin_min")
            lin_exp = sem("lin_exp")
            lin_add = sem("lin_add")
            lin_ready = sem("lin_ready")
            gelu_full = sem("gelu_full")
            gelu_ready = sem("gelu_ready")
            x_ready = sem("x_ready")
            proj_full = sem("proj_full")
            roped = sem("roped")
            rope_ready = sem("rope_ready")
            qk_low_ready = sem("qk_low_ready")
            v_full = sem("v_full")
            v_ready = sem("v_ready")
            max_full = sem("max_full")
            max_done = sem("max_done")
            shift_ready = sem("shift_ready")
            shiftT_full = sem("shiftT_full")
            shiftT_ready = sem("shiftT_ready")
            scores_full = sem("scores_full")
            probs_ready = sem("probs_ready")
            pv_full = sem("pv_full")
            heads_ready = sem("heads_ready")
            out_full = sem("out_full")
            y_ready = sem("y_ready")
            up_full = sem("up_full")
            up_ready = sem("up_ready")
            router_full = sem("router_full")
            logits_read = sem("logits_read")
            route_min = sem("route_min")
            route_exp = sem("route_exp")
            gate_ready = sem("gate_ready")
            gateT_full = sem("gateT_full")
            gateT_ready = sem("gateT_ready")
            bias_full = sem("bias_full")
            moe_up_full = sem("moe_up_full")
            moe_up_ready = sem("moe_up_ready")
            moe_down_full = sem("moe_down_full")
            moe_x_ready = sem("moe_x_ready")
            decay_full = sem("decay_full")
            log_ready = sem("log_ready")
            sums_ready = sem("sums_ready")
            decay_ready = sem("decay_ready")
            qkv_full = sem("qkv_full")
            qkv_ready = sem("qkv_ready")
            sc_full = sem("sc_full")
            sc_ready = sem("sc_ready")
            num_full = sem("num_full")
            num_ready = sem("num_ready")
            xkq_full = sem("xkq_full")
            parts_ready = sem("parts_ready")
            parts_out = sem("parts_out")
            parts_in = sem("parts_in")
            xv_full = sem("xv_full")
            xv_ready = sem("xv_ready")
            kst_one = sem("kst_one")
            xm_full = sem("xm_full")
            xm_done = sem("xm_done")
            xsh_ready = sem("xsh_ready")
            xshT_full = sem("xshT_full")
            xshT_ready = sem("xshT_ready")
            xsh_out = sem("xsh_out")
            xsh_in0 = sem("xsh_in0")
            xsh_in1 = sem("xsh_in1")
            xs_full = sem("xs_full")
            xp_ready = sem("xp_ready")
            xpv_full = sem("xpv_full")
            xo_ready = sem("xo_ready")
            xt_full = sem("xt_full")
            xn_ready = sem("xn_ready")
            xo_full = sem("xo_full")
            xoT_ready = sem("xoT_ready")
            xout_full = sem("xout_full")
            glu_gate_full = sem("glu_gate_full")
            glu_up_full = sem("glu_up_full")
            glu_act = sem("glu_act")
            glu_ready = sem("glu_ready")
            glu_down_full = sem("glu_down_full")
            glu_x_ready = sem("glu_x_ready")
            stored = sem("stored")
            dve_step = sem("dve_step")
            dve_passed = sem("dve_passed")
            sp_passed = sem("sp_passed")
            pool_step = sem("pool_step")
            act_step = sem("act_step")
        dram_q = nc.dram_tensor("dram_q", [3, P, NT], BF16)
        dram_k = nc.dram_tensor("dram_k", [3, P, B * C], BF16)
        dram_s = nc.dram_tensor("dram_s", [B, 2 * H1, S], BF16)

        block = ctx.enter_context(nc.Block())

        @block.sync
        def _(sp):
            see = Seen()
            sp.dma_start(x[:, :, :], a["x"].rearrange("b (t p) d -> p (b t) d", p=P)).then_inc(q.x_in, 16)
            sp.dma_start(wa[:, :, :], a["wa"].rearrange("a p n -> p a n")).then_inc(q.w_early, 16)
            sp.dma_start(cols[:, :], a["cols"]).then_inc(q.w_early, 16)
            sp.dma_start(rows[:, :, :], a["rows"].rearrange("(o a) n -> o a n", o=1)).then_inc(q.small_in, 16)
            sp.dma_start(lrow8[:, :], a["br"].rearrange("(o n) -> o n", o=1)).then_inc(q.small_in, 16)
            sp.dma_start(brow[:, :, :], a["brow"].partition_broadcast(P)).then_inc(q.small_in, 16)
            sp.dma_start(wr[:, :, :], a["wr"].rearrange("a p n -> p a n")).then_inc(q.small_in, 16)
            sp.dma_start(tri8[:, :, :], a["tri8"].partition_broadcast(P)).then_inc(q.small_in, 16)
            sp.dma_start(b2e[:, :], a["b2"]).then_inc(q.small_in, 16)
            for t, name in ((cos, "cos"), (sin, "sin")):
                sp.dma_start(t[:, :], a[name]).then_inc(q.small_in, 16)
            sp.dma_start(sel[:, :, :], a["sel"]).then_inc(q.small_in, 16)
            sp.dma_start(cin, a["ctx"].rearrange("b (t p) d -> p (b t) d", p=CH)).then_inc(q.ctx_in, 16)
            sp.dma_start(maskr8, a["mask1"].rearrange("b s -> (b s)").partition_broadcast(P)).then_inc(q.mask_in, 16)
            sp.dma_start(maskc8[:, :], a["mask1c"]).then_inc(q.mask_in, 16)
            sp.dma_start(m1u8, a["mask2"].rearrange("(t p) c -> p t c", p=P)).then_inc(q.mask_in, 16)
            with sp.Fori(0, LAYERS) as l:
                sp.wait_ge(q.up_ready, l * LAYER["up_ready"])
                sp.sem_inc(q.sp_passed, 1)
                sp.wait_ge(q.y_free, l * LAYER["y_free"])
                sp.sem_inc(q.sp_passed, 1)
                sp.dma_start(lcol[:, :], a["lcol"][l]).then_inc(q.w_small, 16)
                sp.dma_start(lrow[:, :, :], a["lrow"][l].partition_broadcast(P)).then_inc(q.w_small, 16)
                sp.wait_ge(q.v_ready, l * LAYER["v_ready"])
                sp.sem_inc(q.sp_passed, 1)
                sp.wait_ge(q.roped, l * LAYER["roped"])
                sp.sem_inc(q.sp_passed, 1)
                for t, name in ((wq, "sWq"), (wqr, "sWqr"), (wk, "sWk"), (wkr, "sWkr"), (wv, "sWv")):
                    sp.dma_start(t[:, :], a[name][l]).then_inc(q.w_self, 16)
                sp.wait_ge(q.y_ready, l * LAYER["y_ready"])
                sp.sem_inc(q.sp_passed, 1)
                sp.dma_start(wo[:, :, :], a["sWo"][l].rearrange("(c p) n -> p c n", p=P)).then_inc(q.w_sout, 16)
                for t, name in ((cq, "cWq"), (cqr, "cWqr"), (ck, "cWk"), (ckr, "cWkr"), (cv, "cWv")):
                    sp.dma_start(t[:, :], a[name][l]).then_inc(q.w_cross, 16)
                sp.dma_start(co[:, :, :], a["cWo"][l].rearrange("(c p) n -> p c n", p=P)).then_inc(q.w_cout, 16)
                sp.dma_start(f1[:, :], a["fW1"][l]).then_inc(q.w_ff1, 16)
                sp.dma_start(f2[:, :, :], a["fW2"][l].rearrange("(c p) n -> p c n", p=P)).then_inc(q.w_ff2, 16)
            sp.wait_ge(q.y_ready, LAYERS * LAYER["y_ready"])
            sp.dma_start(w1a, a["w1a"].rearrange("a p n -> p a n")).then_inc(q.w_l1, 16)
            sp.dma_start(w1x, a["w1x"].rearrange("a p n -> p a n")).then_inc(q.w_l1, 16)
            sp.dma_start(gup[2][:, 0:2 * HALF], a["sgu"]).then_inc(q.w_l1, 16)
            sp.dma_start(gdn[2], a["sgd"].rearrange("(c p) n -> p c n", p=HP)).then_inc(q.w_l1, 16)

            def load_expert0(k, e):
                w = (q.w_expert0, q.w_expert1)[k]
                sp.dma_start(ew1[k][:, :], a["W1"][e]).then_inc(w, 16)
                sp.dma_start(ew2[k][:, :].rearrange("p (c n) -> p c n", c=F0CH),
                             a["W2"][e].rearrange("(c p) n -> p c n", p=P)).then_inc(w, 16)
                sp.dma_start(eb1[k], a["b1"][e]).then_inc(w, 16)

            def load_expert1(k, e):
                w = (q.w_glu0, q.w_glu1)[k]
                sp.dma_start(gup[k][:, 0:2 * HALF], a["wup"][e]).then_inc(w, 16)
                sp.dma_start(gdn[k], a["wdn"][e].rearrange("(c p) n -> p c n", p=HP)).then_inc(w, 16)

            for k in range(2):
                load_expert0(k, k)
                load_expert1(k, k)
            with sp.Fori(1, E // 2) as i:
                for k in range(2):
                    sp.wait_ge(q.moe_x_ready, i * 4 - 2 + 2 * k)
                    sp.sem_inc(q.sp_passed, 1)
                    load_expert0(k, i * 2 + k)
            sp.wait_ge(q.parts_ready, 1)
            sp.dma_start(dram_k[:, :, :].rearrange("a p t -> p a t"), Kb[:, 0:3, 0:B * C]).then_inc(q.parts_out, 16)
            sp.wait_ge(q.parts_ready, 3)
            sp.dma_start(dram_q[:, :, :].rearrange("a p t -> p a t"), Qb[:, 0:3, :]).then_inc(q.parts_out, 16)
            sp.wait_ge(q.parts_out, 32)
            sp.wait_ge(q.kst_one, 1)
            for i, (kp, qp) in enumerate(((0, 0), (0, 1), (1, 0), (1, 1), (0, 2), (2, 0))):
                r = slice(i * DK, (i + 1) * DK)
                sp.dma_start(Kst[r, :, :], dram_k[kp].rearrange("(h d) t -> d h t", d=DK)).then_inc(q.parts_in, 16)
                sp.dma_start(Qst[r, :, :], dram_q[qp].rearrange("(h d) t -> d h t", d=DK)).then_inc(q.parts_in, 16)
            for b in range(B):
                sp.wait_ge(q.xshT_ready, b + 1)
                sp.dma_start(dram_s[b], shiftT[:, b, :]).then_inc(q.xsh_out, 16)
                sp.wait_ge(q.xsh_out, 16 * (b + 1))
                sp.dma_start(Qst[SPLITS * DK:SPLITS * DK + 2, :, b * S:(b + 1) * S],
                             dram_s[b].rearrange("(a h) t -> a h t", a=2)).then_inc((q.xsh_in0, q.xsh_in1)[b], 16)
            with sp.Fori(1, E // 2) as i:
                for k in range(2):
                    sp.wait_ge(q.glu_x_ready, i * 4 - 2 + 2 * k)
                    sp.sem_inc(q.sp_passed, 1)
                    load_expert1(k, i * 2 + k)
            for b in range(B):
                sp.wait_ge(q.glu_x_ready, 4 * (E // 2) + b + 1)
                sp.dma_start(out.rearrange("b (t p) d -> p (b t) d", p=P)[:, b * TB:(b + 1) * TB, :],
                             x[:, b * TB:(b + 1) * TB, :]).then_inc(q.stored, 16)
            sp.wait_ge(q.stored, 32)

        @block.gpsimd
        def _(pool):
            see = Seen()
            g = nc.gpsimd
            g.memset(ident[:, :], 0.0)
            g.memset(triu[:, :], 1.0)
            g.memset(neghalf[:, :], -0.5)
            g.memset(ones[:, :], 1.0).then_inc(q.pool_step, 1)
            pool.wait_ge(q.pool_step, see.next(q.pool_step))
            g.affine_select(out=ident[:, :], in_=ident[:, :], compare_op=ALU.not_equal, fill=1.0, base=0,
                            pattern=[[-1, P]], channel_multiplier=1).then_inc(q.pool_step, 1)
            g.affine_select(out=triu[:, :], in_=triu[:, :], compare_op=ALU.is_ge, fill=0.0, base=0,
                            pattern=[[1, P]], channel_multiplier=-1).then_inc(q.const, 1)
            pool.wait_ge(q.pool_step, see.next(q.pool_step))
            g.tensor_copy(identb[:, :], ident[:, :]).then_inc(q.const, 1)
            for h in range(HEADS):
                one = slice(DH, P) if h % 2 == 0 else slice(0, DH)
                ins = g.memset(Vs[:, :, h, one], 1.0)
            ins.then_inc(q.const, 1)


            def power():
                pool.wait_ge(q.var_ready, see.next(q.var_ready))
                b = (see.n["var_ready"] - 1) % B
                g.tensor_tensor(rstd[:, b * TB:(b + 1) * TB], var[:, b * TB:(b + 1) * TB],
                                neghalf[:, 0:TB], ALU.pow).then_inc(q.rstd_ready, 1)

            def add_bias(k):
                for b in range(B):
                    pool.wait_ge(q.normed, see.next(q.normed))
                    if b == 0:
                        pool.wait_ge(q.w_small, see.now(q.w_small))
                    v = y[:, b * TB:(b + 1) * TB, :]
                    g.tensor_tensor(v, v, lrow[:, k:k + 1, :].broadcast_to([P, TB, D]), ALU.add).then_inc(q.y_free, 1)

            def rope_sum(dst, w):
                pool.wait_ge(q.roped, see.next(q.roped))
                n = see.n["roped"] - 1
                r = rot[:, n % 2]
                g.tensor_tensor(dst, r[:, 0, 0:w], r[:, 1, 0:w], ALU.add).then_inc(q.rope_ready, 1)

            def norm_powers(bias=None):
                for b in range(B):
                    power()
                if bias is not None:
                    add_bias(bias)

            norm_powers()
            see.expect(q.normed, 2)
            norm_powers()
            see.expect(q.normed, 2)
            with pool.Fori(0, LAYERS) as l:
                see.enter(l, LAYER)
                see.expect(q.w_small, 32)
                norm_powers(0)
                for b in range(B):
                    for t in (KT, QT):
                        for j in range(PAIRS):
                            rope_sum(t[:, j, b * S:(b + 1) * S], S)
                for j in range(PAIRS):
                    rope_sum(KTc[:, j, :], B * C)
                norm_powers(1)
                for b in range(B):
                    for j in range(PAIRS):
                        rope_sum(QT[:, j, b * S:(b + 1) * S], S)
                norm_powers(2)
                see.leave(LAYERS)
            norm_powers()
            norm_powers()
            norm_powers()
            norm_powers()
            g.memset(Kst[0:DH, :, :], 1.0).then_inc(q.kst_one, 1)
            norm_powers()

        @block.vector
        def _(dve):
            see = Seen()
            v = nc.vector

            def link(ins):
                ins.then_inc(q.dve_step, 1)
                dve.wait_ge(q.dve_step, see.next(q.dve_step))

            def alone():
                if see.turn is not None:
                    dve.sem_inc(q.dve_passed, 1)

            def norm(src, dst, rms=False, last=q.normed):
                for b in range(B):
                    ts = range(b * TB, (b + 1) * TB)
                    w = slice(b * TB, (b + 1) * TB)
                    for t in ts:
                        ins = v.bn_stats(stats[:, t, :], src[:, t, :])
                    link(ins)
                    alone()
                    for t in ts:
                        ins = v.bn_aggr(mv[:, t, :], stats[:, t, :])
                    link(ins)
                    if rms:
                        link(v.tensor_tensor(var[:, w], mv[:, w, 0], mv[:, w, 0], ALU.mult))
                        link(v.tensor_tensor(var[:, w], var[:, w], mv[:, w, 1], ALU.add))
                        v.tensor_scalar(var[:, w], var[:, w], 1.0e-16, None, ALU.max).then_inc(q.var_ready, 1)
                    else:
                        v.tensor_scalar(var[:, w], mv[:, w, 1], 1.0e-5, None, ALU.add).then_inc(q.var_ready, 1)
                for b in range(B):
                    dve.wait_ge(q.rstd_ready, see.next(q.rstd_ready))
                    for t in range(b * TB, (b + 1) * TB):
                        if rms:
                            ins = v.tensor_scalar(dst[:, t, :], src[:, t, :], rstd[:, t:t + 1], None, ALU.mult)
                        else:
                            ins = v.tensor_scalar(dst[:, t, :], src[:, t, :], mv[:, t, 0:1], rstd[:, t:t + 1],
                                                  ALU.subtract, ALU.mult)
                    ins.then_inc(last, 1)

            def masks():
                dve.wait_ge(q.mask_in, see.next(q.mask_in, 48))
                v.tensor_scalar(maskrow[:, :], maskr8, 1.0, -NEG, ALU.subtract, ALU.mult)
                v.tensor_scalar(maskcol[:, :], maskc8[:, :], 1.0, -NEG * SCALE, ALU.subtract, ALU.mult)
                v.tensor_scalar(maskq[:, :, :], m1u8, NEG, None, ALU.mult).then_inc(q.mask_ready, 1)

            def linear_attention():
                for b in range(B):
                    w = slice(b * S, (b + 1) * S)
                    for k in range(2):
                        dve.wait_ge(q.lin_full, see.next(q.lin_full))
                        src, col = bank[3 * b + k], cols[:, k:k + 1]
                        v.tensor_scalar(elu[:, k, 0, :], src[:, :], col, 0.0, ALU.add, ALU.min).then_inc(q.lin_min, 1)
                        v.tensor_scalar(elu[:, k, 1, :], src[:, :], col, 0.0, ALU.add, ALU.max).then_inc(q.dve_step, 1)
                        see.expect(q.dve_step)
                    dve.wait_ge(q.lin_full, see.next(q.lin_full))
                    link(v.tensor_scalar(v0T[:, w], bank[3 * b + 2][:, :], cols[:, 2:3], None, ALU.add))
                    for k in range(2):
                        dve.wait_ge(q.lin_exp, see.next(q.lin_exp))
                        o = (q0T, k0T)[k][:, w]
                        link(v.scalar_tensor_tensor(out=o, in0=elu[:, k, 0, :], scalar=-1.0, in1=elu[:, k, 1, :],
                                                    op0=ALU.add, op1=ALU.add))
                        link(v.tensor_scalar(o, o, 1.0, None, ALU.add))
                    link(v.tensor_tensor_reduce(z0T[:, w], k0T[:, w], v0T[:, w], 1.0, 0.0, ALU.mult, ALU.add, kv[:, 2 * b:2 * b + 1]))
                    link(v.tensor_reduce(kv[:, 2 * b + 1:2 * b + 2], k0T[:, w], AX.X, ALU.add))
                    link(v.tensor_scalar(z0T[:, w], q0T[:, w], kv[:, 2 * b + 1:2 * b + 2], 1.0e-6, ALU.mult, ALU.add))
                    link(v.reciprocal(z0T[:, w], z0T[:, w]))
                    v.scalar_tensor_tensor(out=o0T[:, w], in0=q0T[:, w], scalar=kv[:, 2 * b:2 * b + 1], in1=z0T[:, w],
                                           op0=ALU.mult, op1=ALU.mult).then_inc(q.lin_ready, 1)
                for b in range(B):
                    dve.wait_ge(q.gelu_ready, see.next(q.gelu_ready))
                    w = slice(b * TB, (b + 1) * TB)
                    link(v.tensor_tensor(x[:, w, :], x[:, w, :],
                                         g0[:, b * S:(b + 1) * S].rearrange("p (t d) -> p t d", d=D), ALU.add))

            def rope(w, batches):
                see.expect(q.proj_full)
                dve.wait_ge(q.proj_full, see.now(q.proj_full))
                n = see.n["proj_full"] - 1
                src = [bank[2 + 2 * (n % 2) + k][:, 0:w] for k in range(2)]
                if n >= 2:
                    dve.wait_ge(q.rope_ready, see.at(q.rope_ready, n - 1))
                for k, tab in enumerate((cos, sin)):
                    i, o, tb = src[k], rot[:, n % 2, k, 0:w], tab[:, :]
                    if batches:
                        i = i.rearrange("p (b c) -> p b c", b=B)
                        o = o.rearrange("p (b c) -> p b c", b=B)
                        tb = tab[:, 0:C].unsqueeze(1).broadcast_to([P, B, C])
                    ins = v.tensor_tensor(o, i, tb, ALU.mult)
                ins.then_inc(q.roped, 1)
                see.expect(q.rope_ready)

            def maxima_self(b, h):
                for t in range(TB):
                    dve.wait_ge(q.max_full, see.next(q.max_full))
                    alone()
                    n = see.n["max_full"] - 1
                    v.tensor_tensor_reduce(bank[n % 2][:, :], bank[n % 2][:, :], maskrow[:, b * S:(b + 1) * S], 1.0, -3.0e38,
                                           ALU.add, ALU.max, mx[:, t, h:h + 1]).then_inc(q.max_done, 1)

            def maxima_cross(b, h):
                for t in range(0, TB, 2):
                    dve.wait_ge(q.max_full, see.next(q.max_full))
                    n = see.n["max_full"] - 1
                    v.tensor_reduce(mx[:, t:t + 2, h:h + 1], bank[n % 2][:, 0:2 * C].rearrange("p (a c) -> p a c", a=2),
                                    AX.X, ALU.max).then_inc(q.max_done, 1)

            def shifts(heads, done, ready, clamp=None):
                dve.wait_ge(done, see.now(done))
                if clamp is None:
                    link(v.tensor_scalar(shift[:, :, 0:heads], mx[:, :, 0:heads], -1.0, None, ALU.mult))
                else:
                    link(v.tensor_scalar(shift[:, :, 0:heads], mx[:, :, 0:heads], -1.0, clamp, ALU.mult, ALU.min))
                link(v.tensor_copy(shl[:, :, 0:heads], shift[:, :, 0:heads]))
                v.tensor_tensor(shl[:, :, heads:2 * heads], shift[:, :, 0:heads], shl[:, :, 0:heads],
                                ALU.subtract).then_inc(ready, 1)

            def shifts_turned(n, b, full, ready, src):
                dve.wait_ge(full, see.next(full))
                v.tensor_copy(shiftT[0:n, b, :], src[0:n, 0:S // 2].bitcast(BF16)).then_inc(ready, 1)

            def normalise(b, h):
                dve.wait_ge(q.pv_full, see.next(q.pv_full))
                n = see.n["pv_full"] - 1
                o = bank[4 + n % 2]
                val, den = (slice(0, DH), slice(DH, P)) if h % 2 == 0 else (slice(DH, P), slice(0, DH))
                link(v.reciprocal(rec[val, :], o[den, :]))
                v.tensor_tensor(AT[val, h // 2, b * S:(b + 1) * S], o[val, :], rec[val, :], ALU.mult).then_inc(q.heads_ready, 1)

            def residual(b):
                dve.wait_ge(q.out_full, see.next(q.out_full))
                dve.wait_ge(q.y_free, see.next(q.y_free))
                w = y[:, b * TB:(b + 1) * TB, :]
                v.tensor_tensor(w, bank[6 + b][:, :].rearrange("p (t d) -> p t d", d=D), w, ALU.add).then_inc(q.y_ready, 1)
                see.expect(q.y_ready)

            def attend(maxima, nmax):
                for b in range(B):
                    for h in range(HEADS):
                        if b == 0:
                            see.expect(q.max_done, 0)
                            maxima(1, h)
                            see.expect(q.max_done, nmax)
                        if h:
                            normalise(b, h - 1)
                    if b == 0:
                        shifts(HEADS, q.max_done, q.shift_ready)
                    normalise(b, HEADS - 1)
                    if b == 0:
                        shifts_turned(2 * HEADS, 1, q.shiftT_full, q.shiftT_ready, bank[6])
                    residual(b)

            def layer():
                norm(y, nx, True)
                for _ in range(2 * PAIRS):
                    rope(S, False)
                for h in range(HEADS):
                    maxima_self(0, h)
                    see.expect(q.max_done, TB)
                    rope(S, False)
                shifts(HEADS, q.max_done, q.shift_ready)
                shifts_turned(2 * HEADS, 0, q.shiftT_full, q.shiftT_ready, bank[6])
                attend(maxima_self, TB)
                for j in range(PAIRS):
                    rope(B * C, True)
                dve.wait_ge(q.y_ready, see.now(q.y_ready))
                norm(y, nx, True)
                for j in range(2 * PAIRS):
                    rope(S, False)
                for h in range(HEADS):
                    maxima_cross(0, h)
                    see.expect(q.max_done, TB // 2)
                shifts(HEADS, q.max_done, q.shift_ready)
                shifts_turned(2 * HEADS, 0, q.shiftT_full, q.shiftT_ready, bank[6])
                attend(maxima_cross, TB // 2)
                dve.wait_ge(q.y_ready, see.now(q.y_ready))
                norm(y, nx, True)
                for b in range(B):
                    residual(b)
                dve.wait_ge(q.y_ready, see.now(q.y_ready))

            def rank(lg):
                a4 = lg.unsqueeze(2).broadcast_to([P, TILES, E, E])
                b4 = lg.unsqueeze(3).broadcast_to([P, TILES, E, E])
                t4 = tri8[:, :, :].unsqueeze(1).broadcast_to([P, TILES, E, E])
                link(v.tensor_tensor(cmp1, a4, b4, ALU.is_gt))
                link(v.tensor_tensor(cmp2, a4, b4, ALU.is_equal))
                link(v.tensor_tensor(cmp2, cmp2, t4, ALU.mult))
                link(v.tensor_tensor(cmp1, cmp1, cmp2, ALU.add))
                link(v.tensor_reduce(cnt, cmp1, AX.X, ALU.add))
                link(v.tensor_tensor(cmp1, cmp1, a4, ALU.mult))
                link(v.tensor_reduce(csum, cmp1, AX.X, ALU.add))

            def softmax_of(src):
                link(v.tensor_reduce(row, src, AX.X, ALU.max))
                v.tensor_tensor(centred, src, row.unsqueeze(2).broadcast_to([P, TILES, E]),
                                ALU.subtract).then_inc(q.route_min, 1)
                dve.wait_ge(q.route_exp, see.next(q.route_exp))

            def share(t, src):
                link(v.tensor_reduce(row, src, AX.X, ALU.add))
                link(v.reciprocal(row, row))
                return v.tensor_tensor(t, src, row.unsqueeze(2).broadcast_to([P, TILES, E]), ALU.mult)

            def route0():
                dve.wait_ge(q.router_full, see.next(q.router_full))
                v.tensor_copy(logits, bank[0][:, 0:TILES * E].rearrange("p (t e) -> p t e", e=E)).then_inc(q.logits_read, 1)
                dve.wait_ge(q.logits_read, see.next(q.logits_read))
                softmax_of(logits)
                link(share(ex, ex))
                rank(ex)
                link(v.tensor_scalar(csum, csum, 0.8, None, ALU.is_lt))
                link(v.tensor_scalar(cnt, cnt, 1.5, None, ALU.is_lt))
                link(v.tensor_tensor(keep, csum, cnt, ALU.max))
                v.tensor_tensor(gate0, ex, keep, ALU.mult).then_inc(q.gate_ready, 1)
                for b in range(B):
                    dve.wait_ge(q.gateT_full, see.next(q.gateT_full))
                    v.tensor_copy(gateT[:, b * S:(b + 1) * S], bank[1 + b][0:E, :]).then_inc(q.gateT_ready, 1)

            def route1():
                dve.wait_ge(q.router_full, see.next(q.router_full))
                v.tensor_copy(logits, bank[0][:, 0:TILES * E].rearrange("p (t e) -> p t e", e=E)).then_inc(q.logits_read, 1)
                dve.wait_ge(q.logits_read, see.next(q.logits_read))
                rank(logits)
                softmax_of(logits)
                link(v.tensor_scalar(cnt, cnt, 2.5, None, ALU.is_lt))
                link(v.tensor_tensor(ex, ex, cnt, ALU.mult))
                link(share(gate1, ex))

            def gated(full, ready, gate, e):
                for b in range(B):
                    dve.wait_ge(full, see.next(full))
                    for t in range(TB):
                        w = x[:, b * TB + t, :]
                        sc = 1.0 if gate is None else gate[:, b * TB + t, bass.ds(e, 1)]
                        ins = v.scalar_tensor_tensor(out=w, in0=bank[6 + b][:, t * D:(t + 1) * D], scalar=sc, in1=w,
                                                     op0=ALU.mult, op1=ALU.add)
                    ins.then_inc(ready, 1)
                    see.expect(ready)
                    dve.wait_ge(ready, see.now(ready))

            def decayed():
                link(v.memset(V1[:, :, D:D + 1], 1.0))
                link(v.memset(ones_row, 1.0))
                for b in range(B):
                    w = slice(b * S, (b + 1) * S)
                    dve.wait_ge(q.log_ready, see.next(q.log_ready))
                    v.tensor_tensor_scan(CS[:, w][:, ::-1], ones_row, LG[:, w][:, ::-1], 0.0, ALU.mult,
                                         ALU.add).then_inc(q.sums_ready, 1)
                    dve.wait_ge(q.qkv_full, see.next(q.qkv_full))
                    v.tensor_scalar(q1T[:, w], bank[0][:, :], cols[:, 3:4], 0.0, ALU.add, ALU.max).then_inc(q.qkv_ready, 1)
                    dve.wait_ge(q.qkv_full, see.next(q.qkv_full))
                    link(v.tensor_scalar(k1T[:, w], bank[1][:, :], cols[:, 4:5], 0.0, ALU.add, ALU.max))
                    dve.wait_ge(q.decay_ready, see.next(q.decay_ready))
                    v.tensor_tensor(k1T[:, w], k1T[:, w], EX[:, w], ALU.mult).then_inc(q.qkv_ready, 1)
                    dve.wait_ge(q.qkv_full, see.next(q.qkv_full))
                    v.tensor_tensor(V1[:, b * TB:(b + 1) * TB, 0:D], bank[2][:, :].rearrange("p (t d) -> p t d", d=D),
                                    brow[:, 1:2, :].broadcast_to([P, TB, D]), ALU.add).then_inc(q.qkv_ready, 1)
                    for i in range(TB):
                        dve.wait_ge(q.sc_full, see.next(q.sc_full))
                        src = bank[4 + i % 2]
                        if i < TB - 1:
                            v.tensor_copy(SC[:, i, (i + 1) * P:], src[:, (i + 1) * P:])
                        v.tensor_tensor(SC[:, i, i * P:(i + 1) * P], src[:, i * P:(i + 1) * P], triu[:, :],
                                        ALU.mult).then_inc(q.sc_ready, 1)
                    for t in range(TB):
                        dve.wait_ge(q.num_full, see.next(q.num_full))
                        src = bank[6 + t % 2]
                        link(v.tensor_scalar(row[:, 0:1], src[:, D:D + 1], 1.0e-6, None, ALU.add))
                        link(v.reciprocal(row[:, 0:1], row[:, 0:1]))
                        tt = x[:, b * TB + t, :]
                        v.scalar_tensor_tensor(out=tt, in0=src[:, 0:D], scalar=row[:, 0:1], in1=tt, op0=ALU.mult,
                                               op1=ALU.add).then_inc(q.num_ready, 1)
                        dve.wait_ge(q.num_ready, see.next(q.num_ready))

            def split(dst, src, bias, scale, n):
                f = SPL[:, 0:n]
                link(v.tensor_scalar(f, src, bias, scale, ALU.add, ALU.mult))
                link(v.tensor_copy(dst[0], f))
                link(v.tensor_tensor(f, f, dst[0], ALU.subtract))
                link(v.tensor_copy(dst[1], f))
                return v.tensor_tensor(dst[2], f, dst[1], ALU.subtract)

            def last_attention():
                link(v.memset(Vx, 0.0))
                link(v.memset(Vx[:, :, :, DK:DK + 1], 1.0))
                dve.wait_ge(q.xkq_full, see.next(q.xkq_full))
                split(kparts, bank[0][:, 0:B * C], cols[:, 7:8], 1.0, B * C).then_inc(q.parts_ready, 1)
                dve.wait_ge(q.parts_ready, see.next(q.parts_ready))
                for b in range(B):
                    dve.wait_ge(q.xkq_full, see.next(q.xkq_full))
                    split([p[:, b * S:(b + 1) * S] for p in qparts], bank[1 + b][:, :], cols[:, 6:7],
                          float(DK) ** -0.5, S).then_inc(q.parts_ready, 1)
                    dve.wait_ge(q.parts_ready, see.next(q.parts_ready))
                for i in range(2 * B):
                    dve.wait_ge(q.xv_full, see.next(q.xv_full))
                    v.tensor_tensor(Vx[:, i, :, 0:DK], bank[3 + i][0:CH, 0:D].rearrange("p (h d) -> p h d", d=DK),
                                    brow[0:CH, 2, :].rearrange("p (h d) -> p h d", d=DK), ALU.add).then_inc(q.xv_ready, 1)
                for b in range(B):
                    for t in range(TB):
                        for h in range(0, H1, 2):
                            dve.wait_ge(q.xm_full, see.next(q.xm_full))
                            n = see.n["xm_full"] - 1
                            v.tensor_reduce(mx[:, t, h:h + 2], bank[n % 2][:, 0:2 * C].rearrange("p (a c) -> p a c", a=2),
                                            AX.X, ALU.max).then_inc(q.xm_done, 1)
                            see.expect(q.xm_done)
                    shifts(H1, q.xm_done, q.xsh_ready, GUARD)
                    shifts_turned(2 * H1, b, q.xshT_full, q.xshT_ready, bank[2 + b])
                for b in range(B):
                    for g in range(H1 // 4):
                        dve.wait_ge(q.xt_full, see.next(q.xt_full))
                        src = bank[0][:, :].rearrange("p (t j c) -> p t j c", t=TB, j=4)
                        r = rcx.rearrange("p (t j) -> p t j", j=4)
                        link(v.tensor_scalar(r, src[:, :, :, DK], 1.0e-30, None, ALU.max))
                        link(v.reciprocal(r, r))
                        v.tensor_tensor(OX[:, :, 32 * g:32 * g + 32].rearrange("p t (j d) -> p t j d", d=DK),
                                        src[:, :, :, 0:DK], r.unsqueeze(3).broadcast_to([P, TB, 4, DK]),
                                        ALU.mult).then_inc(q.xn_ready, 1)
                    dve.wait_ge(q.xout_full, see.next(q.xout_full))
                    w = x[:, b * TB:(b + 1) * TB, :]
                    v.tensor_tensor(w, bank[7][:, :].rearrange("p (t d) -> p t d", d=D), w, ALU.add).then_inc(q.x_ready, 1)
                    see.expect(q.x_ready)
                dve.wait_ge(q.x_ready, see.now(q.x_ready))

            def glu_products():
                for b in range(B):
                    for c in range(2):
                        dve.wait_ge(q.glu_act, see.next(q.glu_act))
                        dve.wait_ge(q.glu_up_full, see.next(q.glu_up_full))
                        v.tensor_tensor(GA[:, b, c, :], GS[:, b, c, :], bank[2 * c + 1][0:HP, :],
                                        ALU.mult).then_inc(q.glu_ready, 1)

            see.expect(q.const, 3)
            dve.wait_ge(q.x_in, see.next(q.x_in, 16))
            dve.wait_ge(q.const, see.now(q.const))
            norm(x, nx)
            masks()
            dve.wait_ge(q.ctx_full, see.next(q.ctx_full))
            v.tensor_copy(ctxT[:, :], bank[2][:, 0:B * C]).then_inc(q.ctx_ready, 1)
            dve.wait_ge(q.maskT_full, see.next(q.maskT_full))
            v.tensor_copy(maskT[:, :, :], bank[3][0:CH, :].bitcast(BF16).rearrange("p (a c) -> p a c", a=2)).then_inc(q.maskT_ready, 1)
            dve.wait_ge(q.small_in, see.next(q.small_in, 144))
            dve.wait_ge(q.w_early, see.next(q.w_early, 32))
            linear_attention()
            norm(x, y, last=q.normed)
            see.expect(q.normed, 4)
            dve.wait_ge(q.normed, see.now(q.normed))
            with dve.Fori(0, LAYERS) as l:
                see.enter(l, LAYER)
                layer()
                see.leave(LAYERS)
            norm(y, nx, True, last=q.dve_step)
            dve.wait_ge(q.dve_step, see.next(q.dve_step, 2))
            for b in range(B):
                w = slice(b * TB, (b + 1) * TB)
                link(v.tensor_tensor(nx[:, w, :], nx[:, w, :], brow[:, 0:1, :].broadcast_to([P, TB, D]), ALU.mult))
                link(v.tensor_tensor(x[:, w, :], x[:, w, :], nx[:, w, :], ALU.add))
            norm(x, nx)
            route0()
            for b in range(B):
                dve.wait_ge(q.bias_full, see.next(q.bias_full))
                w = slice(b * TB, (b + 1) * TB)
                v.tensor_tensor(x[:, w, :], bank[6 + b][:, :].rearrange("p (t d) -> p t d", d=D), x[:, w, :],
                                ALU.add).then_inc(q.x_ready, 1)
                dve.wait_ge(q.x_ready, see.next(q.x_ready))
            with dve.Fori(0, E // 2) as i:
                see.enter(i, EXPERTS0)
                for k in range(2):
                    gated(q.moe_down_full, q.moe_x_ready, gate0, i * 2 + k)
                see.leave(E // 2)
            norm(x, nx)
            decayed()
            norm(x, nx)
            last_attention()
            norm(x, nx)
            route1()
            with dve.Fori(0, E // 2) as i:
                see.enter(i, EXPERTS1)
                for k in range(2):
                    glu_products()
                    gated(q.glu_down_full, q.glu_x_ready, gate1, i * 2 + k)
                see.leave(E // 2)
            glu_products()
            gated(q.glu_down_full, q.glu_x_ready, None, 0)

        @block.scalar
        def _(act):
            see = Seen()
            c = nc.scalar

            def inputs(gamma=1.0):
                for b in range(B):
                    act.wait_ge(q.hT_full, see.next(q.hT_full))
                    c.activation(hT[:, b * S:(b + 1) * S], bank[6 + b][:, :], ACT.Copy, scale=gamma).then_inc(q.hT_ready, 1)

            def low(dst, src):
                act.wait_ge(q.rope_ready, see.next(q.rope_ready))
                c.activation(dst, src, ACT.Copy).then_inc(q.qk_low_ready, 1)

            def values(dst, n, t):
                act.wait_ge(q.v_full, see.next(q.v_full))
                d = dst.rearrange("p (j e) c -> p j (e c)", e=2)
                for e in range(2):
                    ins = c.activation(d[:, :, e * 192:e * 192 + DH],
                                       bank[6 + t % 2][0:n, :].rearrange("p (j e c) -> p j e c", j=PAIRS, e=2)[:, :, e, :],
                                       ACT.Copy)
                ins.then_inc(q.v_ready, 1)

            def exps(n, tiles, masked):
                for u in range(B * HEADS):
                    if u >= 2:
                        act.wait_ge(q.pv_full, see.at(q.pv_full, see.n["pv_full"] - 1))
                    for k in range(tiles):
                        act.wait_ge(q.scores_full, see.next(q.scores_full))
                        m = see.n["scores_full"] - 1
                        bias = maskcol[:, (u // HEADS) * TB + k:(u // HEADS) * TB + k + 1] if masked else 0.0
                        c.activation(probs[0:n, u % 2, k, :], bank[2 + m % 2][0:n, :], ACT.Exp,
                                     bias=bias, scale=SCALE).then_inc(q.probs_ready, 1)
                    see.expect(q.pv_full)

            see.expect(q.const, 3)
            inputs()
            for b in range(B):
                for k in range(2):
                    act.wait_ge(q.lin_min, see.next(q.lin_min))
                    c.activation(elu[:, k, 0, :], elu[:, k, 0, :], ACT.Exp).then_inc(q.lin_exp, 1)
            for b in range(B):
                act.wait_ge(q.gelu_full, see.next(q.gelu_full))
                c.activation(g0[:, b * S:(b + 1) * S], bank[6 + b][:, :], ACT.Gelu_apprx_tanh).then_inc(q.gelu_ready, 1)
            act.wait_ge(q.mask_ready, see.next(q.mask_ready))
            act.wait_ge(q.const, see.now(q.const))
            with act.Fori(0, LAYERS) as l:
                see.enter(l, LAYER)
                act.wait_ge(q.w_small, see.next(q.w_small, 32))
                inputs(lcol[:, 0:1])
                for b in range(B):
                    for dst, src in ((Kb, KT), (Qb, QT)):
                        for j in range(PAIRS):
                            low(dst[:, j, b * S:(b + 1) * S], src[:, j, b * S:(b + 1) * S])
                for t in range(TILES):
                    values(Vs[:, t], P, t)
                exps(P, TB, True)
                for j in range(PAIRS):
                    low(Kbc[:, j, :], KTc[:, j, :])
                for t in range(2 * B):
                    values(Vc[:, t], CH, t)
                inputs(lcol[:, 1:2])
                for b in range(B):
                    for j in range(PAIRS):
                        low(Qb[:, j, b * S:(b + 1) * S], QT[:, j, b * S:(b + 1) * S])
                exps(CH, 2, False)
                inputs(lcol[:, 2:3])
                for b in range(B):
                    for k in range(FCH):
                        act.wait_ge(q.up_full, see.next(q.up_full))
                        c.activation(probs[:, b, k, :], bank[2 + k][:, :], ACT.Gelu,
                                     bias=lcol[:, 3 + k:4 + k]).then_inc(q.up_ready, 1)
                see.leave(LAYERS)

            inputs()
            act.wait_ge(q.route_min, see.next(q.route_min))
            c.activation(ex, centred, ACT.Exp).then_inc(q.route_exp, 1)
            with act.Fori(0, E // 2) as i:
                see.enter(i, EXPERTS0)
                for k in range(2):
                    w = (q.w_expert0, q.w_expert1)[k]
                    act.wait_ge(w, see.next(w, 48))
                    for b in range(B):
                        for j in range(F0CH):
                            act.wait_ge(q.moe_up_full, see.next(q.moe_up_full))
                            c.activation(probs[:, b, j, :], bank[2 + j][:, :], ACT.Relu,
                                         bias=eb1[k][:, j:j + 1]).then_inc(q.moe_up_ready, 1)
                see.leave(E // 2)

            inputs()
            for b in range(B):
                w = slice(b * S, (b + 1) * S)
                act.wait_ge(q.decay_full, see.next(q.decay_full))
                c.activation(AG[:, w], bank[3][:, :], ACT.Sigmoid, bias=cols[:, 5:6]).then_inc(q.act_step, 1)
                act.wait_ge(q.act_step, see.next(q.act_step))
                c.activation(AG[:, w], AG[:, w], ACT.Copy, bias=1.0e-6).then_inc(q.act_step, 1)
                act.wait_ge(q.act_step, see.next(q.act_step))
                c.activation(LG[:, w], AG[:, w], ACT.Ln).then_inc(q.log_ready, 1)
                act.wait_ge(q.sums_ready, see.next(q.sums_ready))
                c.activation(EX[:, w], CS[:, w], ACT.Exp).then_inc(q.decay_ready, 1)

            inputs()
            for b in range(B):
                for h in range(H1 + 1):
                    if h < H1:
                        if h >= 2:
                            act.wait_ge(q.xpv_full, see.at(q.xpv_full, see.n["xpv_full"] - 1))
                        for k in range(2):
                            act.wait_ge(q.xs_full, see.next(q.xs_full))
                            c.activation(probs[0:CH, h % 2, k, :], bank[2 + k][0:CH, :], ACT.Exp).then_inc(q.xp_ready, 1)
                        see.expect(q.xpv_full)
                    if h and h % 4 == 0:
                        act.wait_ge(q.xpv_full, see.at(q.xpv_full, see.n["xpv_full"] - (1 if h < H1 else 0)))
                        g = h // 4 - 1
                        c.activation(O4[g % 2], bank[4 + g % 2][:, :], ACT.Copy).then_inc(q.xo_ready, 1)
                act.wait_ge(q.xo_full, see.next(q.xo_full))
                c.activation(OXT, bank[1][:, :], ACT.Copy).then_inc(q.xoT_ready, 1)

            inputs()
            act.wait_ge(q.route_min, see.next(q.route_min))
            c.activation(ex, centred, ACT.Exp).then_inc(q.route_exp, 1)

            def gates_of_glu():
                for b in range(B):
                    for k in range(2):
                        act.wait_ge(q.glu_gate_full, see.next(q.glu_gate_full))
                        c.activation(GS[:, b, k, :], bank[2 * k][0:HP, :], ACT.Silu).then_inc(q.glu_act, 1)

            with act.Fori(0, E // 2) as i:
                see.enter(i, EXPERTS1)
                for k in range(2):
                    gates_of_glu()
                see.leave(E // 2)
            gates_of_glu()

        @block.tensor
        def _(pe):
            see = Seen()
            mm, turn = nc.tensor.matmul, nc.tensor.transpose
            reader, read_at = [q.const] * 8, [3] * 8

            def lend(banks, sem):
                n = see.expect(sem)
                for i in banks:
                    reader[i], read_at[i] = sem, n

            def drain():
                for i in range(8):
                    pe.wait_ge(reader[i], see.at(reader[i], read_at[i]))
                    reader[i], read_at[i] = q.const, 3

            def inputs():
                for b in range(B):
                    pe.wait_ge(q.normed, see.next(q.normed))
                    pe.wait_ge(reader[6 + b], see.at(reader[6 + b], read_at[6 + b]))
                    for t in range(TB):
                        ins = turn(bank[6 + b][:, t * P:(t + 1) * P], nx[:, b * TB + t, :], ident[:, :])
                    ins.then_inc(q.hT_full, 1)
                    lend([6 + b], q.hT_ready)

            def hT_of(b):
                return hT[:, b * S:(b + 1) * S]

            def hT_tile(t):
                return hT[:, t * P:(t + 1) * P]

            def hT_wait(b):
                pe.wait_ge(q.hT_ready, see.at(q.hT_ready, see.n["hT_ready"] - (B - 1 - b)))

            def pair(w, wrot, j, rhs, n):
                i = 2 + 2 * (see.n.get("roped", 0) % 2)
                for k in (i, i + 1):
                    pe.wait_ge(reader[k], see.at(reader[k], read_at[k]))
                mm(bank[i][:, 0:n], w[:, j * P:(j + 1) * P], rhs, start=True, stop=True)
                mm(bank[i + 1][:, 0:n], wrot[:, j * P:(j + 1) * P], rhs, start=True, stop=True).then_inc(q.proj_full, 1)
                lend([i, i + 1], q.roped)

            def value_tile(src, n, w, t):
                i = 6 + t % 2
                pe.wait_ge(reader[i], see.at(reader[i], read_at[i]))
                mm(bank[i][0:n, :], src, w[:, :], start=True, stop=True).then_inc(q.v_full, 1)
                lend([i], q.v_ready)

            def head(t, h, cols_):
                r = slice(DH * (h % 2), DH * (h % 2) + DH)
                return t[r, h // 2, cols_]

            def max_self(b, h):
                for t in range(TB):
                    i = see.n.get("max_done", 0) % 2
                    pe.wait_ge(reader[i], see.at(reader[i], read_at[i]))
                    mm(bank[i][:, :], head(Qb, h, slice(b * S + t * P, b * S + (t + 1) * P)),
                       head(Kb, h, slice(b * S, (b + 1) * S)), start=True, stop=True).then_inc(q.max_full, 1)
                    lend([i], q.max_done)

            def max_cross(b, h):
                for t in range(0, TB, 2):
                    i = see.n.get("max_done", 0) % 2
                    pe.wait_ge(reader[i], see.at(reader[i], read_at[i]))
                    for k in range(2):
                        ins = mm(bank[i][:, k * C:(k + 1) * C],
                                 head(Qb, h, slice(b * S + (t + k) * P, b * S + (t + k + 1) * P)),
                                 head(Kbc, h, slice(b * C, (b + 1) * C)), start=True, stop=True)
                    ins.then_inc(q.max_full, 1)
                    lend([i], q.max_done)

            def shifts_turn(i, heads, ready, full, done):
                pe.wait_ge(ready, see.next(ready))
                pe.wait_ge(reader[i], see.at(reader[i], read_at[i]))
                for t in range(TB):
                    ins = turn(bank[i][0:2 * heads, t * P // 2:(t + 1) * P // 2].bitcast(BF16), shl[:, t, 0:2 * heads],
                               identb[:, :])
                ins.then_inc(full, 1)
                lend([i], done)

            def scores(b, h, k, n, kt, step):
                i = 2 + see.n.get("probs_ready", 0) % 2
                pe.wait_ge(reader[i], see.at(reader[i], read_at[i]))
                mm(bank[i][0:n, :], head(kt, h, slice(b * step + k * n, b * step + (k + 1) * n)),
                   head(QT, h, slice(b * S, (b + 1) * S)), start=True, stop=False)
                mm(bank[i][0:n, :], sel[:, h, 0:n], shiftT[0:2 * HEADS, b, :], start=False, stop=True)\
                    .then_inc(q.scores_full, 1)
                lend([i], q.probs_ready)

            def weigh(b, h, k, n, tiles, vals, since):
                i = 4 + see.n.get("heads_ready", 0) % 2
                if k == 0:
                    pe.wait_ge(reader[i], see.at(reader[i], read_at[i]))
                pe.wait_ge(q.probs_ready, see.at(q.probs_ready, since + k + 1))
                ins = mm(bank[i][:, :], vals[0:n, b * tiles + k, h, :], probs[0:n, h % 2, k, :], start=(k == 0),
                         stop=(k == tiles - 1))
                if k == tiles - 1:
                    ins.then_inc(q.pv_full, 1)
                    lend([i], q.heads_ready)

            def attend(maxima, n, tiles, kt, step, vals, w):
                for b in range(B):
                    pe.wait_ge(q.shiftT_ready, see.now(q.shiftT_ready))
                    for h in range(HEADS + 1):
                        if b == 0 and h < HEADS:
                            maxima(1, h)
                        now = see.n.get("probs_ready", 0)
                        for k in range(tiles):
                            if h < HEADS:
                                scores(b, h, k, n, kt, step)
                            if h:
                                weigh(b, h - 1, k, n, tiles, vals, now - tiles)
                    if b == 0:
                        shifts_turn(6, HEADS, q.shift_ready, q.shiftT_full, q.shiftT_ready)
                    pe.wait_ge(q.heads_ready, see.now(q.heads_ready))
                    contract(b, lambda c, t: AT[:, c, t * P:(t + 1) * P], w, PAIRS)

            def contract(b, lhs, w, chunks):
                pe.wait_ge(reader[6 + b], see.at(reader[6 + b], read_at[6 + b]))
                for t in range(TB):
                    for k in range(chunks):
                        ins = mm(bank[6 + b][:, t * P:(t + 1) * P], lhs(k, b * TB + t), w[:, k, :], start=(k == 0),
                                 stop=(k == chunks - 1))
                ins.then_inc(q.out_full, 1)
                lend([6 + b], q.y_ready)

            see.expect(q.const, 3)
            pe.wait_ge(q.const, see.now(q.const))
            pe.wait_ge(q.ctx_in, see.next(q.ctx_in, 16))
            for i in range(2 * B):
                ins = turn(bank[2][:, i * CH:(i + 1) * CH], cin[:, i, :], ident[0:CH, 0:CH])
            ins.then_inc(q.ctx_full, 1)
            lend([2], q.ctx_ready)
            pe.wait_ge(q.mask_ready, see.next(q.mask_ready))
            for k in range(2):
                for t in range(TB):
                    c0 = k * (S // 2) + t * P // 2
                    ins = turn(bank[3][0:CH, c0:c0 + P // 2].bitcast(BF16), maskq[:, t, k * CH:(k + 1) * CH], identb[:, :])
            ins.then_inc(q.maskT_full, 1)
            lend([3], q.maskT_ready)

            inputs()
            pe.wait_ge(q.w_early, see.next(q.w_early, 32))
            pe.wait_ge(q.small_in, see.next(q.small_in, 144))
            for b in range(B):
                hT_wait(b)
                for k in range(3):
                    i = 3 * b + k
                    pe.wait_ge(reader[i], see.at(reader[i], read_at[i]))
                    mm(bank[i][:, :], wa[:, k, :], hT_of(b), start=True, stop=True).then_inc(q.lin_full, 1)
            for b in range(B):
                pe.wait_ge(q.lin_ready, see.next(q.lin_ready))
                pe.wait_ge(reader[6 + b], see.at(reader[6 + b], read_at[6 + b]))
                for t in range(TB):
                    o = bank[6 + b][:, t * P:(t + 1) * P]
                    mm(o, ones[:, :], rows[:, 0, :], start=True, stop=False)
                    ins = mm(o, o0T[:, b * S + t * P:b * S + (t + 1) * P], wa[:, 3, :], start=False, stop=True)
                ins.then_inc(q.gelu_full, 1)
                lend([6 + b], q.gelu_ready)
            see.expect(q.normed, 2)
            drain()

            with pe.Fori(0, LAYERS) as l:
                see.enter(l, LAYER)
                see.expect(q.w_small, 32)
                pe.wait_ge(q.w_self, see.next(q.w_self, 80))
                inputs()
                for b in range(B):
                    hT_wait(b)
                    for h in range(HEADS):
                        if b:
                            pe.wait_ge(q.qk_low_ready, see.at(q.qk_low_ready, PAIRS + h // 2 + 1 + low0))
                            max_self(0, h)
                        else:
                            low0 = see.n.get("qk_low_ready", 0)
                        w, wr_ = (wk, wkr) if h < PAIRS else (wq, wqr)
                        pair(w, wr_, h % PAIRS, hT_of(b), S)
                see.expect(q.qk_low_ready, 4 * PAIRS)
                see.expect(q.rope_ready, 4 * PAIRS)
                for t in range(TILES):
                    value_tile(hT_tile(t), P, wv, t)
                shifts_turn(6, HEADS, q.shift_ready, q.shiftT_full, q.shiftT_ready)
                pe.wait_ge(q.qk_low_ready, see.now(q.qk_low_ready))
                pe.wait_ge(q.rope_ready, see.now(q.rope_ready))
                pe.wait_ge(q.v_ready, see.now(q.v_ready))
                pe.wait_ge(q.w_sout, see.next(q.w_sout, 16))
                attend(max_self, P, TB, KT, S, Vs, wo)

                pe.wait_ge(q.w_cross, see.next(q.w_cross, 80))
                for j in range(PAIRS):
                    pair(ck, ckr, j, ctxT[:, :], B * C)
                for t in range(2 * B):
                    value_tile(ctxT[:, t * CH:(t + 1) * CH], CH, cv, t)
                inputs()
                for b in range(B):
                    hT_wait(b)
                    for j in range(PAIRS):
                        pair(cq, cqr, j, hT_of(b), S)
                see.expect(q.qk_low_ready, 3 * PAIRS)
                see.expect(q.rope_ready, 3 * PAIRS)
                pe.wait_ge(q.qk_low_ready, see.now(q.qk_low_ready))
                pe.wait_ge(q.rope_ready, see.now(q.rope_ready))
                pe.wait_ge(q.v_ready, see.now(q.v_ready))
                for h in range(HEADS):
                    max_cross(0, h)
                shifts_turn(6, HEADS, q.shift_ready, q.shiftT_full, q.shiftT_ready)
                pe.wait_ge(q.w_cout, see.next(q.w_cout, 16))
                attend(max_cross, CH, 2, KTc, C, Vc, co)

                pe.wait_ge(q.w_ff1, see.next(q.w_ff1, 16))
                pe.wait_ge(q.w_ff2, see.next(q.w_ff2, 16))
                inputs()
                for b in range(B):
                    hT_wait(b)
                    for k in range(FCH):
                        pe.wait_ge(reader[2 + k], see.at(reader[2 + k], read_at[2 + k]))
                        mm(bank[2 + k][:, :], f1[:, k * P:(k + 1) * P], hT_of(b), start=True, stop=True)\
                            .then_inc(q.up_full, 1)
                        lend([2 + k], q.up_ready)
                for b in range(B):
                    pe.wait_ge(q.up_ready, see.at(q.up_ready, see.n["up_ready"] - (B - 1 - b) * FCH))
                    contract(b, lambda k, t: probs[:, b, k, (t % TB) * P:(t % TB + 1) * P], f2, FCH)
                drain()
                see.leave(LAYERS)

            def router(w, bias):
                pe.wait_ge(reader[0], see.at(reader[0], read_at[0]))
                for t in range(TILES):
                    if t % TB == 0:
                        hT_wait(t // TB)
                    o = bank[0][:, t * E:(t + 1) * E]
                    ins = mm(o, hT_tile(t), w, start=True, stop=not bias)
                    if bias:
                        ins = mm(o, ones[:, :], lrow8[:, :], start=False, stop=True)
                ins.then_inc(q.router_full, 1)
                lend([0], q.logits_read)

            inputs()
            router(wr[:, 0, :], True)
            pe.wait_ge(q.gate_ready, see.next(q.gate_ready))
            for b in range(B):
                pe.wait_ge(reader[1 + b], see.at(reader[1 + b], read_at[1 + b]))
                for t in range(TB):
                    ins = turn(bank[1 + b][0:E, t * P:(t + 1) * P], gate0[:, b * TB + t, :], ident[:, :])
                ins.then_inc(q.gateT_full, 1)
                lend([1 + b], q.gateT_ready)
            for b in range(B):
                pe.wait_ge(q.gateT_ready, see.at(q.gateT_ready, b + 1))
                pe.wait_ge(reader[6 + b], see.at(reader[6 + b], read_at[6 + b]))
                for t in range(TB):
                    ins = mm(bank[6 + b][:, t * P:(t + 1) * P], gateT[:, b * S + t * P:b * S + (t + 1) * P], b2e[:, :],
                             start=True, stop=True)
                ins.then_inc(q.bias_full, 1)
                lend([6 + b], q.x_ready)
            drain()
            with pe.Fori(0, E // 2) as i:
                see.enter(i, EXPERTS0)
                for k in range(2):
                    w = (q.w_expert0, q.w_expert1)[k]
                    pe.wait_ge(w, see.next(w, 48))
                    for b in range(B):
                        for j in range(F0CH):
                            pe.wait_ge(reader[2 + j], see.at(reader[2 + j], read_at[2 + j]))
                            mm(bank[2 + j][:, :], ew1[k][:, j * P:(j + 1) * P], hT_of(b), start=True, stop=True)\
                                .then_inc(q.moe_up_full, 1)
                            lend([2 + j], q.moe_up_ready)
                    for b in range(B):
                        pe.wait_ge(q.moe_up_ready, see.at(q.moe_up_ready, see.n["moe_up_ready"] - (B - 1 - b) * F0CH))
                        pe.wait_ge(reader[6 + b], see.at(reader[6 + b], read_at[6 + b]))
                        for t in range(TB):
                            for j in range(F0CH):
                                ins = mm(bank[6 + b][:, t * P:(t + 1) * P], probs[:, b, j, t * P:(t + 1) * P],
                                         ew2[k][:, j * D:(j + 1) * D], start=(j == 0), stop=(j == F0CH - 1))
                        ins.then_inc(q.moe_down_full, 1)
                        lend([6 + b], q.moe_x_ready)
                drain()
                see.leave(E // 2)

            pe.wait_ge(q.w_l1, see.next(q.w_l1, 64))
            inputs()
            for b in range(B):
                hT_wait(b)
                pe.wait_ge(reader[3], see.at(reader[3], read_at[3]))
                mm(bank[3][:, :], w1a[:, 3, :], hT_of(b), start=True, stop=True).then_inc(q.decay_full, 1)
                lend([3], q.log_ready)
                for k in range(2):
                    pe.wait_ge(reader[k], see.at(reader[k], read_at[k]))
                    mm(bank[k][:, :], w1a[:, k, :], hT_of(b), start=True, stop=True).then_inc(q.qkv_full, 1)
                    lend([k], q.qkv_ready)
                pe.wait_ge(reader[2], see.at(reader[2], read_at[2]))
                for t in range(TB):
                    ins = mm(bank[2][:, t * P:(t + 1) * P], hT_tile(b * TB + t), w1a[:, 2, :], start=True, stop=True)
                ins.then_inc(q.qkv_full, 1)
                lend([2], q.qkv_ready)
                pe.wait_ge(q.qkv_ready, see.now(q.qkv_ready))
                for j in range(TB):
                    pe.wait_ge(reader[4 + j % 2], see.at(reader[4 + j % 2], read_at[4 + j % 2]))
                    mm(bank[4 + j % 2][:, j * P:], k1T[:, b * S + j * P:b * S + (j + 1) * P],
                       q1T[:, b * S + j * P:(b + 1) * S], start=True, stop=True).then_inc(q.sc_full, 1)
                    lend([4 + j % 2], q.sc_ready)
                for t in range(TB):
                    pe.wait_ge(q.sc_ready, see.at(q.sc_ready, b * TB + t + 1))
                    pe.wait_ge(reader[6 + t % 2], see.at(reader[6 + t % 2], read_at[6 + t % 2]))
                    for j in range(t + 1):
                        ins = mm(bank[6 + t % 2][:, 0:D + 1], SC[:, j, t * P:(t + 1) * P], V1[:, b * TB + j, 0:D + 1],
                                 start=(j == 0), stop=(j == t))
                    ins.then_inc(q.num_full, 1)
                    lend([6 + t % 2], q.num_ready)

            inputs()
            for k in (0, 1, 2, 3, 4, 5):
                pe.wait_ge(reader[k], see.at(reader[k], read_at[k]))
            mm(bank[0][:, 0:B * C], w1x[:, 1, :], ctxT[:, :], start=True, stop=True).then_inc(q.xkq_full, 1)
            lend([0], q.parts_ready)
            for b in range(B):
                hT_wait(b)
                mm(bank[1 + b][:, :], w1x[:, 0, :], hT_of(b), start=True, stop=True).then_inc(q.xkq_full, 1)
                lend([1 + b], q.parts_ready)
            for i in range(2 * B):
                pe.wait_ge(reader[3 + i], see.at(reader[3 + i], read_at[3 + i]))
                mm(bank[3 + i][0:CH, 0:D], ctxT[:, i * CH:(i + 1) * CH], w1x[:, 2, :], start=True, stop=True)\
                    .then_inc(q.xv_full, 1)
                lend([3 + i], q.xv_ready)
            pe.wait_ge(q.parts_in, see.next(q.parts_in, 16 * 2 * SPLITS))
            R = SPLITS * DK
            for b in range(B):
                for t in range(TB):
                    for h in range(0, H1, 2):
                        i = see.n.get("xm_done", 0) % 2
                        pe.wait_ge(reader[i], see.at(reader[i], read_at[i]))
                        for k in range(2):
                            o = bank[i][:, k * C:(k + 1) * C]
                            mm(o, Qst[0:R, h + k, b * S + t * P:b * S + (t + 1) * P], Kst[0:R, h + k, b * C:(b + 1) * C],
                               start=True, stop=False)
                            ins = mm(o, identb[:, :], maskq[:, t, :], start=False, stop=True)
                        ins.then_inc(q.xm_full, 1)
                        lend([i], q.xm_done)
                shifts_turn(2 + b, H1, q.xsh_ready, q.xshT_full, q.xshT_ready)

            def xweigh(b, h):
                g, j = h // 4, h % 4
                if j == 0:
                    pe.wait_ge(reader[4 + g % 2], see.at(reader[4 + g % 2], read_at[4 + g % 2]))
                for k in range(2):
                    pe.wait_ge(q.xp_ready, see.at(q.xp_ready, 2 * (b * H1 + h) + k + 1))
                    ins = mm(bank[4 + g % 2][32 * j:32 * j + 32, :], Vx[:, 2 * b + k, h, :], probs[0:CH, h % 2, k, :],
                             start=(k == 0), stop=(k == 1))
                ins.then_inc(q.xpv_full, 1)

            for b in range(B):
                w = (q.xsh_in0, q.xsh_in1)[b]
                pe.wait_ge(w, see.next(w, 16))
                for h in range(H1 + 1):
                    if h < H1:
                        for k in range(2):
                            pe.wait_ge(reader[2 + k], see.at(reader[2 + k], read_at[2 + k]))
                            o = bank[2 + k][0:CH, :]
                            mm(o, Kst[0:R + 2, h, b * C + k * CH:b * C + (k + 1) * CH], Qst[0:R + 2, h, b * S:(b + 1) * S],
                               start=True, stop=False)
                            mm(o, identb[0:CH, 0:CH], maskT[:, k, :], start=False, stop=True).then_inc(q.xs_full, 1)
                            lend([2 + k], q.xp_ready)
                    if h:
                        xweigh(b, h - 1)
                    if h and h % 4 == 0:
                        g = h // 4 - 1
                        lend([4 + g % 2], q.xo_ready)
                        pe.wait_ge(q.xo_ready, see.now(q.xo_ready))
                        pe.wait_ge(reader[0], see.at(reader[0], read_at[0]))
                        for t in range(TB):
                            ins = turn(bank[0][:, t * P:(t + 1) * P], O4[g % 2][:, t * P:(t + 1) * P], ident[:, :])
                        ins.then_inc(q.xt_full, 1)
                        lend([0], q.xn_ready)
                pe.wait_ge(q.xn_ready, see.now(q.xn_ready))
                pe.wait_ge(reader[1], see.at(reader[1], read_at[1]))
                for t in range(TB):
                    ins = turn(bank[1][:, t * P:(t + 1) * P], OX[:, t, :], ident[:, :])
                ins.then_inc(q.xo_full, 1)
                lend([1], q.xoT_ready)
                pe.wait_ge(q.xoT_ready, see.now(q.xoT_ready))
                pe.wait_ge(reader[7], see.at(reader[7], read_at[7]))
                for t in range(TB):
                    o = bank[7][:, t * P:(t + 1) * P]
                    mm(o, ones[:, :], rows[:, 1, :], start=True, stop=False)
                    ins = mm(o, OXT[:, t * P:(t + 1) * P], w1x[:, 3, :], start=False, stop=True)
                ins.then_inc(q.xout_full, 1)
                lend([7], q.x_ready)

            inputs()
            router(wr[:, 1, :], False)

            def glu(up, down):
                for b in range(B):
                    hT_wait(b)
                    for k in range(2):
                        pe.wait_ge(reader[2 * k], see.at(reader[2 * k], read_at[2 * k]))
                        mm(bank[2 * k][0:HP, :], up[:, k * HP:(k + 1) * HP], hT_of(b), start=True, stop=True)\
                            .then_inc(q.glu_gate_full, 1)
                        lend([2 * k], q.glu_act)
                        pe.wait_ge(reader[2 * k + 1], see.at(reader[2 * k + 1], read_at[2 * k + 1]))
                        mm(bank[2 * k + 1][0:HP, :], up[:, HALF + k * HP:HALF + (k + 1) * HP], hT_of(b), start=True,
                           stop=True).then_inc(q.glu_up_full, 1)
                        lend([2 * k + 1], q.glu_ready)
                for b in range(B):
                    pe.wait_ge(q.glu_ready, see.at(q.glu_ready, see.n["glu_ready"] - (B - 1 - b) * 2))
                    pe.wait_ge(reader[6 + b], see.at(reader[6 + b], read_at[6 + b]))
                    for t in range(TB):
                        for k in range(2):
                            ins = mm(bank[6 + b][:, t * P:(t + 1) * P], GA[:, b, k, t * P:(t + 1) * P], down[:, k, :],
                                     start=(k == 0), stop=(k == 1))
                    ins.then_inc(q.glu_down_full, 1)
                    lend([6 + b], q.glu_x_ready)

            drain()
            for b in range(B):
                hT_wait(b)
            with pe.Fori(0, E // 2) as i:
                see.enter(i, EXPERTS1)
                for k in range(2):
                    w = (q.w_glu0, q.w_glu1)[k]
                    pe.wait_ge(w, see.next(w, 32))
                    glu(gup[k], gdn[k])
                drain()
                see.leave(E // 2)
            glu(gup[2], gdn[2])


def kernel(**inputs):
    import numpy as np
    import concourse.bacc as bacc
    from concourse.bass_utils import run_bass_kernel_spmd

    def arr(name):
        return np.ascontiguousarray(np.asarray(inputs[name]))

    def half_swapped(w):
        w = w.reshape(LAYERS, D, HEADS, DH)
        return np.concatenate([w[..., 16:32], w[..., 0:16], w[..., 32:]], axis=-1).reshape(LAYERS, D, INNER)

    l0 = {n: arr("L0_xattn_" + n) for n in ("sWq", "sWk", "sWv", "sWo", "cWq", "cWk", "cWv", "cWo", "fW1", "fW2")}
    for n in ("sWq", "sWk", "cWq", "cWk"):
        l0[n + "r"] = half_swapped(l0[n])
    gam = [arr("L0_xattn_" + n)[:, :, None] for n in ("sg", "cg", "fg")]
    fb1 = arr("L0_xattn_fb1").reshape(LAYERS, FCH, P).transpose(0, 2, 1)
    arrays = dict(
        x=arr("x"), ctx=arr("ctx_1024"),
        mask1=arr("mask_BxS_bf1"), mask1c=arr("mask_BxS_bf1").reshape(TILES, P).T, mask2=arr("mask_1x1xSxS2_bk1").reshape(S, C),
        wa=np.stack([arr("L0_attn_" + n) for n in ("wq", "wk", "wv", "wo")]),
        cols=np.stack([arr(n) for n in ("L0_attn_bq", "L0_attn_bk", "L0_attn_bv", "L1_attn_b_q", "L1_attn_b_k",
                                        "L1_attn_b_a", "L1_xattn_bq", "L1_xattn_bk")], axis=1),
        rows=np.stack([arr("L0_attn_bo"), arr("L1_xattn_bo"), arr("L1_xattn_bo")]),
        brow=np.stack([arr("L0_xattn_g_out"), arr("L1_attn_b_v"), arr("L1_xattn_bv")]),
        br=arr("L0_ffn_br"), wr=np.stack([arr("L0_ffn_Wr"), arr("L1_ffn_gate_w").T]),
        lcol=np.concatenate(gam + [fb1], axis=2),
        lrow=np.stack([arr("L0_xattn_" + n) for n in ("sbo", "cbo", "fb2")], axis=1),
        W1=arr("L0_ffn_W1"), W2=arr("L0_ffn_W2"), b2=arr("L0_ffn_b2"),
        b1=arr("L0_ffn_b1").reshape(E, F0CH, P).transpose(0, 2, 1),
        w1a=np.stack([arr("L1_attn_" + n).T for n in ("W_q", "W_k", "W_v", "W_a")]),
        w1x=np.stack([arr("L1_xattn_" + n).T for n in ("Wq", "Wk", "Wv", "Wo")]),
        wup=arr("L1_ffn_w_up").transpose(0, 2, 1), wdn=arr("L1_ffn_w_down").transpose(0, 2, 1),
        sgu=np.concatenate([arr("L1_ffn_sg_gate").T, arr("L1_ffn_sg_up").T], axis=1), sgd=arr("L1_ffn_sg_down").T,
        **l0)

    rotd = 32
    inv = (1.0 / 10000.0 ** (np.arange(0, rotd, 2, dtype=np.float32) / np.float32(rotd))).astype(np.float32)
    ang = (np.arange(S, dtype=np.float32)[:, None] * inv[None, :]).astype(np.float32)
    cos, sin = np.cos(ang).T.astype(np.float32), np.sin(ang).T.astype(np.float32)
    one = np.concatenate([cos, cos, np.ones((DH - rotd, S), np.float32)])
    two = np.concatenate([-sin, sin, np.zeros((DH - rotd, S), np.float32)])
    arrays["cos"], arrays["sin"] = np.concatenate([one, one]), np.concatenate([two, two])
    arrays["tri8"] = np.tril(np.ones((E, E), np.float32))
    sel = np.zeros((2, HEADS, HEADS, P), np.float32)
    for h in range(HEADS):
        sel[:, h, h, :] = 1.0
    import ml_dtypes
    arrays["sel"] = sel.reshape(2 * HEADS, HEADS, P).astype(ml_dtypes.bfloat16)

    nc = bacc.Bacc("TRN2", target_bir_lowering=False, num_devices=1)
    nc.disable_value_cache = True
    feeds, aps = {}, {}
    for name, v in arrays.items():
        v = np.ascontiguousarray(v)
        feeds["in_" + name] = v
        aps[name] = nc.dram_tensor("in_" + name, v.shape, mybir.dt.from_np(v.dtype), kind="ExternalInput").ap()
    out = nc.dram_tensor("out_x", (B, S, D), F32, kind="ExternalOutput").ap()
    decoder(nc, aps, out)
    r = run_bass_kernel_spmd(nc, [feeds], core_ids=[0])
    return r.results[0]["out_x"]
```

```python
import concourse.bass as bass
from concourse import mybir
from contextlib import ExitStack

F32 = mybir.dt.float32
BF16 = mybir.dt.bfloat16
F32R = mybir.dt.float32r
U8 = mybir.dt.uint8
ALU = mybir.AluOpType
ACT = mybir.ActivationFunctionType
AX = mybir.AxisListType

P = 128
B, S, D = 2, 512, 128
NT = B * S
TB = S // P
TILES = B * TB
C = 154
CH = C // 2
C2 = C - P
LAYERS, HEADS, DH = 4, 8, 64
PAIRS = HEADS // 2
INNER = HEADS * DH
FF, FCH = 512, 512 // P
E = 8
F0, F0CH = 512, 512 // P
HALF = 192
HP = HALF // 2
H1, DK = 16, 8
SPLITS = 6
SCALE = DH ** -0.5
CONSTS = 3
NEG = -float(2.0 ** 100)
GUARD = 1.0e29

LAYER = dict(
    var_ready=6, rstd_ready=6, normed=6, hT_full=6, hT_ready=6, y_free=6,
    proj_full=28, roped=28, rope_ready=28, high_ready=28, qk_ready=28, swap0=256, swap1=256,
    v_full=12, v_ready=12,
    max_full=64 + 32, max_done=64 + 32, shift_ready=4, shiftT_full=4, shiftT_ready=4,
    scores_full=64 + 32, probs_ready=64 + 32, weighed=32 + 16, summed=21, den_full=7,
    heads_ready=16,
    out_full=6, y_ready=6, up_full=8, up_ready=8,
    w_self=80, w_sout=16, w_cross=80, w_cout=16, w_ff1=16, w_ff2=16, w_small=32, dve_step=48,
)
EXPERTS0 = dict(moe_up_full=16, moe_up_ready=16, moe_down_full=4, moe_x_ready=4, w_expert0=48, w_expert1=48)
EXPERTS1 = dict(glu_gate_full=8, glu_up_full=8, glu_act=8, glu_ready=8, glu_down_full=4, glu_x_ready=4,
                w_glu0=32, w_glu1=32)

LAYER_SELF_SCORES = 2 * PAIRS * B * TB
QUOTA = {TB: (3, 3, 3, 3, 3, 3, 2, 3, 3, 3, 3), 2: (3, 4, 2, 2, 2, 2, 1)}
TURN = {TB: 12, 2: 7}
XQUOTA = (6, 6, 6, 6, 6, 2)
XTURN = 6


def quota(tiles, step):
    return range(sum(QUOTA[tiles][:step]), sum(QUOTA[tiles][:step + 1]))


def direct(b, j, tiles):
    return tiles == 2 or (b, j) == (B - 1, PAIRS - 1)


class Seen:

    def __init__(self):
        self.n, self.turn, self.per = {}, None, {}

    def at(self, sem, n):
        per = self.per.get(sem.name, 0) if self.turn is not None else 0
        return n + self.turn * per if per else n

    def now(self, sem):
        return self.at(sem, self.n[sem.name])

    def expect(self, sem, k=1):
        self.n[sem.name] = self.n.get(sem.name, 0) + k
        return self.n[sem.name]

    def next(self, sem, k=1):
        return self.at(sem, self.expect(sem, k))

    def enter(self, turn, per):
        self.turn, self.per, self.start = turn, per, dict(self.n)

    def leave(self, turns):
        for name, n in self.n.items():
            more = n - self.start.get(name, 0)
            if more:
                assert more == self.per.get(name), (name, more)
                self.n[name] = self.start.get(name, 0) + more * turns
        self.turn, self.per = None, {}


def decoder(nc, a, out):
    ctx = ExitStack()
    with ctx:
        def sb(name, shape, dt=F32):
            return ctx.enter_context(nc.sbuf_tensor(name, shape, dt))

        def sem(name):
            return ctx.enter_context(nc.semaphore(name))

        bank = [ctx.enter_context(nc.psum_tensor(f"bank{i}", [P, 512], F32)) for i in range(8)]

        x = sb("x", [P, TILES, D])
        y = sb("y", [P, TILES, D])
        nx = sb("nx", [P, TILES, D])
        stats = sb("stats", [P, TILES, 6])
        mv = sb("mv", [P, TILES, 2])
        var = sb("var", [P, TILES])
        rstd = sb("rstd", [P, TILES])
        neghalf = sb("neghalf", [P, TILES])
        hT = sb("hT", [P, NT])
        with nc.sbuf_tensor("QHL", [P, HEADS, NT], F32R) as QHL, nc.sbuf_tensor("KHL", [P, HEADS, NT], F32R) as KHL:
            pass
        QA, KA = sb("QA", [P, HEADS * NT]), sb("KA", [P, HEADS * NT])
        KHLc = KHL[:, :, 0:B * C]
        QSW = sb("QSW", [P, 4, S], F32R)
        Vs = sb("Vs", [P, TILES, INNER])
        Vc = Vs[:, 0:2 * B, :]
        ones64 = sb("ones64", [P, DH])
        once64 = sb("once64", [P, DH])
        probs = sb("probs", [P, 2, 4, 512])
        acc = sb("acc", [P, 2, 2, 512])
        ring = probs[:, :, :, :].rearrange("p a b c -> p (a b) c")
        AT = sb("AT", [P, PAIRS, NT])
        rot = sb("rot", [P, 2, 2, 512])
        rec = rot[:, 1, 1, :]

        mx = sb("mx", [P, TB, H1])
        shift = sb("shift", [P, TB, H1])
        shl = sb("shl", [P, TB, 2 * H1], BF16)
        shiftT = sb("shiftT", [2 * H1, B, S], BF16)
        sel = sb("sel", [2 * HEADS, HEADS, P], BF16)
        wq = sb("wq", [P, INNER]); wqr = sb("wqr", [P, INNER])
        wk = sb("wk", [P, INNER]); wkr = sb("wkr", [P, INNER])
        wv = sb("wv", [P, INNER]); wo = sb("wo", [P, PAIRS, D])
        cq = sb("cq", [P, INNER]); cqr = sb("cqr", [P, INNER])
        ck = sb("ck", [P, INNER]); ckr = sb("ckr", [P, INNER])
        cv = sb("cv", [P, INNER]); co = sb("co", [P, PAIRS, D])
        f1 = sb("f1", [P, FF]); f2 = sb("f2", [P, FCH, D])
        lcol = sb("lcol", [P, 3 + FCH])
        lrow = sb("lrow", [P, 3, D])
        ident = sb("ident", [P, P]); identb = sb("identb", [P, P], BF16)
        triu = sb("triu", [P, P])
        cos = sb("cos", [P, S]); sin = sb("sin", [P, S])
        maskrow = sb("maskrow", [P, NT], BF16)
        maskc8 = sb("maskc8", [P, TILES], U8); maskcol = sb("maskcol", [P, TILES])
        maskq = sb("maskq", [P, TB, C], BF16); maskT = sb("maskT", [P, 2, S], BF16)
        ctxT = sb("ctxT", [P, B * C])
        ones = sb("ones", [1, P])
        cols = sb("cols", [P, 8])
        rows = sb("rows", [1, 3, D])
        brow = sb("brow", [P, 3, D])
        lrow8 = sb("lrow8", [1, E])
        wa = sb("wa", [P, 4, D])
        wr = sb("wr", [P, 2, E])
        tri8 = sb("tri8", [P, E, E])

        gates = sb("gates", [P, 2, TILES, E])
        b2e = sb("b2e", [E, D])

        QT = QA[:, 0:4 * NT].rearrange("p (a t) -> p a t", t=NT)
        KT = QA[:, 4 * NT:8 * NT].rearrange("p (a t) -> p a t", t=NT)
        Qb = KA[:, 0:2 * NT].bitcast(BF16).rearrange("p (a t) -> p a t", t=NT)
        Kb = KA[:, 2 * NT:4 * NT].bitcast(BF16).rearrange("p (a t) -> p a t", t=NT)
        cin = probs[0:CH, 0, :, 0:D]
        maskr8 = probs[:, 1, 0, 0:NT // 4].bitcast(U8)
        m1u8 = probs[:, 1, 1, 0:TB * C // 4].bitcast(U8).rearrange("p (t c) -> p t c", t=TB)
        elu = rot
        q0T, k0T, v0T = QT[:, 0, :], QT[:, 1, :], QT[:, 2, :]
        o0T, z0T, g0 = QT[:, 3, :], KT[:, 0, :], KT[:, 1, :]
        kv = mx[:, 0, :]
        ew1, ew2, eb1 = [wq, wqr], [wk, wkr], [wv[:, 0:F0CH], wv[:, F0CH:2 * F0CH]]
        gate0, gate1 = gates[:, 0], gates[:, 1]
        gateT = rot[0:E, 0, :, :].rearrange("p a c -> p (a c)")
        cmp1 = KT[:, 0, 0:512].rearrange("p (t e j) -> p t e j", e=E, j=E)
        cmp2 = KT[:, 1, 0:512].rearrange("p (t e j) -> p t e j", e=E, j=E)

        def small(i):
            return KT[:, 2, 64 * i:64 * i + 64].rearrange("p (t e) -> p t e", e=E)
        cnt, csum, ex, keep, centred, logits = (small(i) for i in range(6))
        row = KT[:, 2, 512:512 + TILES]
        rcx = KA[:, 6656:6672]
        w1a = cq[:, :].rearrange("p (a n) -> p a n", a=4)
        AG, LG, CS, EX = (QT[:, i, :] for i in range(4))
        q1T, k1T = KT[:, 0, :], KT[:, 1, :]
        VsF = Vs[:, :, :].rearrange("p t c -> p (t c)")
        V1 = VsF[:, 0:TILES * 130].rearrange("p (t c) -> p t c", c=130)
        SC = VsF[:, 2048:4096].rearrange("p (t c) -> p t c", t=TB)
        ones_row = KA[:, 0:S]
        w1x = ck[:, :].rearrange("p (a n) -> p a n", a=4)
        Qst = QA[:, :].bitcast(BF16).rearrange("p (h t) -> p h t", h=H1)
        Kst = AT[:, :, :].rearrange("p a c -> p (a c)").bitcast(BF16)[:, 0:H1 * B * C].rearrange("p (h t) -> p h t", h=H1)
        Vx = VsF[:, 0:2048].rearrange("p (i h c) -> p i h c", i=2 * B, h=H1)
        qparts = [Qb[:, i, :] for i in range(3)]
        kparts = [Kb[:, i, 0:B * C] for i in range(3)]
        SPL = KA[:, 4096:4608]
        OX = KA[:, 4608:5120].rearrange("p (t c) -> p t c", t=TB)
        OXT = KA[:, 5120:5632]
        O4 = [KA[:, 5632:6144], KA[:, 6144:6656]]
        gup = [cqr, ckr, f1]
        gdn = [w.rearrange("p (c n) -> p c n", c=2) for w in (cv[0:HP, 0:2 * D], cv[0:HP, 2 * D:4 * D])]
        gdn.append(co[0:HP, 0:2, :])
        GS = probs[0:HP, 0, :, :].rearrange("p (b c) n -> p b c n", b=B)
        GA = probs[0:HP, 1, :, :].rearrange("p (b c) n -> p b c n", b=B)

        class q:
            const = sem("const")
            x_in = sem("x_in")
            w_early = sem("w_early")
            small_in = sem("small_in")
            ctx_in = sem("ctx_in")
            mask_in = sem("mask_in")
            w_self = sem("w_self")
            w_sout = sem("w_sout")
            w_cross = sem("w_cross")
            w_cout = sem("w_cout")
            w_ff1 = sem("w_ff1")
            w_ff2 = sem("w_ff2")
            w_small = sem("w_small")
            w_expert0 = sem("w_expert0")
            w_expert1 = sem("w_expert1")
            w_l1 = sem("w_l1")
            w_glu0 = sem("w_glu0")
            w_glu1 = sem("w_glu1")
            var_ready = sem("var_ready")
            rstd_ready = sem("rstd_ready")
            normed = sem("normed")
            hT_full = sem("hT_full")
            hT_ready = sem("hT_ready")
            y_free = sem("y_free")
            ctx_full = sem("ctx_full")
            ctx_ready = sem("ctx_ready")
            mask_ready = sem("mask_ready")
            maskT_full = sem("maskT_full")
            maskT_ready = sem("maskT_ready")
            lin_full = sem("lin_full")
            lin_min = sem("lin_min")
            lin_exp = sem("lin_exp")
            lin_add = sem("lin_add")
            lin_ready = sem("lin_ready")
            gelu_full = sem("gelu_full")
            gelu_ready = sem("gelu_ready")
            x_ready = sem("x_ready")
            proj_full = sem("proj_full")
            roped = sem("roped")
            rope_ready = sem("rope_ready")
            high_ready = sem("high_ready")
            qk_ready = sem("qk_ready")
            swap0 = sem("swap0")
            swap1 = sem("swap1")
            v_full = sem("v_full")
            v_ready = sem("v_ready")
            max_full = sem("max_full")
            max_done = sem("max_done")
            shift_ready = sem("shift_ready")
            shiftT_full = sem("shiftT_full")
            shiftT_ready = sem("shiftT_ready")
            scores_full = sem("scores_full")
            probs_ready = sem("probs_ready")
            weighed = sem("weighed")
            summed = sem("summed")
            den_full = sem("den_full")
            heads_ready = sem("heads_ready")
            out_full = sem("out_full")
            y_ready = sem("y_ready")
            up_full = sem("up_full")
            up_ready = sem("up_ready")
            router_full = sem("router_full")
            logits_read = sem("logits_read")
            route_min = sem("route_min")
            route_exp = sem("route_exp")
            gate_ready = sem("gate_ready")
            gateT_full = sem("gateT_full")
            gateT_ready = sem("gateT_ready")
            bias_full = sem("bias_full")
            moe_up_full = sem("moe_up_full")
            moe_up_ready = sem("moe_up_ready")
            moe_down_full = sem("moe_down_full")
            moe_x_ready = sem("moe_x_ready")
            decay_full = sem("decay_full")
            log_ready = sem("log_ready")
            sums_ready = sem("sums_ready")
            decay_ready = sem("decay_ready")
            qkv_full = sem("qkv_full")
            qkv_ready = sem("qkv_ready")
            sc_full = sem("sc_full")
            sc_ready = sem("sc_ready")
            num_full = sem("num_full")
            num_ready = sem("num_ready")
            xkq_full = sem("xkq_full")
            parts_ready = sem("parts_ready")
            parts_out = sem("parts_out")
            parts_in = sem("parts_in")
            xv_full = sem("xv_full")
            xv_ready = sem("xv_ready")
            kst_one = sem("kst_one")
            xm_full = sem("xm_full")
            xm_done = sem("xm_done")
            xsh_ready = sem("xsh_ready")
            xshT_full = sem("xshT_full")
            xshT_ready = sem("xshT_ready")
            xsh_out = sem("xsh_out")
            xsh_in0 = sem("xsh_in0")
            xsh_in1 = sem("xsh_in1")
            xs_full = sem("xs_full")
            xp_ready = sem("xp_ready")
            xpv_full = sem("xpv_full")
            xo_ready = sem("xo_ready")
            xt_full = sem("xt_full")
            xn_ready = sem("xn_ready")
            xo_full = sem("xo_full")
            xoT_ready = sem("xoT_ready")
            xout_full = sem("xout_full")
            glu_gate_full = sem("glu_gate_full")
            glu_up_full = sem("glu_up_full")
            glu_act = sem("glu_act")
            glu_ready = sem("glu_ready")
            glu_down_full = sem("glu_down_full")
            glu_x_ready = sem("glu_x_ready")
            stored = sem("stored")
            dve_step = sem("dve_step")
            dve_passed = sem("dve_passed")
            sp_passed = sem("sp_passed")
            pool_step = sem("pool_step")
            act_step = sem("act_step")
        dram_q = nc.dram_tensor("dram_q", [3, P, NT], BF16)
        dram_k = nc.dram_tensor("dram_k", [3, P, B * C], BF16)
        dram_s = nc.dram_tensor("dram_s", [B, 2 * H1, S], BF16)

        block = ctx.enter_context(nc.Block())

        @block.sync
        def _(sp):
            see = Seen()
            sp.dma_start(x[:, :, :], a["x"].rearrange("b (t p) d -> p (b t) d", p=P)).then_inc(q.x_in, 16)
            sp.dma_start(wa[:, :, :], a["wa"].rearrange("a p n -> p a n")).then_inc(q.w_early, 16)
            sp.dma_start(cols[:, :], a["cols"]).then_inc(q.w_early, 16)
            sp.dma_start(rows[:, :, :], a["rows"].rearrange("(o a) n -> o a n", o=1)).then_inc(q.small_in, 16)
            sp.dma_start(lrow8[:, :], a["br"].rearrange("(o n) -> o n", o=1)).then_inc(q.small_in, 16)
            sp.dma_start(brow[:, :, :], a["brow"].partition_broadcast(P)).then_inc(q.small_in, 16)
            sp.dma_start(wr[:, :, :], a["wr"].rearrange("a p n -> p a n")).then_inc(q.small_in, 16)
            sp.dma_start(tri8[:, :, :], a["tri8"].partition_broadcast(P)).then_inc(q.small_in, 16)
            sp.dma_start(b2e[:, :], a["b2"]).then_inc(q.small_in, 16)
            for t, name in ((cos, "cos"), (sin, "sin")):
                sp.dma_start(t[:, :], a[name]).then_inc(q.small_in, 16)
            sp.dma_start(sel[:, :, :], a["sel"]).then_inc(q.small_in, 16)
            sp.dma_start(cin, a["ctx"].rearrange("b (t p) d -> p (b t) d", p=CH)).then_inc(q.ctx_in, 16)
            sp.dma_start(maskr8, a["mask1"].rearrange("b s -> (b s)").partition_broadcast(P)).then_inc(q.mask_in, 16)
            sp.dma_start(maskc8[:, :], a["mask1c"]).then_inc(q.mask_in, 16)
            sp.dma_start(m1u8, a["mask2"].rearrange("(t p) c -> p t c", p=P)).then_inc(q.mask_in, 16)
            def load_small(l):
                sp.dma_start(lcol[:, :], a["lcol"][l]).then_inc(q.w_small, 16)
                sp.dma_start(lrow[:, :, :], a["lrow"][l].partition_broadcast(P)).then_inc(q.w_small, 16)

            def load_self(l):
                for t, name in ((wk, "sWk"), (wkr, "sWkr"), (wq, "sWq"), (wqr, "sWqr"), (wv, "sWv")):
                    sp.dma_start(t[:, :], a[name][l]).then_inc(q.w_self, 16)

            def load_sout(l):
                sp.dma_start(wo[:, :, :], a["sWo"][l].rearrange("(c p) n -> p c n", p=P)).then_inc(q.w_sout, 16)

            def load_cross(l):
                for t, name in ((ck, "cWk"), (ckr, "cWkr"), (cv, "cWv"), (cq, "cWq"), (cqr, "cWqr")):
                    sp.dma_start(t[:, :], a[name][l]).then_inc(q.w_cross, 16)

            def load_cout(l):
                sp.dma_start(co[:, :, :], a["cWo"][l].rearrange("(c p) n -> p c n", p=P)).then_inc(q.w_cout, 16)

            def load_ff(l):
                sp.dma_start(f1[:, :], a["fW1"][l]).then_inc(q.w_ff1, 16)
                sp.dma_start(f2[:, :, :], a["fW2"][l].rearrange("(c p) n -> p c n", p=P)).then_inc(q.w_ff2, 16)

            def wait_alone(sem, value):
                sp.wait_ge(sem, value)
                sp.sem_inc(q.sp_passed, 1)

            def swaps(unit0, scores0, per):
                for b in range(B):
                    for j in range(PAIRS):
                        u = b * PAIRS + j
                        n = (b * 2 * PAIRS + PAIRS + j if unit0 == 0 else 5 * PAIRS + u) + 1
                        wait_alone(q.qk_ready, see.at(q.qk_ready, n))
                        if u >= 2:
                            wait_alone(q.scores_full, see.at(q.scores_full, scores0 + per * (u - 1)))
                        for to in range(2):
                            lo, hi = slice(DH * to, DH * to + DH), slice(DH - DH * to, P - DH * to)
                            sp.dma_start(QSW[lo, 2 * (u % 2):2 * (u % 2) + 2, :].bitcast(F32),
                                         QHL[hi, 2 * j:2 * j + 2, b * S:(b + 1) * S].bitcast(F32))\
                                .then_inc((q.swap0, q.swap1)[u % 2], 16)

            load_self(0)
            load_small(0)
            load_sout(0)
            load_cross(0)
            load_cout(0)
            load_ff(0)
            with sp.Fori(0, LAYERS - 1) as l:
                see.enter(l, LAYER)
                swaps(0, 0, 2 * TB)
                wait_alone(q.v_ready, see.at(q.v_ready, TILES))
                wait_alone(q.roped, see.at(q.roped, 4 * PAIRS))
                load_self(l + 1)
                wait_alone(q.y_ready, see.at(q.y_ready, B))
                load_sout(l + 1)
                swaps(4 * PAIRS, LAYER_SELF_SCORES, 4)
                wait_alone(q.v_ready, see.at(q.v_ready, TILES + 2 * B))
                wait_alone(q.roped, see.at(q.roped, 7 * PAIRS))
                load_cross(l + 1)
                wait_alone(q.y_ready, see.at(q.y_ready, 2 * B))
                load_cout(l + 1)
                wait_alone(q.up_ready, see.at(q.up_ready, B * FCH))
                wait_alone(q.y_free, see.at(q.y_free, 3 * B))
                load_small(l + 1)
                wait_alone(q.y_ready, see.at(q.y_ready, 3 * B))
                load_ff(l + 1)
                see.leave(LAYERS - 1)
            see.enter(LAYERS - 1, LAYER)
            swaps(0, 0, 2 * TB)
            swaps(4 * PAIRS, LAYER_SELF_SCORES, 4)
            see.leave(1)
            sp.wait_ge(q.y_ready, LAYERS * LAYER["y_ready"])
            sp.dma_start(w1a, a["w1a"].rearrange("a p n -> p a n")).then_inc(q.w_l1, 16)
            sp.dma_start(w1x, a["w1x"].rearrange("a p n -> p a n")).then_inc(q.w_l1, 16)
            sp.dma_start(gup[2][:, 0:2 * HALF], a["sgu"]).then_inc(q.w_l1, 16)
            sp.dma_start(gdn[2], a["sgd"].rearrange("(c p) n -> p c n", p=HP)).then_inc(q.w_l1, 16)

            def load_expert0(k, e):
                w = (q.w_expert0, q.w_expert1)[k]
                sp.dma_start(ew1[k][:, :], a["W1"][e]).then_inc(w, 16)
                sp.dma_start(ew2[k][:, :].rearrange("p (c n) -> p c n", c=F0CH),
                             a["W2"][e].rearrange("(c p) n -> p c n", p=P)).then_inc(w, 16)
                sp.dma_start(eb1[k], a["b1"][e]).then_inc(w, 16)

            def load_expert1(k, e):
                w = (q.w_glu0, q.w_glu1)[k]
                sp.dma_start(gup[k][:, 0:2 * HALF], a["wup"][e]).then_inc(w, 16)
                sp.dma_start(gdn[k], a["wdn"][e].rearrange("(c p) n -> p c n", p=HP)).then_inc(w, 16)

            for k in range(2):
                load_expert0(k, k)
                load_expert1(k, k)
            with sp.Fori(1, E // 2) as i:
                for k in range(2):
                    sp.wait_ge(q.moe_x_ready, i * 4 - 2 + 2 * k)
                    sp.sem_inc(q.sp_passed, 1)
                    load_expert0(k, i * 2 + k)
            sp.wait_ge(q.parts_ready, 1)
            sp.dma_start(dram_k[:, :, :].rearrange("a p t -> p a t"), Kb[:, 0:3, 0:B * C]).then_inc(q.parts_out, 16)
            sp.wait_ge(q.parts_ready, 3)
            sp.dma_start(dram_q[:, :, :].rearrange("a p t -> p a t"), Qb[:, 0:3, :]).then_inc(q.parts_out, 16)
            sp.wait_ge(q.parts_out, 32)
            sp.wait_ge(q.kst_one, 3)
            for i, (kp, qp) in enumerate(((0, 0), (0, 1), (1, 0), (1, 1), (0, 2), (2, 0))):
                r = slice(i * DK, (i + 1) * DK)
                sp.dma_start(Kst[r, :, :], dram_k[kp].rearrange("(h d) t -> d h t", d=DK)).then_inc(q.parts_in, 16)
                sp.dma_start(Qst[r, :, :], dram_q[qp].rearrange("(h d) t -> d h t", d=DK)).then_inc(q.parts_in, 16)
            for b in range(B):
                sp.wait_ge(q.xshT_ready, b + 1)
                sp.dma_start(dram_s[b], shiftT[:, b, :]).then_inc(q.xsh_out, 16)
                sp.wait_ge(q.xsh_out, 16 * (b + 1))
                sp.dma_start(Qst[SPLITS * DK:SPLITS * DK + 2, :, b * S:(b + 1) * S],
                             dram_s[b].rearrange("(a h) t -> a h t", a=2)).then_inc((q.xsh_in0, q.xsh_in1)[b], 16)
            with sp.Fori(1, E // 2) as i:
                for k in range(2):
                    sp.wait_ge(q.glu_x_ready, i * 4 - 2 + 2 * k)
                    sp.sem_inc(q.sp_passed, 1)
                    load_expert1(k, i * 2 + k)
            for b in range(B):
                sp.wait_ge(q.glu_x_ready, 4 * (E // 2) + b + 1)
                sp.dma_start(out.rearrange("b (t p) d -> p (b t) d", p=P)[:, b * TB:(b + 1) * TB, :],
                             x[:, b * TB:(b + 1) * TB, :]).then_inc(q.stored, 16)
            sp.wait_ge(q.stored, 32)

        @block.gpsimd
        def _(pool):
            see = Seen()
            g = nc.gpsimd
            g.memset(ident[:, :], 0.0)
            g.memset(triu[:, :], 1.0)
            g.memset(ones64[:, :], 1.0)
            g.memset(neghalf[:, :], -0.5)
            g.memset(ones[:, :], 1.0).then_inc(q.pool_step, 1)
            pool.wait_ge(q.pool_step, see.next(q.pool_step))
            g.affine_select(out=ident[:, :], in_=ident[:, :], compare_op=ALU.not_equal, fill=1.0, base=0,
                            pattern=[[-1, P]], channel_multiplier=1).then_inc(q.pool_step, 1)
            g.affine_select(out=once64[:, :], in_=ones64[:, :], compare_op=ALU.is_ge, fill=0.0, base=-(P - C2),
                            pattern=[[0, DH]], channel_multiplier=1).then_inc(q.const, 1)
            g.affine_select(out=triu[:, :], in_=triu[:, :], compare_op=ALU.is_ge, fill=0.0, base=0,
                            pattern=[[1, P]], channel_multiplier=-1).then_inc(q.const, 1)
            pool.wait_ge(q.pool_step, see.next(q.pool_step))
            g.tensor_copy(identb[:, :], ident[:, :]).then_inc(q.const, 1)
            def power():
                pool.wait_ge(q.var_ready, see.next(q.var_ready))
                b = (see.n["var_ready"] - 1) % B
                g.tensor_tensor(rstd[:, b * TB:(b + 1) * TB], var[:, b * TB:(b + 1) * TB],
                                neghalf[:, 0:TB], ALU.pow).then_inc(q.rstd_ready, 1)

            def add_bias(k):
                for b in range(B):
                    pool.wait_ge(q.normed, see.next(q.normed))
                    if b == 0:
                        pool.wait_ge(q.w_small, see.now(q.w_small))
                    v = y[:, b * TB:(b + 1) * TB, :]
                    g.tensor_tensor(v, v, lrow[:, k:k + 1, :].broadcast_to([P, TB, D]), ALU.add).then_inc(q.y_free, 1)

            def rope_sum(w):
                pool.wait_ge(q.roped, see.next(q.roped))
                r = rot[:, (see.n["roped"] - 1) % 2]
                g.tensor_tensor(r[:, 0, 0:w], r[:, 0, 0:w], r[:, 1, 0:w], ALU.add).then_inc(q.rope_ready, 1)

            def sum_tiles(u):
                to = acc[:, u % 2, :, :]
                for k in range(1, TB):
                    pool.wait_ge(q.probs_ready, see.at(q.probs_ready, 2 * (u * TB + k + 1)))
                    if k == 1 and u >= 2:
                        pool.wait_ge(q.den_full, see.at(q.den_full, u - 1))
                    if k > 1:
                        pool.wait_ge(q.summed, see.now(q.summed))
                    g.tensor_tensor(to, ring[:, 0:2, :] if k == 1 else to, ring[:, 2 * k:2 * k + 2, :],
                                    ALU.add).then_inc(q.summed, 1)
                    see.expect(q.summed)

            def norm_powers(bias=None):
                for b in range(B):
                    power()
                if bias is not None:
                    add_bias(bias)

            norm_powers()
            see.expect(q.normed, 2)
            norm_powers()
            see.expect(q.normed, 2)
            with pool.Fori(0, LAYERS) as l:
                see.enter(l, LAYER)
                see.expect(q.w_small, 32)
                norm_powers(0)
                for _ in range(4 * PAIRS):
                    rope_sum(S)
                for u in range(B * PAIRS):
                    if not direct(u // PAIRS, u % PAIRS, TB):
                        sum_tiles(u)
                for _ in range(PAIRS):
                    rope_sum(B * C)
                norm_powers(1)
                for _ in range(2 * PAIRS):
                    rope_sum(S)
                norm_powers(2)
                see.leave(LAYERS)
            norm_powers()
            norm_powers()
            norm_powers()
            norm_powers()
            g.memset(QA[:, :], 0.0).then_inc(q.kst_one, 1)
            pool.wait_ge(q.kst_one, 1)
            g.memset(Kst[DH:P, :, :], 0.0).then_inc(q.kst_one, 1)
            pool.wait_ge(q.kst_one, 2)
            g.memset(Kst[0:DH, :, :], 1.0).then_inc(q.kst_one, 1)
            norm_powers()

        @block.vector
        def _(dve):
            see = Seen()
            v = nc.vector

            def link(ins):
                ins.then_inc(q.dve_step, 1)
                dve.wait_ge(q.dve_step, see.next(q.dve_step))

            def alone():
                if see.turn is not None:
                    dve.sem_inc(q.dve_passed, 1)

            def norm(src, dst, rms=False, last=q.normed):
                for b in range(B):
                    ts = range(b * TB, (b + 1) * TB)
                    w = slice(b * TB, (b + 1) * TB)
                    for t in ts:
                        ins = v.bn_stats(stats[:, t, :], src[:, t, :])
                    link(ins)
                    alone()
                    for t in ts:
                        ins = v.bn_aggr(mv[:, t, :], stats[:, t, :])
                    link(ins)
                    if rms:
                        link(v.tensor_tensor(var[:, w], mv[:, w, 0], mv[:, w, 0], ALU.mult))
                        link(v.tensor_tensor(var[:, w], var[:, w], mv[:, w, 1], ALU.add))
                        v.tensor_scalar(var[:, w], var[:, w], 1.0e-16, None, ALU.max).then_inc(q.var_ready, 1)
                    else:
                        v.tensor_scalar(var[:, w], mv[:, w, 1], 1.0e-5, None, ALU.add).then_inc(q.var_ready, 1)
                for b in range(B):
                    dve.wait_ge(q.rstd_ready, see.next(q.rstd_ready))
                    for t in range(b * TB, (b + 1) * TB):
                        if rms:
                            ins = v.tensor_scalar(dst[:, t, :], src[:, t, :], rstd[:, t:t + 1], None, ALU.mult)
                        else:
                            ins = v.tensor_scalar(dst[:, t, :], src[:, t, :], mv[:, t, 0:1], rstd[:, t:t + 1],
                                                  ALU.subtract, ALU.mult)
                    ins.then_inc(last, 1)

            def masks():
                dve.wait_ge(q.mask_in, see.next(q.mask_in, 48))
                v.tensor_scalar(maskrow[:, :], maskr8, 1.0, -NEG, ALU.subtract, ALU.mult)
                v.tensor_scalar(maskcol[:, :], maskc8[:, :], 1.0, -NEG * SCALE, ALU.subtract, ALU.mult)
                v.tensor_scalar(maskq[:, :, :], m1u8, NEG, None, ALU.mult).then_inc(q.mask_ready, 1)

            def linear_attention():
                for b in range(B):
                    w = slice(b * S, (b + 1) * S)
                    for k in range(2):
                        dve.wait_ge(q.lin_full, see.next(q.lin_full))
                        src, col = bank[3 * b + k], cols[:, k:k + 1]
                        v.tensor_scalar(elu[:, k, 0, :], src[:, :], col, 0.0, ALU.add, ALU.min).then_inc(q.lin_min, 1)
                        v.tensor_scalar(elu[:, k, 1, :], src[:, :], col, 0.0, ALU.add, ALU.max).then_inc(q.dve_step, 1)
                        see.expect(q.dve_step)
                    dve.wait_ge(q.lin_full, see.next(q.lin_full))
                    link(v.tensor_scalar(v0T[:, w], bank[3 * b + 2][:, :], cols[:, 2:3], None, ALU.add))
                    for k in range(2):
                        dve.wait_ge(q.lin_exp, see.next(q.lin_exp))
                        o = (q0T, k0T)[k][:, w]
                        link(v.scalar_tensor_tensor(out=o, in0=elu[:, k, 0, :], scalar=-1.0, in1=elu[:, k, 1, :],
                                                    op0=ALU.add, op1=ALU.add))
                        link(v.tensor_scalar(o, o, 1.0, None, ALU.add))
                    link(v.tensor_tensor_reduce(z0T[:, w], k0T[:, w], v0T[:, w], 1.0, 0.0, ALU.mult, ALU.add, kv[:, 2 * b:2 * b + 1]))
                    link(v.tensor_reduce(kv[:, 2 * b + 1:2 * b + 2], k0T[:, w], AX.X, ALU.add))
                    link(v.tensor_scalar(z0T[:, w], q0T[:, w], kv[:, 2 * b + 1:2 * b + 2], 1.0e-6, ALU.mult, ALU.add))
                    link(v.reciprocal(z0T[:, w], z0T[:, w]))
                    v.scalar_tensor_tensor(out=o0T[:, w], in0=q0T[:, w], scalar=kv[:, 2 * b:2 * b + 1], in1=z0T[:, w],
                                           op0=ALU.mult, op1=ALU.mult).then_inc(q.lin_ready, 1)
                for b in range(B):
                    dve.wait_ge(q.gelu_ready, see.next(q.gelu_ready))
                    w = slice(b * TB, (b + 1) * TB)
                    link(v.tensor_tensor(x[:, w, :], x[:, w, :],
                                         g0[:, b * S:(b + 1) * S].rearrange("p (t d) -> p t d", d=D), ALU.add))

            def rope(w, batches):
                see.expect(q.proj_full)
                dve.wait_ge(q.proj_full, see.now(q.proj_full))
                n = see.n["proj_full"] - 1
                src = [bank[2 + 2 * (n % 2) + k][:, 0:w] for k in range(2)]
                if n >= 2:
                    dve.wait_ge(q.qk_ready, see.at(q.qk_ready, n - 1))
                for k, tab in enumerate((cos, sin)):
                    i, o, tb = src[k], rot[:, n % 2, k, 0:w], tab[:, :]
                    if batches:
                        i = i.rearrange("p (b c) -> p b c", b=B)
                        o = o.rearrange("p (b c) -> p b c", b=B)
                        tb = tab[:, 0:C].unsqueeze(1).broadcast_to([P, B, C])
                    ins = v.tensor_tensor(o, i, tb, ALU.mult)
                ins.then_inc(q.roped, 1)

            def lows(dst, j, cols_):
                dve.wait_ge(q.high_ready, see.next(q.high_ready))
                r = rot[:, (see.n["high_ready"] - 1) % 2, 0, 0:cols_.stop - cols_.start]
                for e in range(2):
                    hi, lo = slice(DH * e, DH * e + DH), slice(DH - DH * e, P - DH * e)
                    ins = v.tensor_tensor(dst[lo, 2 * j + e, cols_], r[hi, :], dst[hi, 2 * j + e, cols_], ALU.subtract)
                ins.then_inc(q.qk_ready, 1)

            def maximum_self(b, i):
                h, t = i // TB, i % TB
                dve.wait_ge(q.max_full, see.next(q.max_full))
                alone()
                n = see.n["max_full"] - 1
                v.tensor_tensor_reduce(bank[n % 2][:, :], bank[n % 2][:, :], maskrow[:, b * S:(b + 1) * S], 1.0, -3.0e38,
                                       ALU.add, ALU.max, mx[:, t, h:h + 1]).then_inc(q.max_done, 1)
                see.expect(q.max_done)

            def maximum_cross(b, i):
                h, t = i // 2, i % 2 * 2
                dve.wait_ge(q.max_full, see.next(q.max_full))
                n = see.n["max_full"] - 1
                v.tensor_reduce(mx[:, t:t + 2, h:h + 1], bank[n % 2][:, 0:2 * C].rearrange("p (a c) -> p a c", a=2),
                                AX.X, ALU.max).then_inc(q.max_done, 1)
                see.expect(q.max_done)

            def shifts(heads, done, ready, clamp=None):
                dve.wait_ge(done, see.now(done))
                if clamp is None:
                    link(v.tensor_scalar(shift[:, :, 0:heads], mx[:, :, 0:heads], -1.0, None, ALU.mult))
                else:
                    link(v.tensor_scalar(shift[:, :, 0:heads], mx[:, :, 0:heads], -1.0, clamp, ALU.mult, ALU.min))
                link(v.tensor_copy(shl[:, :, 0:heads], shift[:, :, 0:heads]))
                v.tensor_tensor(shl[:, :, heads:2 * heads], shift[:, :, 0:heads], shl[:, :, 0:heads],
                                ALU.subtract).then_inc(ready, 1)

            def shifts_turned(n, b, full, ready, src):
                dve.wait_ge(full, see.next(full))
                v.tensor_copy(shiftT[0:n, b, :], src[0:n, 0:S // 2].bitcast(BF16)).then_inc(ready, 1)

            def normalise(b, j, tiles):
                see.expect(q.weighed, tiles)
                if direct(b, j, tiles):
                    dve.wait_ge(q.weighed, see.now(q.weighed))
                else:
                    dve.wait_ge(q.den_full, see.next(q.den_full))
                i = 4 + 2 * (j % 2)
                n = see.expect(q.heads_ready) - 1
                if n:
                    dve.wait_ge(q.heads_ready, see.at(q.heads_ready, n))
                link(v.reciprocal(rec, bank[i + 1][:, :]))
                v.tensor_tensor(AT[:, j, b * S:(b + 1) * S], bank[i][:, :], rec, ALU.mult).then_inc(q.heads_ready, 1)

            def residual(b):
                dve.wait_ge(q.out_full, see.next(q.out_full))
                dve.wait_ge(q.y_free, see.next(q.y_free))
                w = y[:, b * TB:(b + 1) * TB, :]
                v.tensor_tensor(w, bank[6 + b][:, :].rearrange("p (t d) -> p t d", d=D), w, ALU.add).then_inc(q.y_ready, 1)
                see.expect(q.y_ready)

            def attend(maximum, nmax, tiles):
                for s in range(PAIRS * tiles):
                    if tiles == 2 and s and s % 2 == 0:
                        normalise(0, s // 2 - 1, tiles)
                    for i in quota(tiles, s):
                        maximum(1, i)
                        if i == nmax - 1:
                            shifts(HEADS, q.max_done, q.shift_ready)
                    if s == TURN[tiles]:
                        shifts_turned(2 * HEADS, 1, q.shiftT_full, q.shiftT_ready, bank[0])
                    if tiles == TB and s > TB and s % TB == 1:
                        normalise(0, s // TB - 1, tiles)
                normalise(0, PAIRS - 1, tiles)
                residual(0)
                for j in range(PAIRS):
                    normalise(1, j, tiles)
                residual(1)

            def layer():
                norm(y, nx, True)
                units = [(t, j, slice(b * S, (b + 1) * S)) for b in range(B) for t in (KHL, QHL) for j in range(PAIRS)]
                for n in range(2 * PAIRS):
                    rope(S, False)
                    if n:
                        lows(*units[n - 1])
                for h in range(HEADS):
                    for t in range(TB):
                        maximum_self(0, h * TB + t)
                    rope(S, False)
                    lows(*units[2 * PAIRS + h - 1])
                lows(*units[-1])
                shifts(HEADS, q.max_done, q.shift_ready)
                shifts_turned(2 * HEADS, 0, q.shiftT_full, q.shiftT_ready, bank[0])
                attend(maximum_self, HEADS * TB, TB)
                units = [(KHLc, j, slice(0, B * C)) for j in range(PAIRS)]
                for j in range(PAIRS):
                    rope(B * C, True)
                    if j:
                        lows(*units[j - 1])
                lows(*units[-1])
                dve.wait_ge(q.y_ready, see.now(q.y_ready))
                norm(y, nx, True)
                units = [(QHL, j, slice(b * S, (b + 1) * S)) for b in range(B) for j in range(PAIRS)]
                for n in range(2 * PAIRS):
                    if n >= PAIRS:
                        for i in range(TB):
                            maximum_cross(0, (n - PAIRS) * TB + i)
                    rope(S, False)
                    if n:
                        lows(*units[n - 1])
                lows(*units[-1])
                shifts(HEADS, q.max_done, q.shift_ready)
                shifts_turned(2 * HEADS, 0, q.shiftT_full, q.shiftT_ready, bank[0])
                attend(maximum_cross, HEADS * TB // 2, 2)
                dve.wait_ge(q.y_ready, see.now(q.y_ready))
                norm(y, nx, True)
                for b in range(B):
                    residual(b)
                dve.wait_ge(q.y_ready, see.now(q.y_ready))

            def rank(lg):
                a4 = lg.unsqueeze(2).broadcast_to([P, TILES, E, E])
                b4 = lg.unsqueeze(3).broadcast_to([P, TILES, E, E])
                t4 = tri8[:, :, :].unsqueeze(1).broadcast_to([P, TILES, E, E])
                link(v.tensor_tensor(cmp1, a4, b4, ALU.is_gt))
                link(v.tensor_tensor(cmp2, a4, b4, ALU.is_equal))
                link(v.tensor_tensor(cmp2, cmp2, t4, ALU.mult))
                link(v.tensor_tensor(cmp1, cmp1, cmp2, ALU.add))
                link(v.tensor_reduce(cnt, cmp1, AX.X, ALU.add))
                link(v.tensor_tensor(cmp1, cmp1, a4, ALU.mult))
                link(v.tensor_reduce(csum, cmp1, AX.X, ALU.add))

            def softmax_of(src):
                link(v.tensor_reduce(row, src, AX.X, ALU.max))
                v.tensor_tensor(centred, src, row.unsqueeze(2).broadcast_to([P, TILES, E]),
                                ALU.subtract).then_inc(q.route_min, 1)
                dve.wait_ge(q.route_exp, see.next(q.route_exp))

            def share(t, src):
                link(v.tensor_reduce(row, src, AX.X, ALU.add))
                link(v.reciprocal(row, row))
                return v.tensor_tensor(t, src, row.unsqueeze(2).broadcast_to([P, TILES, E]), ALU.mult)

            def route0():
                dve.wait_ge(q.router_full, see.next(q.router_full))
                v.tensor_copy(logits, bank[0][:, 0:TILES * E].rearrange("p (t e) -> p t e", e=E)).then_inc(q.logits_read, 1)
                dve.wait_ge(q.logits_read, see.next(q.logits_read))
                softmax_of(logits)
                link(share(ex, ex))
                rank(ex)
                link(v.tensor_scalar(csum, csum, 0.8, None, ALU.is_lt))
                link(v.tensor_scalar(cnt, cnt, 1.5, None, ALU.is_lt))
                link(v.tensor_tensor(keep, csum, cnt, ALU.max))
                v.tensor_tensor(gate0, ex, keep, ALU.mult).then_inc(q.gate_ready, 1)
                for b in range(B):
                    dve.wait_ge(q.gateT_full, see.next(q.gateT_full))
                    v.tensor_copy(gateT[:, b * S:(b + 1) * S], bank[1 + b][0:E, :]).then_inc(q.gateT_ready, 1)

            def route1():
                dve.wait_ge(q.router_full, see.next(q.router_full))
                v.tensor_copy(logits, bank[0][:, 0:TILES * E].rearrange("p (t e) -> p t e", e=E)).then_inc(q.logits_read, 1)
                dve.wait_ge(q.logits_read, see.next(q.logits_read))
                rank(logits)
                softmax_of(logits)
                link(v.tensor_scalar(cnt, cnt, 2.5, None, ALU.is_lt))
                link(v.tensor_tensor(ex, ex, cnt, ALU.mult))
                link(share(gate1, ex))

            def gated(full, ready, gate, e):
                for b in range(B):
                    dve.wait_ge(full, see.next(full))
                    for t in range(TB):
                        w = x[:, b * TB + t, :]
                        sc = 1.0 if gate is None else gate[:, b * TB + t, bass.ds(e, 1)]
                        ins = v.scalar_tensor_tensor(out=w, in0=bank[6 + b][:, t * D:(t + 1) * D], scalar=sc, in1=w,
                                                     op0=ALU.mult, op1=ALU.add)
                    ins.then_inc(ready, 1)
                    see.expect(ready)
                    dve.wait_ge(ready, see.now(ready))

            def decayed():
                link(v.memset(V1[:, :, D:D + 1], 1.0))
                link(v.memset(ones_row, 1.0))
                for b in range(B):
                    w = slice(b * S, (b + 1) * S)
                    dve.wait_ge(q.log_ready, see.next(q.log_ready))
                    v.tensor_tensor_scan(CS[:, w][:, ::-1], ones_row, LG[:, w][:, ::-1], 0.0, ALU.mult,
                                         ALU.add).then_inc(q.sums_ready, 1)
                    dve.wait_ge(q.qkv_full, see.next(q.qkv_full))
                    v.tensor_scalar(q1T[:, w], bank[0][:, :], cols[:, 3:4], 0.0, ALU.add, ALU.max).then_inc(q.qkv_ready, 1)
                    dve.wait_ge(q.qkv_full, see.next(q.qkv_full))
                    link(v.tensor_scalar(k1T[:, w], bank[1][:, :], cols[:, 4:5], 0.0, ALU.add, ALU.max))
                    dve.wait_ge(q.decay_ready, see.next(q.decay_ready))
                    v.tensor_tensor(k1T[:, w], k1T[:, w], EX[:, w], ALU.mult).then_inc(q.qkv_ready, 1)
                    dve.wait_ge(q.qkv_full, see.next(q.qkv_full))
                    v.tensor_tensor(V1[:, b * TB:(b + 1) * TB, 0:D], bank[2][:, :].rearrange("p (t d) -> p t d", d=D),
                                    brow[:, 1:2, :].broadcast_to([P, TB, D]), ALU.add).then_inc(q.qkv_ready, 1)
                    for i in range(TB):
                        dve.wait_ge(q.sc_full, see.next(q.sc_full))
                        src = bank[4 + i % 2]
                        if i < TB - 1:
                            v.tensor_copy(SC[:, i, (i + 1) * P:], src[:, (i + 1) * P:])
                        v.tensor_tensor(SC[:, i, i * P:(i + 1) * P], src[:, i * P:(i + 1) * P], triu[:, :],
                                        ALU.mult).then_inc(q.sc_ready, 1)
                    for t in range(TB):
                        dve.wait_ge(q.num_full, see.next(q.num_full))
                        src = bank[6 + t % 2]
                        link(v.tensor_scalar(row[:, 0:1], src[:, D:D + 1], 1.0e-6, None, ALU.add))
                        link(v.reciprocal(row[:, 0:1], row[:, 0:1]))
                        tt = x[:, b * TB + t, :]
                        v.scalar_tensor_tensor(out=tt, in0=src[:, 0:D], scalar=row[:, 0:1], in1=tt, op0=ALU.mult,
                                               op1=ALU.add).then_inc(q.num_ready, 1)
                        dve.wait_ge(q.num_ready, see.next(q.num_ready))

            def split(dst, src, bias, scale, n):
                f = SPL[:, 0:n]
                link(v.tensor_scalar(f, src, bias, scale, ALU.add, ALU.mult))
                link(v.tensor_copy(dst[0], f))
                link(v.tensor_tensor(f, f, dst[0], ALU.subtract))
                link(v.tensor_copy(dst[1], f))
                return v.tensor_tensor(dst[2], f, dst[1], ALU.subtract)

            def last_attention():
                link(v.memset(Vx, 0.0))
                link(v.memset(Vx[:, :, :, DK:DK + 1], 1.0))
                dve.wait_ge(q.xkq_full, see.next(q.xkq_full))
                split(kparts, bank[0][:, 0:B * C], cols[:, 7:8], 1.0, B * C).then_inc(q.parts_ready, 1)
                dve.wait_ge(q.parts_ready, see.next(q.parts_ready))
                for b in range(B):
                    dve.wait_ge(q.xkq_full, see.next(q.xkq_full))
                    split([p[:, b * S:(b + 1) * S] for p in qparts], bank[1 + b][:, :], cols[:, 6:7],
                          float(DK) ** -0.5, S).then_inc(q.parts_ready, 1)
                    dve.wait_ge(q.parts_ready, see.next(q.parts_ready))
                for i in range(2 * B):
                    dve.wait_ge(q.xv_full, see.next(q.xv_full))
                    link(v.tensor_tensor(Vx[:, i, :, 0:DK], bank[3 + i][:, 0:D].rearrange("p (h d) -> p h d", d=DK),
                                         brow[:, 2, :].rearrange("p (h d) -> p h d", d=DK), ALU.add))
                    v.tensor_scalar(Vx[:, i, :, :], Vx[:, i, :, :], once64[:, 0:1] if i % 2 else 1.0, None,
                                    ALU.mult).then_inc(q.xv_ready, 1)

                def maximum(i):
                    t, h = i // (H1 // 2), i % (H1 // 2) * 2
                    dve.wait_ge(q.xm_full, see.next(q.xm_full))
                    n = see.n["xm_full"] - 1
                    v.tensor_reduce(mx[:, t, h:h + 2], bank[n % 2][:, 0:2 * C].rearrange("p (a c) -> p a c", a=2),
                                    AX.X, ALU.max).then_inc(q.xm_done, 1)
                    see.expect(q.xm_done)

                def divide(g):
                    dve.wait_ge(q.xt_full, see.next(q.xt_full))
                    src = bank[6][:, :].rearrange("p (t j c) -> p t j c", t=TB, j=4)
                    r = rcx.rearrange("p (t j) -> p t j", j=4)
                    link(v.tensor_scalar(r, src[:, :, :, DK], 1.0e-30, None, ALU.max))
                    link(v.reciprocal(r, r))
                    v.tensor_tensor(OX[:, :, 32 * g:32 * g + 32].rearrange("p t (j d) -> p t j d", d=DK),
                                    src[:, :, :, 0:DK], r.unsqueeze(3).broadcast_to([P, TB, 4, DK]),
                                    ALU.mult).then_inc(q.xn_ready, 1)
                    dve.wait_ge(q.xn_ready, see.next(q.xn_ready))

                def xresidual(b):
                    dve.wait_ge(q.xout_full, see.next(q.xout_full))
                    w = x[:, b * TB:(b + 1) * TB, :]
                    v.tensor_tensor(w, bank[7][:, :].rearrange("p (t d) -> p t d", d=D), w, ALU.add).then_inc(q.x_ready, 1)
                    see.expect(q.x_ready)

                for i in range(TB * H1 // 2):
                    maximum(i)
                shifts(H1, q.xm_done, q.xsh_ready, GUARD)
                shifts_turned(2 * H1, 0, q.xshT_full, q.xshT_ready, bank[0])
                for b in range(B):
                    for u in range(H1 // 2):
                        if b and u == 0:
                            divide(H1 // 4 - 1)
                        if b and u == 2:
                            xresidual(0)
                        if u >= 3 and u % 2:
                            divide((u - 3) // 2)
                        if b == 0 and u < len(XQUOTA):
                            for i in range(sum(XQUOTA[:u]), sum(XQUOTA[:u + 1])):
                                maximum(i)
                            if u == len(XQUOTA) - 1:
                                shifts(H1, q.xm_done, q.xsh_ready, GUARD)
                        if b == 0 and u == XTURN:
                            shifts_turned(2 * H1, 1, q.xshT_full, q.xshT_ready, bank[0])
                divide(H1 // 4 - 1)
                xresidual(1)
                dve.wait_ge(q.x_ready, see.now(q.x_ready))

            def glu_products():
                for b in range(B):
                    for c in range(2):
                        dve.wait_ge(q.glu_act, see.next(q.glu_act))
                        dve.wait_ge(q.glu_up_full, see.next(q.glu_up_full))
                        v.tensor_tensor(GA[:, b, c, :], GS[:, b, c, :], bank[2 * c + 1][0:HP, :],
                                        ALU.mult).then_inc(q.glu_ready, 1)

            see.expect(q.const, CONSTS)
            dve.wait_ge(q.x_in, see.next(q.x_in, 16))
            dve.wait_ge(q.const, see.now(q.const))
            norm(x, nx)
            masks()
            dve.wait_ge(q.ctx_full, see.next(q.ctx_full))
            v.tensor_copy(ctxT[:, :], bank[2][:, 0:B * C]).then_inc(q.ctx_ready, 1)
            dve.wait_ge(q.maskT_full, see.next(q.maskT_full))
            v.tensor_copy(maskT[:, :, :], bank[3][:, :].bitcast(BF16).rearrange("p (a c) -> p a c", a=2)).then_inc(q.maskT_ready, 1)
            dve.wait_ge(q.small_in, see.next(q.small_in, 144))
            dve.wait_ge(q.w_early, see.next(q.w_early, 32))
            linear_attention()
            norm(x, y, last=q.normed)
            see.expect(q.normed, 4)
            dve.wait_ge(q.normed, see.now(q.normed))
            with dve.Fori(0, LAYERS) as l:
                see.enter(l, LAYER)
                layer()
                see.leave(LAYERS)
            norm(y, nx, True, last=q.dve_step)
            dve.wait_ge(q.dve_step, see.next(q.dve_step, 2))
            for b in range(B):
                w = slice(b * TB, (b + 1) * TB)
                link(v.tensor_tensor(nx[:, w, :], nx[:, w, :], brow[:, 0:1, :].broadcast_to([P, TB, D]), ALU.mult))
                link(v.tensor_tensor(x[:, w, :], x[:, w, :], nx[:, w, :], ALU.add))
            norm(x, nx)
            route0()
            for b in range(B):
                dve.wait_ge(q.bias_full, see.next(q.bias_full))
                w = slice(b * TB, (b + 1) * TB)
                v.tensor_tensor(x[:, w, :], bank[6 + b][:, :].rearrange("p (t d) -> p t d", d=D), x[:, w, :],
                                ALU.add).then_inc(q.x_ready, 1)
                dve.wait_ge(q.x_ready, see.next(q.x_ready))
            with dve.Fori(0, E // 2) as i:
                see.enter(i, EXPERTS0)
                for k in range(2):
                    gated(q.moe_down_full, q.moe_x_ready, gate0, i * 2 + k)
                see.leave(E // 2)
            norm(x, nx)
            decayed()
            norm(x, nx)
            last_attention()
            norm(x, nx)
            route1()
            with dve.Fori(0, E // 2) as i:
                see.enter(i, EXPERTS1)
                for k in range(2):
                    glu_products()
                    gated(q.glu_down_full, q.glu_x_ready, gate1, i * 2 + k)
                see.leave(E // 2)
            glu_products()
            gated(q.glu_down_full, q.glu_x_ready, None, 0)

        @block.scalar
        def _(act):
            see = Seen()
            c = nc.scalar

            def inputs(gamma=1.0):
                for b in range(B):
                    act.wait_ge(q.hT_full, see.next(q.hT_full))
                    c.activation(hT[:, b * S:(b + 1) * S], bank[6 + b][:, :], ACT.Copy, scale=gamma).then_inc(q.hT_ready, 1)

            def high(dst, j, cols_):
                act.wait_ge(q.rope_ready, see.next(q.rope_ready))
                r = rot[:, (see.n["rope_ready"] - 1) % 2, 0, 0:cols_.stop - cols_.start]
                for e in range(2):
                    hi = slice(DH * e, DH * e + DH)
                    ins = c.activation(dst[hi, 2 * j + e, cols_], r[hi, :], ACT.Copy)
                ins.then_inc(q.high_ready, 1)

            def values(dst, t, weight=1.0):
                act.wait_ge(q.v_full, see.next(q.v_full))
                c.activation(dst, bank[6 + t % 2][:, :], ACT.Copy, scale=weight).then_inc(q.v_ready, 1)

            def exps(tiles, masked):
                for u in range(B * PAIRS * tiles):
                    if u >= 4:
                        act.wait_ge(q.weighed, see.at(q.weighed, see.n.get("weighed", 0) - 3))
                        if tiles == TB:
                            pair, k = divmod(u - 4, TB)
                            act.wait_ge(q.summed, see.at(q.summed, (TB - 1) * pair + max(k, 1)))
                    for e in range(2):
                        act.wait_ge(q.scores_full, see.next(q.scores_full))
                        t = u // (PAIRS * tiles) * TB + u % tiles
                        bias = maskcol[:, t:t + 1] if masked else 0.0
                        c.activation(ring[:, 2 * (u % 4) + e, :], bank[2 + e][:, :], ACT.Exp,
                                     bias=bias, scale=SCALE).then_inc(q.probs_ready, 1)
                    see.expect(q.weighed)

            see.expect(q.const, CONSTS)
            inputs()
            for b in range(B):
                for k in range(2):
                    act.wait_ge(q.lin_min, see.next(q.lin_min))
                    c.activation(elu[:, k, 0, :], elu[:, k, 0, :], ACT.Exp).then_inc(q.lin_exp, 1)
            for b in range(B):
                act.wait_ge(q.gelu_full, see.next(q.gelu_full))
                c.activation(g0[:, b * S:(b + 1) * S], bank[6 + b][:, :], ACT.Gelu_apprx_tanh).then_inc(q.gelu_ready, 1)
            act.wait_ge(q.mask_ready, see.next(q.mask_ready))
            act.wait_ge(q.const, see.now(q.const))
            with act.Fori(0, LAYERS) as l:
                see.enter(l, LAYER)
                act.wait_ge(q.w_small, see.next(q.w_small, 32))
                inputs(lcol[:, 0:1])
                for b in range(B):
                    for n in range(2 * PAIRS):
                        high(QHL if n // PAIRS else KHL, n % PAIRS, slice(b * S, (b + 1) * S))
                        if b:
                            values(Vs[:, n, :], n)
                exps(TB, True)
                for j in range(PAIRS):
                    high(KHLc, j, slice(0, B * C))
                for t in range(2 * B):
                    values(Vc[:, t, :], t, once64[:, 0:1] if t % 2 else 1.0)
                inputs(lcol[:, 1:2])
                for b in range(B):
                    for j in range(PAIRS):
                        high(QHL, j, slice(b * S, (b + 1) * S))
                exps(2, False)
                inputs(lcol[:, 2:3])
                for b in range(B):
                    for k in range(FCH):
                        act.wait_ge(q.up_full, see.next(q.up_full))
                        c.activation(probs[:, b, k, :], bank[2 + k][:, :], ACT.Gelu,
                                     bias=lcol[:, 3 + k:4 + k]).then_inc(q.up_ready, 1)
                see.leave(LAYERS)

            inputs()
            act.wait_ge(q.route_min, see.next(q.route_min))
            c.activation(ex, centred, ACT.Exp).then_inc(q.route_exp, 1)
            with act.Fori(0, E // 2) as i:
                see.enter(i, EXPERTS0)
                for k in range(2):
                    w = (q.w_expert0, q.w_expert1)[k]
                    act.wait_ge(w, see.next(w, 48))
                    for b in range(B):
                        for j in range(F0CH):
                            act.wait_ge(q.moe_up_full, see.next(q.moe_up_full))
                            c.activation(probs[:, b, j, :], bank[2 + j][:, :], ACT.Relu,
                                         bias=eb1[k][:, j:j + 1]).then_inc(q.moe_up_ready, 1)
                see.leave(E // 2)

            inputs()
            for b in range(B):
                w = slice(b * S, (b + 1) * S)
                act.wait_ge(q.decay_full, see.next(q.decay_full))
                c.activation(AG[:, w], bank[3][:, :], ACT.Sigmoid, bias=cols[:, 5:6]).then_inc(q.act_step, 1)
                act.wait_ge(q.act_step, see.next(q.act_step))
                c.activation(AG[:, w], AG[:, w], ACT.Copy, bias=1.0e-6).then_inc(q.act_step, 1)
                act.wait_ge(q.act_step, see.next(q.act_step))
                c.activation(LG[:, w], AG[:, w], ACT.Ln).then_inc(q.log_ready, 1)
                act.wait_ge(q.sums_ready, see.next(q.sums_ready))
                c.activation(EX[:, w], CS[:, w], ACT.Exp).then_inc(q.decay_ready, 1)

            inputs()
            def turned_copy():
                act.wait_ge(q.xo_full, see.next(q.xo_full))
                c.activation(OXT, bank[6][:, :], ACT.Copy).then_inc(q.xoT_ready, 1)

            for b in range(B):
                for u in range(H1 // 2 + 1):
                    if u < H1 // 2:
                        if b or u >= 2:
                            act.wait_ge(q.xpv_full, b * H1 // 2 + u - 1)
                        for n in range(4):
                            act.wait_ge(q.xs_full, see.next(q.xs_full))
                            c.activation(ring[:, u % 2 * 4 + n, :], bank[2 + n % 2][:, :], ACT.Exp).then_inc(q.xp_ready, 1)
                    if u and u % 2 == 0:
                        act.wait_ge(q.xpv_full, b * H1 // 2 + u)
                        g = u // 2 - 1
                        if b or g >= 2:
                            act.wait_ge(q.xt_full, b * H1 // 4 + g - 1)
                        c.activation(O4[g % 2], bank[4 + g % 2][:, :], ACT.Copy).then_inc(q.xo_ready, 1)
                    if b and u == 1:
                        turned_copy()
            turned_copy()

            inputs()
            act.wait_ge(q.route_min, see.next(q.route_min))
            c.activation(ex, centred, ACT.Exp).then_inc(q.route_exp, 1)

            def gates_of_glu():
                for b in range(B):
                    for k in range(2):
                        act.wait_ge(q.glu_gate_full, see.next(q.glu_gate_full))
                        c.activation(GS[:, b, k, :], bank[2 * k][0:HP, :], ACT.Silu).then_inc(q.glu_act, 1)

            with act.Fori(0, E // 2) as i:
                see.enter(i, EXPERTS1)
                for k in range(2):
                    gates_of_glu()
                see.leave(E // 2)
            gates_of_glu()

        @block.tensor
        def _(pe):
            see = Seen()
            mm, turn = nc.tensor.matmul, nc.tensor.transpose
            reader, read_at = [q.const] * 8, [CONSTS] * 8

            def lend(banks, sem):
                n = see.expect(sem)
                for i in banks:
                    reader[i], read_at[i] = sem, n

            def drain():
                for i in range(8):
                    pe.wait_ge(reader[i], see.at(reader[i], read_at[i]))
                    reader[i], read_at[i] = q.const, CONSTS

            def inputs():
                for b in range(B):
                    pe.wait_ge(q.normed, see.next(q.normed))
                    pe.wait_ge(reader[6 + b], see.at(reader[6 + b], read_at[6 + b]))
                    for t in range(TB):
                        ins = turn(bank[6 + b][:, t * P:(t + 1) * P], nx[:, b * TB + t, :], ident[:, :])
                    ins.then_inc(q.hT_full, 1)
                    lend([6 + b], q.hT_ready)

            def hT_of(b):
                return hT[:, b * S:(b + 1) * S]

            def hT_tile(t):
                return hT[:, t * P:(t + 1) * P]

            def hT_wait(b):
                pe.wait_ge(q.hT_ready, see.at(q.hT_ready, see.n["hT_ready"] - (B - 1 - b)))

            def pair(w, wrot, j, rhs, n):
                i = 2 + 2 * (see.n.get("roped", 0) % 2)
                for k in (i, i + 1):
                    pe.wait_ge(reader[k], see.at(reader[k], read_at[k]))
                mm(bank[i][:, 0:n], w[:, j * P:(j + 1) * P], rhs, start=True, stop=True)
                mm(bank[i + 1][:, 0:n], wrot[:, j * P:(j + 1) * P], rhs, start=True, stop=True).then_inc(q.proj_full, 1)
                lend([i, i + 1], q.roped)

            def value_tile(src, w, t):
                i = 6 + t % 2
                pe.wait_ge(reader[i], see.at(reader[i], read_at[i]))
                mm(bank[i][:, :], src, w[:, :], start=True, stop=True).then_inc(q.v_full, 1)
                lend([i], q.v_ready)

            def max_self(b, n):
                h, t = n // TB, n % TB
                i = see.n.get("max_done", 0) % 2
                pe.wait_ge(reader[i], see.at(reader[i], read_at[i]))
                mm(bank[i][:, :], QHL[:, h, b * S + t * P:b * S + (t + 1) * P], KHL[:, h, b * S:(b + 1) * S],
                   start=True, stop=True).then_inc(q.max_full, 1)
                lend([i], q.max_done)

            def max_cross(b, n):
                h, t = n // 2, n % 2 * 2
                i = see.n.get("max_done", 0) % 2
                pe.wait_ge(reader[i], see.at(reader[i], read_at[i]))
                for k in range(2):
                    ins = mm(bank[i][:, k * C:(k + 1) * C], QHL[:, h, b * S + (t + k) * P:b * S + (t + k + 1) * P],
                             KHLc[:, h, b * C:(b + 1) * C], start=True, stop=True)
                ins.then_inc(q.max_full, 1)
                lend([i], q.max_done)

            def shifts_turn(i, heads, ready, full, done):
                pe.wait_ge(ready, see.next(ready))
                pe.wait_ge(reader[i], see.at(reader[i], read_at[i]))
                for t in range(TB):
                    ins = turn(bank[i][0:2 * heads, t * P // 2:(t + 1) * P // 2].bitcast(BF16), shl[:, t, 0:2 * heads],
                               identb[:, :])
                ins.then_inc(full, 1)
                lend([i], done)

            def scores(b, h, k, kt, per_batch, step):
                i = 2 + h % 2
                keys = kt[:, h, b * per_batch + k * step:b * per_batch + k * step + P]
                pe.wait_ge(reader[i], see.at(reader[i], read_at[i]))
                mm(bank[i][:, :], sel[:, h, :], shiftT[0:2 * HEADS, b, :], start=True, stop=False)
                mm(bank[i][:, :], keys, QHL[:, h, b * S:(b + 1) * S], start=False, stop=False)
                mm(bank[i][:, :], keys, QSW[:, h % 4, :], start=False, stop=True).then_inc(q.scores_full, 1)
                lend([i], q.probs_ready)

            def weigh(b, j, k, tiles, vals, ready):
                i = 4 + 2 * (j % 2)
                if k == 0:
                    for bk in (i, i + 1):
                        pe.wait_ge(reader[bk], see.at(reader[bk], read_at[bk]))
                pe.wait_ge(q.probs_ready, see.at(q.probs_ready, ready))
                first, last = k == 0, k == tiles - 1
                for ones_too in range(1 + direct(b, j, tiles)):
                    for e in range(2):
                        h = 2 * j + e
                        lhs = vals[:, b * tiles + k, h * DH:(h + 1) * DH]
                        if ones_too:
                            lhs = once64[:, :] if tiles == 2 and k else ones64[:, :]
                        ins = mm(bank[i + ones_too][DH * e:DH * e + DH, :], lhs,
                                 ring[:, 2 * ((j * tiles + k) % 4) + e, :], start=first, stop=last)
                ins.then_inc(q.weighed, 1)
                see.expect(q.weighed)
                if last and direct(b, j, tiles):
                    lend([i, i + 1], q.heads_ready)

            def sum_up(b, j):
                u, i = b * PAIRS + j, 4 + 2 * (j % 2)
                pe.wait_ge(q.summed, see.next(q.summed, TB - 1))
                for e in range(2):
                    ins = mm(bank[i + 1][DH * e:DH * e + DH, :], ones64[:, :], acc[:, u % 2, e, :], start=True, stop=True)
                ins.then_inc(q.den_full, 1)
                see.expect(q.den_full)
                lend([i, i + 1], q.heads_ready)

            def attend(maximum, tiles, kt, per_batch, step, vals, w):
                steps = PAIRS * tiles
                for b in range(B):
                    pe.wait_ge(q.shiftT_ready, see.now(q.shiftT_ready))
                    for s in range(steps + 1):
                        before = see.n.get("probs_ready", 0)
                        if s < steps:
                            j, k = divmod(s, tiles)
                            if k == 0:
                                swap = (q.swap0, q.swap1)[j % 2]
                                pe.wait_ge(swap, see.next(swap, 32))
                            for e in range(2):
                                scores(b, 2 * j + e, k, kt, per_batch, step)
                        if b and s == 0 and not direct(0, PAIRS - 1, tiles):
                            sum_up(0, PAIRS - 1)
                        if b and s == (0 if tiles == 2 else 2):
                            pe.wait_ge(q.heads_ready, see.now(q.heads_ready))
                            contract(0, lambda c, t: AT[:, c, t * P:(t + 1) * P], w, PAIRS)
                        if s:
                            weigh(b, (s - 1) // tiles, (s - 1) % tiles, tiles, vals, before)
                        if b == 0 and s < steps:
                            for i in quota(tiles, s):
                                maximum(1, i)
                            if s == TURN[tiles]:
                                shifts_turn(0, HEADS, q.shift_ready, q.shiftT_full, q.shiftT_ready)
                        if s > tiles and s % tiles == 1 and not direct(b, s // tiles - 1, tiles):
                            sum_up(b, s // tiles - 1)
                pe.wait_ge(q.heads_ready, see.now(q.heads_ready))
                contract(1, lambda c, t: AT[:, c, t * P:(t + 1) * P], w, PAIRS)

            def contract(b, lhs, w, chunks):
                pe.wait_ge(reader[6 + b], see.at(reader[6 + b], read_at[6 + b]))
                for t in range(TB):
                    for k in range(chunks):
                        ins = mm(bank[6 + b][:, t * P:(t + 1) * P], lhs(k, b * TB + t), w[:, k, :], start=(k == 0),
                                 stop=(k == chunks - 1))
                ins.then_inc(q.out_full, 1)
                lend([6 + b], q.y_ready)

            see.expect(q.const, CONSTS)
            pe.wait_ge(q.const, see.now(q.const))
            pe.wait_ge(q.ctx_in, see.next(q.ctx_in, 16))
            for i in range(2 * B):
                ins = turn(bank[2][:, i * CH:(i + 1) * CH], cin[:, i, :], ident[0:CH, 0:CH])
            ins.then_inc(q.ctx_full, 1)
            lend([2], q.ctx_ready)
            pe.wait_ge(q.mask_ready, see.next(q.mask_ready))
            for k in range(2):
                for t in range(TB):
                    c0 = k * (S // 2) + t * P // 2
                    ins = turn(bank[3][:, c0:c0 + P // 2].bitcast(BF16), maskq[:, t, k * C2:k * C2 + P], identb[:, :])
            ins.then_inc(q.maskT_full, 1)
            lend([3], q.maskT_ready)

            inputs()
            pe.wait_ge(q.w_early, see.next(q.w_early, 32))
            pe.wait_ge(q.small_in, see.next(q.small_in, 144))
            for b in range(B):
                hT_wait(b)
                for k in range(3):
                    i = 3 * b + k
                    pe.wait_ge(reader[i], see.at(reader[i], read_at[i]))
                    mm(bank[i][:, :], wa[:, k, :], hT_of(b), start=True, stop=True).then_inc(q.lin_full, 1)
            for b in range(B):
                pe.wait_ge(q.lin_ready, see.next(q.lin_ready))
                pe.wait_ge(reader[6 + b], see.at(reader[6 + b], read_at[6 + b]))
                for t in range(TB):
                    o = bank[6 + b][:, t * P:(t + 1) * P]
                    mm(o, ones[:, :], rows[:, 0, :], start=True, stop=False)
                    ins = mm(o, o0T[:, b * S + t * P:b * S + (t + 1) * P], wa[:, 3, :], start=False, stop=True)
                ins.then_inc(q.gelu_full, 1)
                lend([6 + b], q.gelu_ready)
            see.expect(q.normed, 2)
            drain()

            with pe.Fori(0, LAYERS) as l:
                see.enter(l, LAYER)
                see.expect(q.w_small, 32)
                pe.wait_ge(q.w_self, see.next(q.w_self, 80))
                inputs()
                for b in range(B):
                    hT_wait(b)
                    low0 = see.n.get("qk_ready", 0)
                    for h in range(HEADS):
                        w, wr_ = (wk, wkr) if h < PAIRS else (wq, wqr)
                        pair(w, wr_, h % PAIRS, hT_of(b), S)
                        if b:
                            pe.wait_ge(q.qk_ready, see.at(q.qk_ready, PAIRS + h // 2 + 1 + low0))
                            for t in range(TB):
                                max_self(0, h * TB + t)
                            value_tile(hT_tile(h), wv, h)
                see.expect(q.qk_ready, 4 * PAIRS)
                see.expect(q.rope_ready, 4 * PAIRS)
                shifts_turn(0, HEADS, q.shift_ready, q.shiftT_full, q.shiftT_ready)
                pe.wait_ge(q.qk_ready, see.now(q.qk_ready))
                pe.wait_ge(q.rope_ready, see.now(q.rope_ready))
                pe.wait_ge(q.v_ready, see.now(q.v_ready))
                pe.wait_ge(q.w_sout, see.next(q.w_sout, 16))
                attend(max_self, TB, KHL, S, P, Vs, wo)

                pe.wait_ge(q.w_cross, see.next(q.w_cross, 80))
                for j in range(PAIRS):
                    pair(ck, ckr, j, ctxT[:, :], B * C)
                for t in range(2 * B):
                    c0 = t // 2 * C + t % 2 * C2
                    value_tile(ctxT[:, c0:c0 + P], cv, t)
                inputs()
                queries0 = see.n["qk_ready"] + PAIRS
                for b in range(B):
                    hT_wait(b)
                    for j in range(PAIRS):
                        pair(cq, cqr, j, hT_of(b), S)
                        if b:
                            pe.wait_ge(q.qk_ready, see.at(q.qk_ready, queries0 + j + 1))
                            for i in range(TB):
                                max_cross(0, j * TB + i)
                see.expect(q.qk_ready, 3 * PAIRS)
                see.expect(q.rope_ready, 3 * PAIRS)
                pe.wait_ge(q.qk_ready, see.now(q.qk_ready))
                pe.wait_ge(q.rope_ready, see.now(q.rope_ready))
                pe.wait_ge(q.v_ready, see.now(q.v_ready))
                shifts_turn(0, HEADS, q.shift_ready, q.shiftT_full, q.shiftT_ready)
                pe.wait_ge(q.w_cout, see.next(q.w_cout, 16))
                attend(max_cross, 2, KHLc, C, C2, Vc, co)

                pe.wait_ge(q.w_ff1, see.next(q.w_ff1, 16))
                pe.wait_ge(q.w_ff2, see.next(q.w_ff2, 16))
                inputs()
                for b in range(B):
                    hT_wait(b)
                    for k in range(FCH):
                        pe.wait_ge(reader[2 + k], see.at(reader[2 + k], read_at[2 + k]))
                        mm(bank[2 + k][:, :], f1[:, k * P:(k + 1) * P], hT_of(b), start=True, stop=True)\
                            .then_inc(q.up_full, 1)
                        lend([2 + k], q.up_ready)
                for b in range(B):
                    pe.wait_ge(q.up_ready, see.at(q.up_ready, see.n["up_ready"] - (B - 1 - b) * FCH))
                    contract(b, lambda k, t: probs[:, b, k, (t % TB) * P:(t % TB + 1) * P], f2, FCH)
                drain()
                see.leave(LAYERS)

            def router(w, bias):
                pe.wait_ge(reader[0], see.at(reader[0], read_at[0]))
                for t in range(TILES):
                    if t % TB == 0:
                        hT_wait(t // TB)
                    o = bank[0][:, t * E:(t + 1) * E]
                    ins = mm(o, hT_tile(t), w, start=True, stop=not bias)
                    if bias:
                        ins = mm(o, ones[:, :], lrow8[:, :], start=False, stop=True)
                ins.then_inc(q.router_full, 1)
                lend([0], q.logits_read)

            inputs()
            router(wr[:, 0, :], True)
            pe.wait_ge(q.gate_ready, see.next(q.gate_ready))
            for b in range(B):
                pe.wait_ge(reader[1 + b], see.at(reader[1 + b], read_at[1 + b]))
                for t in range(TB):
                    ins = turn(bank[1 + b][0:E, t * P:(t + 1) * P], gate0[:, b * TB + t, :], ident[:, :])
                ins.then_inc(q.gateT_full, 1)
                lend([1 + b], q.gateT_ready)
            for b in range(B):
                pe.wait_ge(q.gateT_ready, see.at(q.gateT_ready, b + 1))
                pe.wait_ge(reader[6 + b], see.at(reader[6 + b], read_at[6 + b]))
                for t in range(TB):
                    ins = mm(bank[6 + b][:, t * P:(t + 1) * P], gateT[:, b * S + t * P:b * S + (t + 1) * P], b2e[:, :],
                             start=True, stop=True)
                ins.then_inc(q.bias_full, 1)
                lend([6 + b], q.x_ready)
            drain()
            with pe.Fori(0, E // 2) as i:
                see.enter(i, EXPERTS0)
                for k in range(2):
                    w = (q.w_expert0, q.w_expert1)[k]
                    pe.wait_ge(w, see.next(w, 48))
                    for b in range(B):
                        for j in range(F0CH):
                            pe.wait_ge(reader[2 + j], see.at(reader[2 + j], read_at[2 + j]))
                            mm(bank[2 + j][:, :], ew1[k][:, j * P:(j + 1) * P], hT_of(b), start=True, stop=True)\
                                .then_inc(q.moe_up_full, 1)
                            lend([2 + j], q.moe_up_ready)
                    for b in range(B):
                        pe.wait_ge(q.moe_up_ready, see.at(q.moe_up_ready, see.n["moe_up_ready"] - (B - 1 - b) * F0CH))
                        pe.wait_ge(reader[6 + b], see.at(reader[6 + b], read_at[6 + b]))
                        for t in range(TB):
                            for j in range(F0CH):
                                ins = mm(bank[6 + b][:, t * P:(t + 1) * P], probs[:, b, j, t * P:(t + 1) * P],
                                         ew2[k][:, j * D:(j + 1) * D], start=(j == 0), stop=(j == F0CH - 1))
                        ins.then_inc(q.moe_down_full, 1)
                        lend([6 + b], q.moe_x_ready)
                drain()
                see.leave(E // 2)

            pe.wait_ge(q.w_l1, see.next(q.w_l1, 64))
            inputs()
            for b in range(B):
                hT_wait(b)
                pe.wait_ge(reader[3], see.at(reader[3], read_at[3]))
                mm(bank[3][:, :], w1a[:, 3, :], hT_of(b), start=True, stop=True).then_inc(q.decay_full, 1)
                lend([3], q.log_ready)
                for k in range(2):
                    pe.wait_ge(reader[k], see.at(reader[k], read_at[k]))
                    mm(bank[k][:, :], w1a[:, k, :], hT_of(b), start=True, stop=True).then_inc(q.qkv_full, 1)
                    lend([k], q.qkv_ready)
                pe.wait_ge(reader[2], see.at(reader[2], read_at[2]))
                for t in range(TB):
                    ins = mm(bank[2][:, t * P:(t + 1) * P], hT_tile(b * TB + t), w1a[:, 2, :], start=True, stop=True)
                ins.then_inc(q.qkv_full, 1)
                lend([2], q.qkv_ready)
                pe.wait_ge(q.qkv_ready, see.now(q.qkv_ready))
                for j in range(TB):
                    pe.wait_ge(reader[4 + j % 2], see.at(reader[4 + j % 2], read_at[4 + j % 2]))
                    mm(bank[4 + j % 2][:, j * P:], k1T[:, b * S + j * P:b * S + (j + 1) * P],
                       q1T[:, b * S + j * P:(b + 1) * S], start=True, stop=True).then_inc(q.sc_full, 1)
                    lend([4 + j % 2], q.sc_ready)
                for t in range(TB):
                    pe.wait_ge(q.sc_ready, see.at(q.sc_ready, b * TB + t + 1))
                    pe.wait_ge(reader[6 + t % 2], see.at(reader[6 + t % 2], read_at[6 + t % 2]))
                    for j in range(t + 1):
                        ins = mm(bank[6 + t % 2][:, 0:D + 1], SC[:, j, t * P:(t + 1) * P], V1[:, b * TB + j, 0:D + 1],
                                 start=(j == 0), stop=(j == t))
                    ins.then_inc(q.num_full, 1)
                    lend([6 + t % 2], q.num_ready)

            inputs()
            for k in (0, 1, 2, 3, 4, 5):
                pe.wait_ge(reader[k], see.at(reader[k], read_at[k]))
            mm(bank[0][:, 0:B * C], w1x[:, 1, :], ctxT[:, :], start=True, stop=True).then_inc(q.xkq_full, 1)
            lend([0], q.parts_ready)
            for b in range(B):
                hT_wait(b)
                mm(bank[1 + b][:, :], w1x[:, 0, :], hT_of(b), start=True, stop=True).then_inc(q.xkq_full, 1)
                lend([1 + b], q.parts_ready)
            for i in range(2 * B):
                pe.wait_ge(reader[3 + i], see.at(reader[3 + i], read_at[3 + i]))
                c0 = i // 2 * C + i % 2 * C2
                mm(bank[3 + i][:, 0:D], ctxT[:, c0:c0 + P], w1x[:, 2, :], start=True, stop=True)\
                    .then_inc(q.xv_full, 1)
                lend([3 + i], q.xv_ready)
            pe.wait_ge(q.parts_in, see.next(q.parts_in, 16 * 2 * SPLITS))

            def xmax(b, n):
                t, h = n // (H1 // 2), n % (H1 // 2) * 2
                i = see.n.get("xm_done", 0) % 2
                pe.wait_ge(reader[i], see.at(reader[i], read_at[i]))
                for k in range(2):
                    o = bank[i][:, k * C:(k + 1) * C]
                    mm(o, Qst[:, h + k, b * S + t * P:b * S + (t + 1) * P], Kst[:, h + k, b * C:(b + 1) * C],
                       start=True, stop=False)
                    ins = mm(o, identb[:, :], maskq[:, t, :], start=False, stop=True)
                ins.then_inc(q.xm_full, 1)
                lend([i], q.xm_done)

            def xscores(b, u):
                for e in range(2):
                    for k in range(2):
                        pe.wait_ge(reader[2 + k], see.at(reader[2 + k], read_at[2 + k]))
                        c0 = b * C + k * C2
                        mm(bank[2 + k][:, :], Kst[:, 2 * u + e, c0:c0 + P], Qst[:, 2 * u + e, b * S:(b + 1) * S],
                           start=True, stop=False)
                        mm(bank[2 + k][:, :], identb[:, :], maskT[:, k, :], start=False, stop=True).then_inc(q.xs_full, 1)
                        lend([2 + k], q.xp_ready)

            def xweigh(b, u):
                g = u // 2
                if u % 2 == 0:
                    pe.wait_ge(reader[4 + g % 2], see.at(reader[4 + g % 2], read_at[4 + g % 2]))
                pe.wait_ge(q.xp_ready, 4 * (b * H1 // 2 + u + 1))
                for k in range(2):
                    for e in range(2):
                        j = u % 2 * 2 + e
                        ins = mm(bank[4 + g % 2][32 * j:32 * j + 32, :], Vx[:, 2 * b + k, 2 * u + e, :],
                                 ring[:, u % 2 * 4 + 2 * e + k, :], start=(k == 0), stop=(k == 1))
                ins.then_inc(q.xpv_full, 1)
                if u % 2:
                    lend([4 + g % 2], q.xo_ready)

            def xturn(b, g):
                pe.wait_ge(q.xo_ready, b * H1 // 4 + g + 1)
                pe.wait_ge(reader[6], see.at(reader[6], read_at[6]))
                for t in range(TB):
                    ins = turn(bank[6][:, t * P:(t + 1) * P], O4[g % 2][:, t * P:(t + 1) * P], ident[:, :])
                ins.then_inc(q.xt_full, 1)
                lend([6], q.xn_ready)

            def xgather():
                pe.wait_ge(q.xn_ready, see.now(q.xn_ready))
                for t in range(TB):
                    ins = turn(bank[6][:, t * P:(t + 1) * P], OX[:, t, :], ident[:, :])
                ins.then_inc(q.xo_full, 1)
                lend([6], q.xoT_ready)

            def xproject():
                pe.wait_ge(q.xoT_ready, see.now(q.xoT_ready))
                pe.wait_ge(reader[7], see.at(reader[7], read_at[7]))
                for t in range(TB):
                    o = bank[7][:, t * P:(t + 1) * P]
                    mm(o, ones[:, :], rows[:, 1, :], start=True, stop=False)
                    ins = mm(o, OXT[:, t * P:(t + 1) * P], w1x[:, 3, :], start=False, stop=True)
                ins.then_inc(q.xout_full, 1)
                lend([7], q.x_ready)

            for n in range(TB * H1 // 2):
                xmax(0, n)
            shifts_turn(0, H1, q.xsh_ready, q.xshT_full, q.xshT_ready)
            for b in range(B):
                w = (q.xsh_in0, q.xsh_in1)[b]
                pe.wait_ge(w, see.next(w, 16))
                for u in range(H1 // 2 + 1):
                    if u < H1 // 2:
                        xscores(b, u)
                    if b and u == 0:
                        xturn(0, H1 // 4 - 1)
                    if b and u == 1:
                        xgather()
                    if b and u == 2:
                        xproject()
                    if u >= 3 and u % 2:
                        xturn(b, (u - 3) // 2)
                    if u:
                        xweigh(b, u - 1)
                    if b == 0 and u < len(XQUOTA):
                        for n in range(sum(XQUOTA[:u]), sum(XQUOTA[:u + 1])):
                            xmax(1, n)
                    if b == 0 and u == XTURN:
                        shifts_turn(0, H1, q.xsh_ready, q.xshT_full, q.xshT_ready)
            xturn(1, H1 // 4 - 1)
            xgather()
            xproject()

            inputs()
            router(wr[:, 1, :], False)

            def glu(up, down):
                for b in range(B):
                    hT_wait(b)
                    for k in range(2):
                        pe.wait_ge(reader[2 * k], see.at(reader[2 * k], read_at[2 * k]))
                        mm(bank[2 * k][0:HP, :], up[:, k * HP:(k + 1) * HP], hT_of(b), start=True, stop=True)\
                            .then_inc(q.glu_gate_full, 1)
                        lend([2 * k], q.glu_act)
                        pe.wait_ge(reader[2 * k + 1], see.at(reader[2 * k + 1], read_at[2 * k + 1]))
                        mm(bank[2 * k + 1][0:HP, :], up[:, HALF + k * HP:HALF + (k + 1) * HP], hT_of(b), start=True,
                           stop=True).then_inc(q.glu_up_full, 1)
                        lend([2 * k + 1], q.glu_ready)
                for b in range(B):
                    pe.wait_ge(q.glu_ready, see.at(q.glu_ready, see.n["glu_ready"] - (B - 1 - b) * 2))
                    pe.wait_ge(reader[6 + b], see.at(reader[6 + b], read_at[6 + b]))
                    for t in range(TB):
                        for k in range(2):
                            ins = mm(bank[6 + b][:, t * P:(t + 1) * P], GA[:, b, k, t * P:(t + 1) * P], down[:, k, :],
                                     start=(k == 0), stop=(k == 1))
                    ins.then_inc(q.glu_down_full, 1)
                    lend([6 + b], q.glu_x_ready)

            drain()
            for b in range(B):
                hT_wait(b)
            with pe.Fori(0, E // 2) as i:
                see.enter(i, EXPERTS1)
                for k in range(2):
                    w = (q.w_glu0, q.w_glu1)[k]
                    pe.wait_ge(w, see.next(w, 32))
                    glu(gup[k], gdn[k])
                drain()
                see.leave(E // 2)
            glu(gup[2], gdn[2])


def kernel(**inputs):
    import numpy as np
    import concourse.bacc as bacc
    from concourse.bass_utils import run_bass_kernel_spmd

    def arr(name):
        return np.ascontiguousarray(np.asarray(inputs[name]))

    def half_swapped(w):
        w = w.reshape(LAYERS, D, HEADS, DH)
        return np.concatenate([w[..., 16:32], w[..., 0:16], w[..., 32:]], axis=-1).reshape(LAYERS, D, INNER)

    l0 = {n: arr("L0_xattn_" + n) for n in ("sWq", "sWk", "sWv", "sWo", "cWq", "cWk", "cWv", "cWo", "fW1", "fW2")}
    for n in ("sWq", "sWk", "cWq", "cWk"):
        l0[n + "r"] = half_swapped(l0[n])
    gam = [arr("L0_xattn_" + n)[:, :, None] for n in ("sg", "cg", "fg")]
    fb1 = arr("L0_xattn_fb1").reshape(LAYERS, FCH, P).transpose(0, 2, 1)
    arrays = dict(
        x=arr("x"), ctx=arr("ctx_1024"),
        mask1=arr("mask_BxS_bf1"), mask1c=arr("mask_BxS_bf1").reshape(TILES, P).T, mask2=arr("mask_1x1xSxS2_bk1").reshape(S, C),
        wa=np.stack([arr("L0_attn_" + n) for n in ("wq", "wk", "wv", "wo")]),
        cols=np.stack([arr(n) for n in ("L0_attn_bq", "L0_attn_bk", "L0_attn_bv", "L1_attn_b_q", "L1_attn_b_k",
                                        "L1_attn_b_a", "L1_xattn_bq", "L1_xattn_bk")], axis=1),
        rows=np.stack([arr("L0_attn_bo"), arr("L1_xattn_bo"), arr("L1_xattn_bo")]),
        brow=np.stack([arr("L0_xattn_g_out"), arr("L1_attn_b_v"), arr("L1_xattn_bv")]),
        br=arr("L0_ffn_br"), wr=np.stack([arr("L0_ffn_Wr"), arr("L1_ffn_gate_w").T]),
        lcol=np.concatenate(gam + [fb1], axis=2),
        lrow=np.stack([arr("L0_xattn_" + n) for n in ("sbo", "cbo", "fb2")], axis=1),
        W1=arr("L0_ffn_W1"), W2=arr("L0_ffn_W2"), b2=arr("L0_ffn_b2"),
        b1=arr("L0_ffn_b1").reshape(E, F0CH, P).transpose(0, 2, 1),
        w1a=np.stack([arr("L1_attn_" + n).T for n in ("W_q", "W_k", "W_v", "W_a")]),
        w1x=np.stack([arr("L1_xattn_" + n).T for n in ("Wq", "Wk", "Wv", "Wo")]),
        wup=arr("L1_ffn_w_up").transpose(0, 2, 1), wdn=arr("L1_ffn_w_down").transpose(0, 2, 1),
        sgu=np.concatenate([arr("L1_ffn_sg_gate").T, arr("L1_ffn_sg_up").T], axis=1), sgd=arr("L1_ffn_sg_down").T,
        **l0)

    rotd = 32
    inv = (1.0 / 10000.0 ** (np.arange(0, rotd, 2, dtype=np.float32) / np.float32(rotd))).astype(np.float32)
    ang = (np.arange(S, dtype=np.float32)[:, None] * inv[None, :]).astype(np.float32)
    cos, sin = np.cos(ang).T.astype(np.float32), np.sin(ang).T.astype(np.float32)
    one = np.concatenate([cos, cos, np.ones((DH - rotd, S), np.float32)])
    two = np.concatenate([-sin, sin, np.zeros((DH - rotd, S), np.float32)])
    arrays["cos"], arrays["sin"] = np.concatenate([one, one]), np.concatenate([two, two])
    arrays["tri8"] = np.tril(np.ones((E, E), np.float32))
    sel = np.zeros((2, HEADS, HEADS, P), np.float32)
    for h in range(HEADS):
        sel[:, h, h, :] = 1.0
    import ml_dtypes
    arrays["sel"] = sel.reshape(2 * HEADS, HEADS, P).astype(ml_dtypes.bfloat16)

    nc = bacc.Bacc("TRN2", target_bir_lowering=False, num_devices=1)
    nc.disable_value_cache = True
    feeds, aps = {}, {}
    for name, v in arrays.items():
        v = np.ascontiguousarray(v)
        feeds["in_" + name] = v
        aps[name] = nc.dram_tensor("in_" + name, v.shape, mybir.dt.from_np(v.dtype), kind="ExternalInput").ap()
    out = nc.dram_tensor("out_x", (B, S, D), F32, kind="ExternalOutput").ap()
    decoder(nc, aps, out)
    r = run_bass_kernel_spmd(nc, [feeds], core_ids=[0])
    return r.results[0]["out_x"]
```

```python
import concourse.bass as bass
from concourse import mybir
from contextlib import ExitStack

F32 = mybir.dt.float32
BF16 = mybir.dt.bfloat16
F32R = mybir.dt.float32r
U8 = mybir.dt.uint8
ALU = mybir.AluOpType
ACT = mybir.ActivationFunctionType
AX = mybir.AxisListType

P = 128
B, S, D = 2, 512, 128
NT = B * S
TB = S // P
TILES = B * TB
C = 154
CH = C // 2
C2 = C - P
LAYERS, HEADS, DH = 4, 8, 64
PAIRS = HEADS // 2
INNER = HEADS * DH
FF, FCH = 512, 512 // P
E = 8
F0, F0CH = 512, 512 // P
HALF = 192
HP = HALF // 2
H1, DK = 16, 8
SPLITS = 6
SCALE = DH ** -0.5
CONSTS = 3
NEG = -float(2.0 ** 100)
GUARD = 1.0e29

LAYER = dict(
    var_ready=6, rstd_ready=6, normed=6, hT_full=6, hT_ready=6, y_free=6,
    proj_full=28, roped=28, rope_ready=28, high_ready=28, qk_ready=28, swap0=256, swap1=256,
    v_full=12, v_ready=12,
    max_full=64 + 32, max_done=64 + 32, shift_ready=16, shiftT_full=16, shiftT_ready=16,
    scores_full=64 + 32, probs_ready=64 + 32, weighed=32 + 16, summed=21, den_full=7,
    heads_ready=16,
    out_full=6, y_ready=6, up_full=8, up_ready=8,
    w_self=80, w_sout=16, w_cross=80, w_cout=16, w_ff1=16, w_ff2=16, w_small=32, dve_step=72,
)
EXPERTS0 = dict(moe_up_full=16, moe_up_ready=16, moe_down_full=4, moe_x_ready=4, w_expert0=48, w_expert1=48,
                split_high=2, split_ready=2)
EXPERTS1 = dict(glu_gate_full=8, glu_up_full=8, glu_act=8, glu_ready=8, glu_down_full=4, glu_x_ready=4,
                w_glu0=32, w_glu1=32, split_high=2, split_ready=2)

LAYER_SELF_SCORES = 2 * PAIRS * B * TB
UNITS = B * PAIRS
QUOTA = {TB: (2, 2, 2, 2), 2: (2, 2)}


def quota(tiles, step):
    return range(sum(QUOTA[tiles][:step]), sum(QUOTA[tiles][:step + 1]))


XQUOTA = (6, 6, 6, 6, 6, 2)
XTURN = 6


def quota(tiles, step):
    return range(sum(QUOTA[tiles][:step]), sum(QUOTA[tiles][:step + 1]))


CONTRACT = {TB: 3, 2: 1}
TURN = {TB: 1, 2: 0}


def direct(b, j, tiles):
    return tiles == 2 or (b, j) == (B - 1, PAIRS - 1)


class Seen:

    def __init__(self):
        self.n, self.turn, self.per = {}, None, {}

    def at(self, sem, n):
        per = self.per.get(sem.name, 0) if self.turn is not None else 0
        return n + self.turn * per if per else n

    def now(self, sem):
        return self.at(sem, self.n[sem.name])

    def expect(self, sem, k=1):
        self.n[sem.name] = self.n.get(sem.name, 0) + k
        return self.n[sem.name]

    def next(self, sem, k=1):
        return self.at(sem, self.expect(sem, k))

    def enter(self, turn, per):
        self.turn, self.per, self.start = turn, per, dict(self.n)

    def leave(self, turns):
        for name, n in self.n.items():
            more = n - self.start.get(name, 0)
            if more:
                assert more == self.per.get(name), (name, more)
                self.n[name] = self.start.get(name, 0) + more * turns
        self.turn, self.per = None, {}


def decoder(nc, a, out):
    ctx = ExitStack()
    with ctx:
        def sb(name, shape, dt=F32):
            return ctx.enter_context(nc.sbuf_tensor(name, shape, dt))

        def sem(name):
            return ctx.enter_context(nc.semaphore(name))

        bank = [ctx.enter_context(nc.psum_tensor(f"bank{i}", [P, 512], F32)) for i in range(8)]

        x = sb("x", [P, TILES, D])
        y = sb("y", [P, TILES, D])
        nx = sb("nx", [P, TILES, D])
        stats = sb("stats", [P, TILES, 6])
        mv = sb("mv", [P, TILES, 2])
        var = sb("var", [P, TILES])
        rstd = sb("rstd", [P, TILES])
        neghalf = sb("neghalf", [P, TILES])
        hT = sb("hT", [P, NT])
        with nc.sbuf_tensor("QHL", [P, HEADS, NT], F32R) as QHL, nc.sbuf_tensor("KHL", [P, HEADS, NT], F32R) as KHL:
            pass
        QA, KA = sb("QA", [P, HEADS * NT]), sb("KA", [P, HEADS * NT])
        KHLc = KHL[:, :, 0:B * C]
        QSW = sb("QSW", [P, 4, S], F32R)
        Vs = sb("Vs", [P, TILES, INNER])
        Vc = Vs[:, 0:2 * B, :]
        ones64 = sb("ones64", [P, DH])
        once64 = sb("once64", [P, DH])
        probs = sb("probs", [P, 2, 4, 512])
        acc = sb("acc", [P, 2, 2, 512])
        ring = probs[:, :, :, :].rearrange("p a b c -> p (a b) c")
        AT = sb("AT", [P, PAIRS, NT])
        rot = sb("rot", [P, 2, 2, 512])
        rec = nx[:, TB:TILES, :].rearrange("p t d -> p (t d)")

        mx = sb("mx", [P, TB, H1])
        shift = sb("shift", [P, TB, H1])
        shl = sb("shl", [P, TB, 2 * H1], BF16)
        shiftT = sb("shiftT", [2 * H1, 2, S], BF16)
        sel = sb("sel", [4, 2, P], BF16)
        wq = sb("wq", [P, INNER]); wqr = sb("wqr", [P, INNER])
        wk = sb("wk", [P, INNER]); wkr = sb("wkr", [P, INNER])
        wv = sb("wv", [P, INNER]); wo = sb("wo", [P, PAIRS, D])
        cq = sb("cq", [P, INNER]); cqr = sb("cqr", [P, INNER])
        ck = sb("ck", [P, INNER]); ckr = sb("ckr", [P, INNER])
        cv = sb("cv", [P, INNER]); co = sb("co", [P, PAIRS, D])
        f1 = sb("f1", [P, FF]); f2 = sb("f2", [P, FCH, D])
        lcol = sb("lcol", [P, 3 + FCH])
        lrow = sb("lrow", [P, 3, D])
        ident = sb("ident", [P, P]); identb = sb("identb", [P, P], BF16)
        triu = sb("triu", [P, P])
        cos = sb("cos", [P, S]); sin = sb("sin", [P, S])
        maskrow = sb("maskrow", [P, NT], BF16)
        maskc8 = sb("maskc8", [P, TILES], U8); maskcol = sb("maskcol", [P, TILES])
        maskq = sb("maskq", [P, TB, C], BF16); maskT = sb("maskT", [P, 2, S], BF16)
        ctxT = sb("ctxT", [P, B * C])
        ones = sb("ones", [1, P])
        cols = sb("cols", [P, 8])
        rows = sb("rows", [1, 3, D])
        brow = sb("brow", [P, 3, D])
        lrow8 = sb("lrow8", [1, E])
        wa = sb("wa", [P, 4, D])
        wr = sb("wr", [P, 2, E])
        tri8 = sb("tri8", [P, E, E])

        gates = sb("gates", [P, 2, TILES, E])
        b2e = sb("b2e", [E, D])

        QT = QA[:, 0:4 * NT].rearrange("p (a t) -> p a t", t=NT)
        KT = QA[:, 4 * NT:8 * NT].rearrange("p (a t) -> p a t", t=NT)
        Qb = KA[:, 0:2 * NT].bitcast(BF16).rearrange("p (a t) -> p a t", t=NT)
        Kb = KA[:, 2 * NT:4 * NT].bitcast(BF16).rearrange("p (a t) -> p a t", t=NT)
        cin = probs[0:CH, 0, :, 0:D]
        maskr8 = probs[:, 1, 0, 0:NT // 4].bitcast(U8)
        m1u8 = probs[:, 1, 1, 0:TB * C // 4].bitcast(U8).rearrange("p (t c) -> p t c", t=TB)
        elu = rot
        q0T, k0T, v0T = QT[:, 0, :], QT[:, 1, :], QT[:, 2, :]
        o0T, z0T, g0 = QT[:, 3, :], KT[:, 0, :], KT[:, 1, :]
        kv = mx[:, 0, :]
        ew1, ew2, eb1 = [wq, wqr], [wk, wkr], [wv[:, 0:F0CH], wv[:, F0CH:2 * F0CH]]
        gate0, gate1 = gates[:, 0], gates[:, 1]
        gateT = rot[0:E, 0, :, :].rearrange("p a c -> p (a c)")
        cmp1 = KT[:, 0, 0:512].rearrange("p (t e j) -> p t e j", e=E, j=E)
        cmp2 = KT[:, 1, 0:512].rearrange("p (t e j) -> p t e j", e=E, j=E)

        def small(i):
            return KT[:, 2, 64 * i:64 * i + 64].rearrange("p (t e) -> p t e", e=E)
        cnt, csum, ex, keep, centred, logits = (small(i) for i in range(6))
        row = KT[:, 2, 512:512 + TILES]
        rcx = KA[:, 6656:6672]
        w1a = cq[:, :].rearrange("p (a n) -> p a n", a=4)
        AG, LG, CS, EX = (QT[:, i, :] for i in range(4))
        q1T, k1T = KT[:, 0, :], KT[:, 1, :]
        VsF = Vs[:, :, :].rearrange("p t c -> p (t c)")
        V1 = VsF[:, 0:TILES * 130].rearrange("p (t c) -> p t c", c=130)
        SC = VsF[:, 2048:4096].rearrange("p (t c) -> p t c", t=TB)
        ones_row = KA[:, 0:S]
        w1x = ck[:, :].rearrange("p (a n) -> p a n", a=4)
        Qst = QA[:, :].bitcast(BF16).rearrange("p (h t) -> p h t", h=H1)
        Kst = AT[:, :, :].rearrange("p a c -> p (a c)").bitcast(BF16)[:, 0:H1 * B * C].rearrange("p (h t) -> p h t", h=H1)
        Vx = VsF[:, 0:2048].rearrange("p (i h c) -> p i h c", i=2 * B, h=H1)
        qparts = [Qb[:, i, :] for i in range(3)]
        kparts = [Kb[:, i, 0:B * C] for i in range(3)]
        SPL = KA[:, 4096:4608]
        OX = KA[:, 4608:5120].rearrange("p (t c) -> p t c", t=TB)
        OXT = KA[:, 5120:5632]
        O4 = [KA[:, 5632:6144], KA[:, 6144:6656]]
        hTh, hTl = KHL[:, 0, :], KHL[:, 1, :]
        wh = [KHL[:, 2, k * FF:(k + 1) * FF] for k in range(2)] + [KHL[:, 4, 0:FF]]
        wl = [KHL[:, 3, k * FF:(k + 1) * FF] for k in range(2)] + [KHL[:, 4, FF:2 * FF]]
        gup = [cqr, ckr, f1]
        gdn = [w.rearrange("p (c n) -> p c n", c=2) for w in (cv[0:HP, 0:2 * D], cv[0:HP, 2 * D:4 * D])]
        gdn.append(co[0:HP, 0:2, :])
        GS = probs[0:HP, 0, :, :].rearrange("p (b c) n -> p b c n", b=B)
        GA = probs[0:HP, 1, :, :].rearrange("p (b c) n -> p b c n", b=B)

        class q:
            const = sem("const")
            x_in = sem("x_in")
            w_early = sem("w_early")
            small_in = sem("small_in")
            ctx_in = sem("ctx_in")
            mask_in = sem("mask_in")
            w_self = sem("w_self")
            w_sout = sem("w_sout")
            w_cross = sem("w_cross")
            w_cout = sem("w_cout")
            w_ff1 = sem("w_ff1")
            w_ff2 = sem("w_ff2")
            w_small = sem("w_small")
            w_expert0 = sem("w_expert0")
            w_expert1 = sem("w_expert1")
            w_l1 = sem("w_l1")
            w_glu0 = sem("w_glu0")
            w_glu1 = sem("w_glu1")
            var_ready = sem("var_ready")
            rstd_ready = sem("rstd_ready")
            normed = sem("normed")
            hT_full = sem("hT_full")
            hT_ready = sem("hT_ready")
            y_free = sem("y_free")
            ctx_full = sem("ctx_full")
            ctx_ready = sem("ctx_ready")
            mask_ready = sem("mask_ready")
            maskT_full = sem("maskT_full")
            maskT_ready = sem("maskT_ready")
            lin_full = sem("lin_full")
            lin_min = sem("lin_min")
            lin_exp = sem("lin_exp")
            lin_add = sem("lin_add")
            lin_ready = sem("lin_ready")
            gelu_full = sem("gelu_full")
            gelu_ready = sem("gelu_ready")
            x_ready = sem("x_ready")
            proj_full = sem("proj_full")
            roped = sem("roped")
            rope_ready = sem("rope_ready")
            high_ready = sem("high_ready")
            qk_ready = sem("qk_ready")
            swap0 = sem("swap0")
            swap1 = sem("swap1")
            v_full = sem("v_full")
            v_ready = sem("v_ready")
            max_full = sem("max_full")
            max_done = sem("max_done")
            shift_ready = sem("shift_ready")
            shiftT_full = sem("shiftT_full")
            shiftT_ready = sem("shiftT_ready")
            scores_full = sem("scores_full")
            probs_ready = sem("probs_ready")
            weighed = sem("weighed")
            summed = sem("summed")
            den_full = sem("den_full")
            heads_ready = sem("heads_ready")
            out_full = sem("out_full")
            y_ready = sem("y_ready")
            up_full = sem("up_full")
            up_ready = sem("up_ready")
            router_full = sem("router_full")
            logits_read = sem("logits_read")
            route_min = sem("route_min")
            route_exp = sem("route_exp")
            gate_ready = sem("gate_ready")
            gateT_full = sem("gateT_full")
            gateT_ready = sem("gateT_ready")
            bias_full = sem("bias_full")
            split_high = sem("split_high")
            split_ready = sem("split_ready")
            moe_up_full = sem("moe_up_full")
            moe_up_ready = sem("moe_up_ready")
            moe_down_full = sem("moe_down_full")
            moe_x_ready = sem("moe_x_ready")
            decay_full = sem("decay_full")
            log_ready = sem("log_ready")
            sums_ready = sem("sums_ready")
            decay_ready = sem("decay_ready")
            qkv_full = sem("qkv_full")
            qkv_ready = sem("qkv_ready")
            sc_full = sem("sc_full")
            sc_ready = sem("sc_ready")
            num_full = sem("num_full")
            num_ready = sem("num_ready")
            xkq_full = sem("xkq_full")
            parts_ready = sem("parts_ready")
            parts_out = sem("parts_out")
            parts_in = sem("parts_in")
            xv_full = sem("xv_full")
            xv_ready = sem("xv_ready")
            kst_one = sem("kst_one")
            xm_full = sem("xm_full")
            xm_done = sem("xm_done")
            xsh_ready = sem("xsh_ready")
            xshT_full = sem("xshT_full")
            xshT_ready = sem("xshT_ready")
            xsh_out = sem("xsh_out")
            xsh_in0 = sem("xsh_in0")
            xsh_in1 = sem("xsh_in1")
            xs_full = sem("xs_full")
            xp_ready = sem("xp_ready")
            xpv_full = sem("xpv_full")
            xo_ready = sem("xo_ready")
            xt_full = sem("xt_full")
            xn_ready = sem("xn_ready")
            xo_full = sem("xo_full")
            xoT_ready = sem("xoT_ready")
            xout_full = sem("xout_full")
            glu_gate_full = sem("glu_gate_full")
            glu_up_full = sem("glu_up_full")
            glu_act = sem("glu_act")
            glu_ready = sem("glu_ready")
            glu_down_full = sem("glu_down_full")
            glu_x_ready = sem("glu_x_ready")
            stored = sem("stored")
            dve_step = sem("dve_step")
            dve_passed = sem("dve_passed")
            sp_passed = sem("sp_passed")
            pool_step = sem("pool_step")
            act_step = sem("act_step")
        dram_q = nc.dram_tensor("dram_q", [3, P, NT], BF16)
        dram_k = nc.dram_tensor("dram_k", [3, P, B * C], BF16)
        dram_s = nc.dram_tensor("dram_s", [B, 2 * H1, S], BF16)

        block = ctx.enter_context(nc.Block())

        @block.sync
        def _(sp):
            see = Seen()
            sp.dma_start(x[:, :, :], a["x"].rearrange("b (t p) d -> p (b t) d", p=P)).then_inc(q.x_in, 16)
            sp.dma_start(wa[:, :, :], a["wa"].rearrange("a p n -> p a n")).then_inc(q.w_early, 16)
            sp.dma_start(cols[:, :], a["cols"]).then_inc(q.w_early, 16)
            sp.dma_start(rows[:, :, :], a["rows"].rearrange("(o a) n -> o a n", o=1)).then_inc(q.small_in, 16)
            sp.dma_start(lrow8[:, :], a["br"].rearrange("(o n) -> o n", o=1)).then_inc(q.small_in, 16)
            sp.dma_start(brow[:, :, :], a["brow"].partition_broadcast(P)).then_inc(q.small_in, 16)
            sp.dma_start(wr[:, :, :], a["wr"].rearrange("a p n -> p a n")).then_inc(q.small_in, 16)
            sp.dma_start(tri8[:, :, :], a["tri8"].partition_broadcast(P)).then_inc(q.small_in, 16)
            sp.dma_start(b2e[:, :], a["b2"]).then_inc(q.small_in, 16)
            for t, name in ((cos, "cos"), (sin, "sin")):
                sp.dma_start(t[:, :], a[name]).then_inc(q.small_in, 16)
            sp.dma_start(sel[:, :, :], a["sel"]).then_inc(q.small_in, 16)
            sp.dma_start(cin, a["ctx"].rearrange("b (t p) d -> p (b t) d", p=CH)).then_inc(q.ctx_in, 16)
            sp.dma_start(maskr8, a["mask1"].rearrange("b s -> (b s)").partition_broadcast(P)).then_inc(q.mask_in, 16)
            sp.dma_start(maskc8[:, :], a["mask1c"]).then_inc(q.mask_in, 16)
            sp.dma_start(m1u8, a["mask2"].rearrange("(t p) c -> p t c", p=P)).then_inc(q.mask_in, 16)
            def load_small(l):
                sp.dma_start(lcol[:, :], a["lcol"][l]).then_inc(q.w_small, 16)
                sp.dma_start(lrow[:, :, :], a["lrow"][l].partition_broadcast(P)).then_inc(q.w_small, 16)

            def load_self(l):
                for t, name in ((wk, "sWk"), (wkr, "sWkr"), (wq, "sWq"), (wqr, "sWqr"), (wv, "sWv")):
                    sp.dma_start(t[:, :], a[name][l]).then_inc(q.w_self, 16)

            def load_sout(l):
                sp.dma_start(wo[:, :, :], a["sWo"][l].rearrange("(c p) n -> p c n", p=P)).then_inc(q.w_sout, 16)

            def load_cross(l):
                for t, name in ((ck, "cWk"), (ckr, "cWkr"), (cv, "cWv"), (cq, "cWq"), (cqr, "cWqr")):
                    sp.dma_start(t[:, :], a[name][l]).then_inc(q.w_cross, 16)

            def load_cout(l):
                sp.dma_start(co[:, :, :], a["cWo"][l].rearrange("(c p) n -> p c n", p=P)).then_inc(q.w_cout, 16)

            def load_ff(l):
                sp.dma_start(f1[:, :], a["fW1"][l]).then_inc(q.w_ff1, 16)
                sp.dma_start(f2[:, :, :], a["fW2"][l].rearrange("(c p) n -> p c n", p=P)).then_inc(q.w_ff2, 16)

            def wait_alone(sem, value):
                sp.wait_ge(sem, value)
                sp.sem_inc(q.sp_passed, 1)

            def swaps(unit0, scores0, per):
                for b in range(B):
                    for j in range(PAIRS):
                        u = b * PAIRS + j
                        n = (b * 2 * PAIRS + PAIRS + j if unit0 == 0 else 5 * PAIRS + u) + 1
                        wait_alone(q.qk_ready, see.at(q.qk_ready, n))
                        if u >= 2:
                            wait_alone(q.scores_full, see.at(q.scores_full, scores0 + per * (u - 1)))
                        for to in range(2):
                            lo, hi = slice(DH * to, DH * to + DH), slice(DH - DH * to, P - DH * to)
                            sp.dma_start(QSW[lo, 2 * (u % 2):2 * (u % 2) + 2, :].bitcast(F32),
                                         QHL[hi, 2 * j:2 * j + 2, b * S:(b + 1) * S].bitcast(F32))\
                                .then_inc((q.swap0, q.swap1)[u % 2], 16)

            load_self(0)
            load_small(0)
            load_sout(0)
            load_cross(0)
            load_cout(0)
            load_ff(0)
            with sp.Fori(0, LAYERS - 1) as l:
                see.enter(l, LAYER)
                swaps(0, 0, 2 * TB)
                wait_alone(q.v_ready, see.at(q.v_ready, TILES))
                wait_alone(q.roped, see.at(q.roped, 4 * PAIRS))
                load_self(l + 1)
                wait_alone(q.y_ready, see.at(q.y_ready, B))
                load_sout(l + 1)
                swaps(4 * PAIRS, LAYER_SELF_SCORES, 4)
                wait_alone(q.v_ready, see.at(q.v_ready, TILES + 2 * B))
                wait_alone(q.roped, see.at(q.roped, 7 * PAIRS))
                load_cross(l + 1)
                wait_alone(q.y_ready, see.at(q.y_ready, 2 * B))
                load_cout(l + 1)
                wait_alone(q.up_ready, see.at(q.up_ready, B * FCH))
                wait_alone(q.y_free, see.at(q.y_free, 3 * B))
                load_small(l + 1)
                wait_alone(q.y_ready, see.at(q.y_ready, 3 * B))
                load_ff(l + 1)
                see.leave(LAYERS - 1)
            see.enter(LAYERS - 1, LAYER)
            swaps(0, 0, 2 * TB)
            swaps(4 * PAIRS, LAYER_SELF_SCORES, 4)
            see.leave(1)
            sp.wait_ge(q.y_ready, LAYERS * LAYER["y_ready"])
            sp.dma_start(w1a, a["w1a"].rearrange("a p n -> p a n")).then_inc(q.w_l1, 16)
            sp.dma_start(w1x, a["w1x"].rearrange("a p n -> p a n")).then_inc(q.w_l1, 16)
            sp.dma_start(gup[2][:, 0:2 * HALF], a["sgu"]).then_inc(q.w_l1, 16)
            sp.dma_start(gdn[2], a["sgd"].rearrange("(c p) n -> p c n", p=HP)).then_inc(q.w_l1, 16)

            def load_expert0(k, e):
                w = (q.w_expert0, q.w_expert1)[k]
                sp.dma_start(ew1[k][:, :], a["W1"][e]).then_inc(w, 16)
                sp.dma_start(ew2[k][:, :].rearrange("p (c n) -> p c n", c=F0CH),
                             a["W2"][e].rearrange("(c p) n -> p c n", p=P)).then_inc(w, 16)
                sp.dma_start(eb1[k], a["b1"][e]).then_inc(w, 16)

            def load_expert1(k, e):
                w = (q.w_glu0, q.w_glu1)[k]
                sp.dma_start(gup[k][:, 0:2 * HALF], a["wup"][e]).then_inc(w, 16)
                sp.dma_start(gdn[k], a["wdn"][e].rearrange("(c p) n -> p c n", p=HP)).then_inc(w, 16)

            for k in range(2):
                load_expert0(k, k)
                load_expert1(k, k)
            with sp.Fori(1, E // 2) as i:
                for k in range(2):
                    sp.wait_ge(q.moe_x_ready, i * 4 - 2 + 2 * k)
                    sp.sem_inc(q.sp_passed, 1)
                    load_expert0(k, i * 2 + k)
            sp.wait_ge(q.parts_ready, 1)
            sp.dma_start(dram_k[:, :, :].rearrange("a p t -> p a t"), Kb[:, 0:3, 0:B * C]).then_inc(q.parts_out, 16)
            sp.wait_ge(q.parts_ready, 3)
            sp.dma_start(dram_q[:, :, :].rearrange("a p t -> p a t"), Qb[:, 0:3, :]).then_inc(q.parts_out, 16)
            sp.wait_ge(q.parts_out, 32)
            sp.wait_ge(q.kst_one, 3)
            for i, (kp, qp) in enumerate(((0, 0), (0, 1), (1, 0), (1, 1), (0, 2), (2, 0))):
                r = slice(i * DK, (i + 1) * DK)
                sp.dma_start(Kst[r, :, :], dram_k[kp].rearrange("(h d) t -> d h t", d=DK)).then_inc(q.parts_in, 16)
                sp.dma_start(Qst[r, :, :], dram_q[qp].rearrange("(h d) t -> d h t", d=DK)).then_inc(q.parts_in, 16)
            for b in range(B):
                sp.wait_ge(q.xshT_ready, b + 1)
                sp.dma_start(dram_s[b], shiftT[:, b, :]).then_inc(q.xsh_out, 16)
                sp.wait_ge(q.xsh_out, 16 * (b + 1))
                sp.dma_start(Qst[SPLITS * DK:SPLITS * DK + 2, :, b * S:(b + 1) * S],
                             dram_s[b].rearrange("(a h) t -> a h t", a=2)).then_inc((q.xsh_in0, q.xsh_in1)[b], 16)
            with sp.Fori(1, E // 2) as i:
                for k in range(2):
                    sp.wait_ge(q.glu_x_ready, i * 4 - 2 + 2 * k)
                    sp.sem_inc(q.sp_passed, 1)
                    load_expert1(k, i * 2 + k)
            for b in range(B):
                sp.wait_ge(q.glu_x_ready, 4 * (E // 2) + b + 1)
                sp.dma_start(out.rearrange("b (t p) d -> p (b t) d", p=P)[:, b * TB:(b + 1) * TB, :],
                             x[:, b * TB:(b + 1) * TB, :]).then_inc(q.stored, 16)
            sp.wait_ge(q.stored, 32)

        @block.gpsimd
        def _(pool):
            see = Seen()
            g = nc.gpsimd
            g.memset(ident[:, :], 0.0)
            g.memset(triu[:, :], 1.0)
            g.memset(ones64[:, :], 1.0)
            g.memset(neghalf[:, :], -0.5)
            g.memset(ones[:, :], 1.0).then_inc(q.pool_step, 1)
            pool.wait_ge(q.pool_step, see.next(q.pool_step))
            g.affine_select(out=ident[:, :], in_=ident[:, :], compare_op=ALU.not_equal, fill=1.0, base=0,
                            pattern=[[-1, P]], channel_multiplier=1).then_inc(q.pool_step, 1)
            g.affine_select(out=once64[:, :], in_=ones64[:, :], compare_op=ALU.is_ge, fill=0.0, base=-(P - C2),
                            pattern=[[0, DH]], channel_multiplier=1).then_inc(q.const, 1)
            g.affine_select(out=triu[:, :], in_=triu[:, :], compare_op=ALU.is_ge, fill=0.0, base=0,
                            pattern=[[1, P]], channel_multiplier=-1).then_inc(q.const, 1)
            pool.wait_ge(q.pool_step, see.next(q.pool_step))
            g.tensor_copy(identb[:, :], ident[:, :]).then_inc(q.const, 1)
            def power():
                pool.wait_ge(q.var_ready, see.next(q.var_ready))
                b = (see.n["var_ready"] - 1) % B
                g.tensor_tensor(rstd[:, b * TB:(b + 1) * TB], var[:, b * TB:(b + 1) * TB],
                                neghalf[:, 0:TB], ALU.pow).then_inc(q.rstd_ready, 1)

            def add_bias(k, b):
                pool.wait_ge(q.normed, see.next(q.normed))
                if b == 0:
                    pool.wait_ge(q.w_small, see.now(q.w_small))
                v = y[:, b * TB:(b + 1) * TB, :]
                g.tensor_tensor(v, v, lrow[:, k:k + 1, :].broadcast_to([P, TB, D]), ALU.add).then_inc(q.y_free, 1)

            def rope_sum(w):
                pool.wait_ge(q.roped, see.next(q.roped))
                r = rot[:, (see.n["roped"] - 1) % 2]
                g.tensor_tensor(r[:, 0, 0:w], r[:, 0, 0:w], r[:, 1, 0:w], ALU.add).then_inc(q.rope_ready, 1)

            def sum_tile(u, k):
                to = acc[:, u % 2, :, :]
                pool.wait_ge(q.probs_ready, see.at(q.probs_ready, 2 * (u * TB + k + 1)))
                if k == 1 and u >= 2:
                    pool.wait_ge(q.den_full, see.at(q.den_full, u - 1))
                if k > 1:
                    pool.wait_ge(q.summed, see.now(q.summed))
                g.tensor_tensor(to, ring[:, 0:2, :] if k == 1 else to, ring[:, 2 * k:2 * k + 2, :],
                                ALU.add).then_inc(q.summed, 1)
                see.expect(q.summed)

            def norm_powers():
                for b in range(B):
                    power()

            def low_weights(to, w, high):
                pool.wait_ge(q.split_high, see.next(q.split_high))
                g.tensor_tensor(to, w, high, ALU.subtract).then_inc(q.split_ready, 1)

            def low_inputs():
                low_weights(hTl, hT[:, :], hTh)

            norm_powers()
            see.expect(q.normed, 2)
            norm_powers()
            see.expect(q.normed, 2)
            norm_powers()
            with pool.Fori(0, LAYERS) as l:
                see.enter(l, LAYER)
                see.expect(q.w_small, 32)
                for b in range(B):
                    add_bias(0, b)
                for _ in range(4 * PAIRS):
                    rope_sum(S)
                for u in range(5):
                    for k in range(1, TB):
                        sum_tile(u, k)
                power()
                for k in range(1, TB):
                    sum_tile(5, k)
                add_bias(1, 0)
                for k in range(1, TB):
                    rope_sum(B * C)
                    sum_tile(6, k)
                rope_sum(B * C)
                for _ in range(2):
                    rope_sum(S)
                power()
                rope_sum(S)
                add_bias(1, 1)
                for _ in range(2 * PAIRS - 3):
                    rope_sum(S)
                for b in range(B):
                    power()
                    add_bias(2, b)
                norm_powers()
                see.leave(LAYERS)
            norm_powers()
            low_inputs()
            with pool.Fori(0, E // 2) as i:
                see.enter(i, EXPERTS0)
                for k in range(2):
                    low_weights(wl[k], ew1[k][:, :], wh[k])
                see.leave(E // 2)
            norm_powers()
            norm_powers()
            g.memset(QA[:, :], 0.0).then_inc(q.kst_one, 1)
            pool.wait_ge(q.kst_one, 1)
            g.memset(Kst[DH:P, :, :], 0.0).then_inc(q.kst_one, 1)
            pool.wait_ge(q.kst_one, 2)
            g.memset(Kst[0:DH, :, :], 1.0).then_inc(q.kst_one, 1)
            norm_powers()
            low_inputs()
            with pool.Fori(0, E // 2) as i:
                see.enter(i, EXPERTS1)
                for k in range(2):
                    low_weights(wl[k][:, 0:2 * HALF], gup[k][:, 0:2 * HALF], wh[k][:, 0:2 * HALF])
                see.leave(E // 2)
            low_weights(wl[2][:, 0:2 * HALF], gup[2][:, 0:2 * HALF], wh[2][:, 0:2 * HALF])

        @block.vector
        def _(dve):
            see = Seen()
            v = nc.vector

            def link(ins):
                ins.then_inc(q.dve_step, 1)
                dve.wait_ge(q.dve_step, see.next(q.dve_step))

            def alone():
                if see.turn is not None:
                    dve.sem_inc(q.dve_passed, 1)

            def norm_stats(b, src, rms):
                ts = range(b * TB, (b + 1) * TB)
                w = slice(b * TB, (b + 1) * TB)
                for t in ts:
                    ins = v.bn_stats(stats[:, t, :], src[:, t, :])
                link(ins)
                alone()
                for t in ts:
                    ins = v.bn_aggr(mv[:, t, :], stats[:, t, :])
                link(ins)
                if rms:
                    link(v.tensor_tensor(var[:, w], mv[:, w, 0], mv[:, w, 0], ALU.mult))
                    link(v.tensor_tensor(var[:, w], var[:, w], mv[:, w, 1], ALU.add))
                    v.tensor_scalar(var[:, w], var[:, w], 1.0e-16, None, ALU.max).then_inc(q.var_ready, 1)
                else:
                    v.tensor_scalar(var[:, w], mv[:, w, 1], 1.0e-5, None, ALU.add).then_inc(q.var_ready, 1)

            def norm_scale(b, src, dst, rms, last=q.normed):
                dve.wait_ge(q.rstd_ready, see.next(q.rstd_ready))
                for t in range(b * TB, (b + 1) * TB):
                    if rms:
                        ins = v.tensor_scalar(dst[:, t, :], src[:, t, :], rstd[:, t:t + 1], None, ALU.mult)
                    else:
                        ins = v.tensor_scalar(dst[:, t, :], src[:, t, :], mv[:, t, 0:1], rstd[:, t:t + 1],
                                              ALU.subtract, ALU.mult)
                ins.then_inc(last, 1)

            def norm(src, dst, rms=False, last=q.normed):
                for b in range(B):
                    norm_stats(b, src, rms)
                for b in range(B):
                    norm_scale(b, src, dst, rms, last)

            def masks():
                dve.wait_ge(q.mask_in, see.next(q.mask_in, 48))
                v.tensor_scalar(maskrow[:, :], maskr8, 1.0, -NEG, ALU.subtract, ALU.mult)
                v.tensor_scalar(maskcol[:, :], maskc8[:, :], 1.0, -NEG * SCALE, ALU.subtract, ALU.mult)
                v.tensor_scalar(maskq[:, :, :], m1u8, NEG, None, ALU.mult).then_inc(q.mask_ready, 1)

            def linear_attention():
                for b in range(B):
                    w = slice(b * S, (b + 1) * S)
                    for k in range(2):
                        dve.wait_ge(q.lin_full, see.next(q.lin_full))
                        src, col = bank[3 * b + k], cols[:, k:k + 1]
                        v.tensor_scalar(elu[:, k, 0, :], src[:, :], col, 0.0, ALU.add, ALU.min).then_inc(q.lin_min, 1)
                        v.tensor_scalar(elu[:, k, 1, :], src[:, :], col, 0.0, ALU.add, ALU.max).then_inc(q.dve_step, 1)
                        see.expect(q.dve_step)
                    dve.wait_ge(q.lin_full, see.next(q.lin_full))
                    link(v.tensor_scalar(v0T[:, w], bank[3 * b + 2][:, :], cols[:, 2:3], None, ALU.add))
                    for k in range(2):
                        dve.wait_ge(q.lin_exp, see.next(q.lin_exp))
                        o = (q0T, k0T)[k][:, w]
                        link(v.scalar_tensor_tensor(out=o, in0=elu[:, k, 0, :], scalar=-1.0, in1=elu[:, k, 1, :],
                                                    op0=ALU.add, op1=ALU.add))
                        link(v.tensor_scalar(o, o, 1.0, None, ALU.add))
                    link(v.tensor_tensor_reduce(z0T[:, w], k0T[:, w], v0T[:, w], 1.0, 0.0, ALU.mult, ALU.add, kv[:, 2 * b:2 * b + 1]))
                    link(v.tensor_reduce(kv[:, 2 * b + 1:2 * b + 2], k0T[:, w], AX.X, ALU.add))
                    link(v.tensor_scalar(z0T[:, w], q0T[:, w], kv[:, 2 * b + 1:2 * b + 2], 1.0e-6, ALU.mult, ALU.add))
                    link(v.reciprocal(z0T[:, w], z0T[:, w]))
                    v.scalar_tensor_tensor(out=o0T[:, w], in0=q0T[:, w], scalar=kv[:, 2 * b:2 * b + 1], in1=z0T[:, w],
                                           op0=ALU.mult, op1=ALU.mult).then_inc(q.lin_ready, 1)
                for b in range(B):
                    dve.wait_ge(q.gelu_ready, see.next(q.gelu_ready))
                    w = slice(b * TB, (b + 1) * TB)
                    link(v.tensor_tensor(x[:, w, :], x[:, w, :],
                                         g0[:, b * S:(b + 1) * S].rearrange("p (t d) -> p t d", d=D), ALU.add))

            def rope(w, batches, first=None):
                see.expect(q.proj_full)
                dve.wait_ge(q.proj_full, see.now(q.proj_full))
                n = see.n["proj_full"] - 1
                if first is None:
                    first = 2 + 2 * (n % 2)
                src = [bank[first + k][:, 0:w] for k in range(2)]
                if n >= 2:
                    dve.wait_ge(q.qk_ready, see.at(q.qk_ready, n - 1))
                for k, tab in enumerate((cos, sin)):
                    i, o, tb = src[k], rot[:, n % 2, k, 0:w], tab[:, :]
                    if batches:
                        i = i.rearrange("p (b c) -> p b c", b=B)
                        o = o.rearrange("p (b c) -> p b c", b=B)
                        tb = tab[:, 0:C].unsqueeze(1).broadcast_to([P, B, C])
                    ins = v.tensor_tensor(o, i, tb, ALU.mult)
                ins.then_inc(q.roped, 1)

            def lows(dst, j, cols_):
                dve.wait_ge(q.high_ready, see.next(q.high_ready))
                r = rot[:, (see.n["high_ready"] - 1) % 2, 0, 0:cols_.stop - cols_.start]
                for e in range(2):
                    hi, lo = slice(DH * e, DH * e + DH), slice(DH - DH * e, P - DH * e)
                    ins = v.tensor_tensor(dst[lo, 2 * j + e, cols_], r[hi, :], dst[hi, 2 * j + e, cols_], ALU.subtract)
                ins.then_inc(q.qk_ready, 1)

            def maximum_self(u, i):
                b, h, t = u // PAIRS, u % PAIRS * 2 + i // TB, i % TB
                dve.wait_ge(q.max_full, see.next(q.max_full))
                alone()
                n = see.n["max_full"] - 1
                v.tensor_tensor_reduce(bank[n % 2][:, :], bank[n % 2][:, :], maskrow[:, b * S:(b + 1) * S], 1.0, -3.0e38,
                                       ALU.add, ALU.max, mx[:, t, h:h + 1]).then_inc(q.max_done, 1)
                see.expect(q.max_done)

            def maximum_cross(u, i):
                h, t = u % PAIRS * 2 + i // 2, i % 2 * 2
                dve.wait_ge(q.max_full, see.next(q.max_full))
                n = see.n["max_full"] - 1
                v.tensor_reduce(mx[:, t:t + 2, h:h + 1], bank[n % 2][:, 0:2 * C].rearrange("p (a c) -> p a c", a=2),
                                AX.X, ALU.max).then_inc(q.max_done, 1)
                see.expect(q.max_done)

            def shifts(first, heads, done, ready, clamp=None):
                dve.wait_ge(done, see.now(done))
                to, m = shift[:, :, 0:heads], mx[:, :, first:first + heads]
                if clamp is None:
                    link(v.tensor_scalar(to, m, -1.0, None, ALU.mult))
                else:
                    link(v.tensor_scalar(to, m, -1.0, clamp, ALU.mult, ALU.min))
                link(v.tensor_copy(shl[:, :, 0:heads], to))
                v.tensor_tensor(shl[:, :, heads:2 * heads], to, shl[:, :, 0:heads], ALU.subtract).then_inc(ready, 1)

            def shifts_turned(n, b, full, ready, src):
                dve.wait_ge(full, see.next(full))
                v.tensor_copy(shiftT[0:n, b, :], src[0:n, 0:S // 2].bitcast(BF16)).then_inc(ready, 1)

            def normalise(u, tiles):
                b, j = u // PAIRS, u % PAIRS
                see.expect(q.weighed, tiles)
                if direct(b, j, tiles):
                    dve.wait_ge(q.weighed, see.now(q.weighed))
                else:
                    dve.wait_ge(q.den_full, see.next(q.den_full))
                i = 4 + 2 * (j % 2)
                n = see.expect(q.heads_ready) - 1
                if n:
                    dve.wait_ge(q.heads_ready, see.at(q.heads_ready, n))
                link(v.reciprocal(rec, bank[i + 1][:, :]))
                v.tensor_tensor(AT[:, j, b * S:(b + 1) * S], bank[i][:, :], rec, ALU.mult).then_inc(q.heads_ready, 1)

            def residual(b):
                dve.wait_ge(q.out_full, see.next(q.out_full))
                dve.wait_ge(q.y_free, see.next(q.y_free))
                w = y[:, b * TB:(b + 1) * TB, :]
                v.tensor_tensor(w, bank[6 + b][:, :].rearrange("p (t d) -> p t d", d=D), w, ALU.add).then_inc(q.y_ready, 1)
                see.expect(q.y_ready)

            def pair_shifts(u):
                shifts(u % PAIRS * 2, 2, q.max_done, q.shift_ready)

            def pair_shifts_turned(u):
                shifts_turned(4, u % 2, q.shiftT_full, q.shiftT_ready, bank[0])

            def begin_cross(u, k):
                def keys(j):
                    rope(B * C, True, 0)

                def keys_low(j):
                    lows(KHLc, j, slice(0, B * C))

                if (u, k) == (4, TB - 1):
                    dve.wait_ge(q.y_ready, see.now(q.y_ready))
                    norm_stats(0, y, True)
                elif (u, k) == (5, 2):
                    norm_scale(0, y, nx, True)
                elif (u, k) == (6, 0):
                    keys(0)
                elif (u, k) == (6, 1):
                    keys(1)
                elif (u, k) == (6, 2):
                    keys_low(0)
                    keys(2)
                elif (u, k) == (6, 3):
                    keys_low(1)
                elif (u, k) == (7, 0):
                    keys(3)
                    keys_low(2)
                elif (u, k) == (7, 2):
                    keys_low(3)

            def begin_ff(u, k):
                if (u, k) == (5, 0):
                    dve.wait_ge(q.y_ready, see.now(q.y_ready))
                    norm_stats(0, y, True)
                elif (u, k) == (6, 0):
                    norm_scale(0, y, nx, True)

            def attend(maximum, tiles):
                for u in range(UNITS):
                    for k in range(tiles):
                        if k == TURN[tiles] and u + 1 < UNITS:
                            pair_shifts_turned(u + 1)
                        if u == PAIRS and k == CONTRACT[tiles]:
                            residual(0)
                        if u + 2 < UNITS:
                            for i in quota(tiles, k):
                                maximum(u + 2, i)
                            if k == tiles - 1:
                                pair_shifts(u + 2)
                        if tiles == 2 and k == 0 and u:
                            normalise(u - 1, tiles)
                        if u >= PAIRS:
                            (begin_cross if tiles == TB else begin_ff)(u, k)
                        if tiles == TB and k == 1 and u:
                            normalise(u - 1, tiles)
                normalise(UNITS - 1, tiles)

            def layer():
                units = [(t, j, slice(b * S, (b + 1) * S)) for b in range(B) for t in (KHL, QHL) for j in range(PAIRS)]
                for n in range(2 * PAIRS):
                    rope(S, False)
                    if n:
                        lows(*units[n - 1])
                for h in range(HEADS):
                    if h == 6:
                        pair_shifts_turned(0)
                    for i in (2 * h, 2 * h + 1):
                        maximum_self(h // PAIRS, i % HEADS)
                    if h % PAIRS == PAIRS - 1:
                        pair_shifts(h // PAIRS)
                    rope(S, False)
                    lows(*units[2 * PAIRS + h - 1])
                lows(*units[-1])
                attend(maximum_self, TB)
                units = [(QHL, j, slice(b * S, (b + 1) * S)) for b in range(B) for j in range(PAIRS)]
                rope(S, False)
                rope(S, False)
                lows(*units[0])
                residual(1)
                dve.wait_ge(q.y_ready, see.now(q.y_ready))
                norm_stats(1, y, True)
                rope(S, False)
                lows(*units[1])
                norm_scale(1, y, nx, True)
                for n in range(PAIRS - 1, 2 * PAIRS):
                    if n == 2 * PAIRS - 1:
                        pair_shifts_turned(0)
                    if n >= PAIRS:
                        for i in range(2):
                            maximum_cross(n // 2 - 2, n % 2 * 2 + i)
                        if n % 2:
                            pair_shifts(n // 2 - 2)
                    rope(S, False)
                    lows(*units[n - 1])
                lows(*units[-1])
                attend(maximum_cross, 2)
                residual(1)
                dve.wait_ge(q.y_ready, see.now(q.y_ready))
                norm_stats(1, y, True)
                norm_scale(1, y, nx, True)
                for b in range(B):
                    residual(b)
                    dve.wait_ge(q.y_ready, see.now(q.y_ready))
                    norm_stats(b, y, True)
                    norm_scale(b, y, nx, True)

            def rank(lg):
                a4 = lg.unsqueeze(2).broadcast_to([P, TILES, E, E])
                b4 = lg.unsqueeze(3).broadcast_to([P, TILES, E, E])
                t4 = tri8[:, :, :].unsqueeze(1).broadcast_to([P, TILES, E, E])
                link(v.tensor_tensor(cmp1, a4, b4, ALU.is_gt))
                link(v.tensor_tensor(cmp2, a4, b4, ALU.is_equal))
                link(v.tensor_tensor(cmp2, cmp2, t4, ALU.mult))
                link(v.tensor_tensor(cmp1, cmp1, cmp2, ALU.add))
                link(v.tensor_reduce(cnt, cmp1, AX.X, ALU.add))
                link(v.tensor_tensor(cmp1, cmp1, a4, ALU.mult))
                link(v.tensor_reduce(csum, cmp1, AX.X, ALU.add))

            def softmax_of(src):
                link(v.tensor_reduce(row, src, AX.X, ALU.max))
                v.tensor_tensor(centred, src, row.unsqueeze(2).broadcast_to([P, TILES, E]),
                                ALU.subtract).then_inc(q.route_min, 1)
                dve.wait_ge(q.route_exp, see.next(q.route_exp))

            def share(t, src):
                link(v.tensor_reduce(row, src, AX.X, ALU.add))
                link(v.reciprocal(row, row))
                return v.tensor_tensor(t, src, row.unsqueeze(2).broadcast_to([P, TILES, E]), ALU.mult)

            def route0():
                dve.wait_ge(q.router_full, see.next(q.router_full))
                v.tensor_copy(logits, bank[0][:, 0:TILES * E].rearrange("p (t e) -> p t e", e=E)).then_inc(q.logits_read, 1)
                dve.wait_ge(q.logits_read, see.next(q.logits_read))
                softmax_of(logits)
                link(share(ex, ex))
                rank(ex)
                link(v.tensor_scalar(csum, csum, 0.8, None, ALU.is_lt))
                link(v.tensor_scalar(cnt, cnt, 1.5, None, ALU.is_lt))
                link(v.tensor_tensor(keep, csum, cnt, ALU.max))
                v.tensor_tensor(gate0, ex, keep, ALU.mult).then_inc(q.gate_ready, 1)
                for b in range(B):
                    dve.wait_ge(q.gateT_full, see.next(q.gateT_full))
                    v.tensor_copy(gateT[:, b * S:(b + 1) * S], bank[1 + b][0:E, :]).then_inc(q.gateT_ready, 1)

            def route1():
                dve.wait_ge(q.router_full, see.next(q.router_full))
                v.tensor_copy(logits, bank[0][:, 0:TILES * E].rearrange("p (t e) -> p t e", e=E)).then_inc(q.logits_read, 1)
                dve.wait_ge(q.logits_read, see.next(q.logits_read))
                rank(logits)
                softmax_of(logits)
                link(v.tensor_scalar(cnt, cnt, 2.5, None, ALU.is_lt))
                link(v.tensor_tensor(ex, ex, cnt, ALU.mult))
                link(share(gate1, ex))

            def gated(full, ready, gate, e):
                for b in range(B):
                    dve.wait_ge(full, see.next(full))
                    for t in range(TB):
                        w = x[:, b * TB + t, :]
                        sc = 1.0 if gate is None else gate[:, b * TB + t, bass.ds(e, 1)]
                        ins = v.scalar_tensor_tensor(out=w, in0=bank[6 + b][:, t * D:(t + 1) * D], scalar=sc, in1=w,
                                                     op0=ALU.mult, op1=ALU.add)
                    ins.then_inc(ready, 1)
                    see.expect(ready)
                    dve.wait_ge(ready, see.now(ready))

            def decayed():
                link(v.memset(V1[:, :, D:D + 1], 1.0))
                link(v.memset(ones_row, 1.0))
                for b in range(B):
                    w = slice(b * S, (b + 1) * S)
                    dve.wait_ge(q.log_ready, see.next(q.log_ready))
                    v.tensor_tensor_scan(CS[:, w][:, ::-1], ones_row, LG[:, w][:, ::-1], 0.0, ALU.mult,
                                         ALU.add).then_inc(q.sums_ready, 1)
                    dve.wait_ge(q.qkv_full, see.next(q.qkv_full))
                    v.tensor_scalar(q1T[:, w], bank[0][:, :], cols[:, 3:4], 0.0, ALU.add, ALU.max).then_inc(q.qkv_ready, 1)
                    dve.wait_ge(q.qkv_full, see.next(q.qkv_full))
                    link(v.tensor_scalar(k1T[:, w], bank[1][:, :], cols[:, 4:5], 0.0, ALU.add, ALU.max))
                    dve.wait_ge(q.decay_ready, see.next(q.decay_ready))
                    v.tensor_tensor(k1T[:, w], k1T[:, w], EX[:, w], ALU.mult).then_inc(q.qkv_ready, 1)
                    dve.wait_ge(q.qkv_full, see.next(q.qkv_full))
                    v.tensor_tensor(V1[:, b * TB:(b + 1) * TB, 0:D], bank[2][:, :].rearrange("p (t d) -> p t d", d=D),
                                    brow[:, 1:2, :].broadcast_to([P, TB, D]), ALU.add).then_inc(q.qkv_ready, 1)
                    for i in range(TB):
                        dve.wait_ge(q.sc_full, see.next(q.sc_full))
                        src = bank[4 + i % 2]
                        if i < TB - 1:
                            v.tensor_copy(SC[:, i, (i + 1) * P:], src[:, (i + 1) * P:])
                        v.tensor_tensor(SC[:, i, i * P:(i + 1) * P], src[:, i * P:(i + 1) * P], triu[:, :],
                                        ALU.mult).then_inc(q.sc_ready, 1)
                    for t in range(TB):
                        dve.wait_ge(q.num_full, see.next(q.num_full))
                        src = bank[6 + t % 2]
                        link(v.tensor_scalar(row[:, 0:1], src[:, D:D + 1], 1.0e-6, None, ALU.add))
                        link(v.reciprocal(row[:, 0:1], row[:, 0:1]))
                        tt = x[:, b * TB + t, :]
                        v.scalar_tensor_tensor(out=tt, in0=src[:, 0:D], scalar=row[:, 0:1], in1=tt, op0=ALU.mult,
                                               op1=ALU.add).then_inc(q.num_ready, 1)
                        dve.wait_ge(q.num_ready, see.next(q.num_ready))

            def split(dst, src, bias, scale, n):
                f = SPL[:, 0:n]
                link(v.tensor_scalar(f, src, bias, scale, ALU.add, ALU.mult))
                link(v.tensor_copy(dst[0], f))
                link(v.tensor_tensor(f, f, dst[0], ALU.subtract))
                link(v.tensor_copy(dst[1], f))
                return v.tensor_tensor(dst[2], f, dst[1], ALU.subtract)

            def last_attention():
                link(v.memset(Vx, 0.0))
                link(v.memset(Vx[:, :, :, DK:DK + 1], 1.0))
                dve.wait_ge(q.xkq_full, see.next(q.xkq_full))
                split(kparts, bank[0][:, 0:B * C], cols[:, 7:8], 1.0, B * C).then_inc(q.parts_ready, 1)
                dve.wait_ge(q.parts_ready, see.next(q.parts_ready))
                for b in range(B):
                    dve.wait_ge(q.xkq_full, see.next(q.xkq_full))
                    split([p[:, b * S:(b + 1) * S] for p in qparts], bank[1 + b][:, :], cols[:, 6:7],
                          float(DK) ** -0.5, S).then_inc(q.parts_ready, 1)
                    dve.wait_ge(q.parts_ready, see.next(q.parts_ready))
                for i in range(2 * B):
                    dve.wait_ge(q.xv_full, see.next(q.xv_full))
                    link(v.tensor_tensor(Vx[:, i, :, 0:DK], bank[3 + i][:, 0:D].rearrange("p (h d) -> p h d", d=DK),
                                         brow[:, 2, :].rearrange("p (h d) -> p h d", d=DK), ALU.add))
                    v.tensor_scalar(Vx[:, i, :, :], Vx[:, i, :, :], once64[:, 0:1] if i % 2 else 1.0, None,
                                    ALU.mult).then_inc(q.xv_ready, 1)

                def maximum(i):
                    t, h = i // (H1 // 2), i % (H1 // 2) * 2
                    dve.wait_ge(q.xm_full, see.next(q.xm_full))
                    n = see.n["xm_full"] - 1
                    v.tensor_reduce(mx[:, t, h:h + 2], bank[n % 2][:, 0:2 * C].rearrange("p (a c) -> p a c", a=2),
                                    AX.X, ALU.max).then_inc(q.xm_done, 1)
                    see.expect(q.xm_done)

                def divide(g):
                    dve.wait_ge(q.xt_full, see.next(q.xt_full))
                    src = bank[6][:, :].rearrange("p (t j c) -> p t j c", t=TB, j=4)
                    r = rcx.rearrange("p (t j) -> p t j", j=4)
                    link(v.tensor_scalar(r, src[:, :, :, DK], 1.0e-30, None, ALU.max))
                    link(v.reciprocal(r, r))
                    v.tensor_tensor(OX[:, :, 32 * g:32 * g + 32].rearrange("p t (j d) -> p t j d", d=DK),
                                    src[:, :, :, 0:DK], r.unsqueeze(3).broadcast_to([P, TB, 4, DK]),
                                    ALU.mult).then_inc(q.xn_ready, 1)
                    dve.wait_ge(q.xn_ready, see.next(q.xn_ready))

                def xresidual(b):
                    dve.wait_ge(q.xout_full, see.next(q.xout_full))
                    w = x[:, b * TB:(b + 1) * TB, :]
                    v.tensor_tensor(w, bank[7][:, :].rearrange("p (t d) -> p t d", d=D), w, ALU.add).then_inc(q.x_ready, 1)
                    see.expect(q.x_ready)

                for i in range(TB * H1 // 2):
                    maximum(i)
                shifts(0, H1, q.xm_done, q.xsh_ready, GUARD)
                shifts_turned(2 * H1, 0, q.xshT_full, q.xshT_ready, bank[0])
                for b in range(B):
                    for u in range(H1 // 2):
                        if b and u == 0:
                            divide(H1 // 4 - 1)
                        if b and u == 2:
                            xresidual(0)
                        if u >= 3 and u % 2:
                            divide((u - 3) // 2)
                        if b == 0 and u < len(XQUOTA):
                            for i in range(sum(XQUOTA[:u]), sum(XQUOTA[:u + 1])):
                                maximum(i)
                            if u == len(XQUOTA) - 1:
                                shifts(0, H1, q.xm_done, q.xsh_ready, GUARD)
                        if b == 0 and u == XTURN:
                            shifts_turned(2 * H1, 1, q.xshT_full, q.xshT_ready, bank[0])
                divide(H1 // 4 - 1)
                xresidual(1)
                dve.wait_ge(q.x_ready, see.now(q.x_ready))

            def glu_products():
                for b in range(B):
                    for c in range(2):
                        dve.wait_ge(q.glu_act, see.next(q.glu_act))
                        dve.wait_ge(q.glu_up_full, see.next(q.glu_up_full))
                        v.tensor_tensor(GA[:, b, c, :], GS[:, b, c, :], bank[2 * c + 1][0:HP, :],
                                        ALU.mult).then_inc(q.glu_ready, 1)

            see.expect(q.const, CONSTS)
            dve.wait_ge(q.x_in, see.next(q.x_in, 16))
            dve.wait_ge(q.const, see.now(q.const))
            norm(x, nx)
            masks()
            dve.wait_ge(q.ctx_full, see.next(q.ctx_full))
            v.tensor_copy(ctxT[:, :], bank[2][:, 0:B * C]).then_inc(q.ctx_ready, 1)
            dve.wait_ge(q.maskT_full, see.next(q.maskT_full))
            v.tensor_copy(maskT[:, :, :], bank[3][:, :].bitcast(BF16).rearrange("p (a c) -> p a c", a=2)).then_inc(q.maskT_ready, 1)
            dve.wait_ge(q.small_in, see.next(q.small_in, 144))
            dve.wait_ge(q.w_early, see.next(q.w_early, 32))
            linear_attention()
            norm(x, y, last=q.normed)
            see.expect(q.normed, 4)
            dve.wait_ge(q.normed, see.now(q.normed))
            norm(y, nx, True)
            with dve.Fori(0, LAYERS) as l:
                see.enter(l, LAYER)
                layer()
                see.leave(LAYERS)
            see.expect(q.normed, LAYERS * LAYER["normed"] + 2)
            dve.wait_ge(q.normed, see.now(q.normed))
            for b in range(B):
                w = slice(b * TB, (b + 1) * TB)
                link(v.tensor_tensor(nx[:, w, :], nx[:, w, :], brow[:, 0:1, :].broadcast_to([P, TB, D]), ALU.mult))
                link(v.tensor_tensor(x[:, w, :], x[:, w, :], nx[:, w, :], ALU.add))
            norm(x, nx)
            route0()
            for b in range(B):
                dve.wait_ge(q.bias_full, see.next(q.bias_full))
                w = slice(b * TB, (b + 1) * TB)
                v.tensor_tensor(x[:, w, :], bank[6 + b][:, :].rearrange("p (t d) -> p t d", d=D), x[:, w, :],
                                ALU.add).then_inc(q.x_ready, 1)
                dve.wait_ge(q.x_ready, see.next(q.x_ready))
            with dve.Fori(0, E // 2) as i:
                see.enter(i, EXPERTS0)
                for k in range(2):
                    gated(q.moe_down_full, q.moe_x_ready, gate0, i * 2 + k)
                see.leave(E // 2)
            norm(x, nx)
            decayed()
            norm(x, nx)
            last_attention()
            norm(x, nx)
            route1()
            with dve.Fori(0, E // 2) as i:
                see.enter(i, EXPERTS1)
                for k in range(2):
                    glu_products()
                    gated(q.glu_down_full, q.glu_x_ready, gate1, i * 2 + k)
                see.leave(E // 2)
            glu_products()
            gated(q.glu_down_full, q.glu_x_ready, None, 0)

        @block.scalar
        def _(act):
            see = Seen()
            c = nc.scalar

            def input_of(b, i, gamma):
                act.wait_ge(q.hT_full, see.next(q.hT_full))
                c.activation(hT[:, b * S:(b + 1) * S], bank[i][:, :], ACT.Copy, scale=gamma).then_inc(q.hT_ready, 1)
                see.expect(q.hT_ready)

            def inputs(gamma=1.0):
                for b in range(B):
                    input_of(b, 6 + b, gamma)

            def high(dst, j, cols_):
                act.wait_ge(q.rope_ready, see.next(q.rope_ready))
                r = rot[:, (see.n["rope_ready"] - 1) % 2, 0, 0:cols_.stop - cols_.start]
                for e in range(2):
                    hi = slice(DH * e, DH * e + DH)
                    ins = c.activation(dst[hi, 2 * j + e, cols_], r[hi, :], ACT.Copy)
                ins.then_inc(q.high_ready, 1)

            def values(dst, i, weight=1.0):
                act.wait_ge(q.v_full, see.next(q.v_full))
                c.activation(dst, bank[i][:, :], ACT.Copy, scale=weight).then_inc(q.v_ready, 1)

            def split_inputs():
                act.wait_ge(q.hT_ready, see.now(q.hT_ready))
                c.activation(hTh, hT[:, :], ACT.Copy).then_inc(q.split_high, 1)

            def split_weights(to, w):
                c.activation(to, w, ACT.Copy).then_inc(q.split_high, 1)

            def begin_cross(u, k):
                s = u * TB + k - (6 * TB + 2)
                if 0 <= s < PAIRS:
                    high(KHLc, s, slice(0, B * C))
                elif s == PAIRS:
                    cross_values(0)
                elif s == PAIRS + 1:
                    cross_values(1)

            def cross_values(t):
                values(Vc[:, t, :], t % 2, once64[:, 0:1] if t % 2 else 1.0)

            def exps(tiles, masked):
                for u in range(B * PAIRS * tiles):
                    if u >= 4:
                        act.wait_ge(q.weighed, see.at(q.weighed, see.n.get("weighed", 0) - 3))
                        if tiles == TB:
                            pair, k = divmod(u - 4, TB)
                            act.wait_ge(q.summed, see.at(q.summed, (TB - 1) * pair + max(k, 1)))
                    for e in range(2):
                        act.wait_ge(q.scores_full, see.next(q.scores_full))
                        t = u // (PAIRS * tiles) * TB + u % tiles
                        bias = maskcol[:, t:t + 1] if masked else 0.0
                        c.activation(ring[:, 2 * (u % 4) + e, :], bank[2 + e][:, :], ACT.Exp,
                                     bias=bias, scale=SCALE).then_inc(q.probs_ready, 1)
                    see.expect(q.weighed)
                    if tiles == TB:
                        begin_cross(u // TB, u % TB)

            see.expect(q.const, CONSTS)
            inputs()
            for b in range(B):
                for k in range(2):
                    act.wait_ge(q.lin_min, see.next(q.lin_min))
                    c.activation(elu[:, k, 0, :], elu[:, k, 0, :], ACT.Exp).then_inc(q.lin_exp, 1)
            for b in range(B):
                act.wait_ge(q.gelu_full, see.next(q.gelu_full))
                c.activation(g0[:, b * S:(b + 1) * S], bank[6 + b][:, :], ACT.Gelu_apprx_tanh).then_inc(q.gelu_ready, 1)
            act.wait_ge(q.mask_ready, see.next(q.mask_ready))
            act.wait_ge(q.const, see.now(q.const))
            with act.Fori(0, LAYERS) as l:
                see.enter(l, LAYER)
                act.wait_ge(q.w_small, see.next(q.w_small, 32))
                inputs(lcol[:, 0:1])
                for b in range(B):
                    for n in range(2 * PAIRS):
                        high(QHL if n // PAIRS else KHL, n % PAIRS, slice(b * S, (b + 1) * S))
                        if b:
                            values(Vs[:, n, :], 6 + n % 2)
                exps(TB, True)
                for t in (2, 3):
                    cross_values(t)
                input_of(0, 0, lcol[:, 1:2])
                for j in range(PAIRS - 1):
                    high(QHL, j, slice(0, S))
                input_of(1, 1, lcol[:, 1:2])
                high(QHL, PAIRS - 1, slice(0, S))
                for j in range(PAIRS):
                    high(QHL, j, slice(S, 2 * S))
                exps(2, False)
                for b in range(B):
                    input_of(b, b, lcol[:, 2:3])
                    for k in range(FCH):
                        act.wait_ge(q.up_full, see.next(q.up_full))
                        c.activation(probs[:, b, k, :], bank[2 + k][:, :], ACT.Gelu,
                                     bias=lcol[:, 3 + k:4 + k]).then_inc(q.up_ready, 1)
                see.leave(LAYERS)

            inputs()
            split_inputs()
            act.wait_ge(q.route_min, see.next(q.route_min))
            c.activation(ex, centred, ACT.Exp).then_inc(q.route_exp, 1)
            with act.Fori(0, E // 2) as i:
                see.enter(i, EXPERTS0)
                for k in range(2):
                    w = (q.w_expert0, q.w_expert1)[k]
                    act.wait_ge(w, see.next(w, 48))
                    split_weights(wh[k], ew1[k][:, :])
                    for b in range(B):
                        for j in range(F0CH):
                            act.wait_ge(q.moe_up_full, see.next(q.moe_up_full))
                            c.activation(probs[:, b, j, :], bank[2 + j][:, :], ACT.Relu,
                                         bias=eb1[k][:, j:j + 1]).then_inc(q.moe_up_ready, 1)
                see.leave(E // 2)

            inputs()
            for b in range(B):
                w = slice(b * S, (b + 1) * S)
                act.wait_ge(q.decay_full, see.next(q.decay_full))
                c.activation(AG[:, w], bank[3][:, :], ACT.Sigmoid, bias=cols[:, 5:6]).then_inc(q.act_step, 1)
                act.wait_ge(q.act_step, see.next(q.act_step))
                c.activation(AG[:, w], AG[:, w], ACT.Copy, bias=1.0e-6).then_inc(q.act_step, 1)
                act.wait_ge(q.act_step, see.next(q.act_step))
                c.activation(LG[:, w], AG[:, w], ACT.Ln).then_inc(q.log_ready, 1)
                act.wait_ge(q.sums_ready, see.next(q.sums_ready))
                c.activation(EX[:, w], CS[:, w], ACT.Exp).then_inc(q.decay_ready, 1)

            inputs()
            def turned_copy():
                act.wait_ge(q.xo_full, see.next(q.xo_full))
                c.activation(OXT, bank[6][:, :], ACT.Copy).then_inc(q.xoT_ready, 1)

            for b in range(B):
                for u in range(H1 // 2 + 1):
                    if u < H1 // 2:
                        if b or u >= 2:
                            act.wait_ge(q.xpv_full, b * H1 // 2 + u - 1)
                        for n in range(4):
                            act.wait_ge(q.xs_full, see.next(q.xs_full))
                            c.activation(ring[:, u % 2 * 4 + n, :], bank[2 + n % 2][:, :], ACT.Exp).then_inc(q.xp_ready, 1)
                    if u and u % 2 == 0:
                        act.wait_ge(q.xpv_full, b * H1 // 2 + u)
                        g = u // 2 - 1
                        if b or g >= 2:
                            act.wait_ge(q.xt_full, b * H1 // 4 + g - 1)
                        c.activation(O4[g % 2], bank[4 + g % 2][:, :], ACT.Copy).then_inc(q.xo_ready, 1)
                    if b and u == 1:
                        turned_copy()
            turned_copy()

            inputs()
            split_inputs()
            act.wait_ge(q.route_min, see.next(q.route_min))
            c.activation(ex, centred, ACT.Exp).then_inc(q.route_exp, 1)

            def gates_of_glu():
                for b in range(B):
                    for k in range(2):
                        act.wait_ge(q.glu_gate_full, see.next(q.glu_gate_full))
                        c.activation(GS[:, b, k, :], bank[2 * k][0:HP, :], ACT.Silu).then_inc(q.glu_act, 1)

            with act.Fori(0, E // 2) as i:
                see.enter(i, EXPERTS1)
                for k in range(2):
                    w = (q.w_glu0, q.w_glu1)[k]
                    act.wait_ge(w, see.next(w, 32))
                    split_weights(wh[k][:, 0:2 * HALF], gup[k][:, 0:2 * HALF])
                    gates_of_glu()
                see.leave(E // 2)
            act.wait_ge(q.w_l1, 64)
            split_weights(wh[2][:, 0:2 * HALF], gup[2][:, 0:2 * HALF])
            gates_of_glu()

        @block.tensor
        def _(pe):
            see = Seen()
            mm, turn = nc.tensor.matmul, nc.tensor.transpose
            reader, read_at = [q.const] * 8, [CONSTS] * 8

            def lend(banks, sem):
                n = see.expect(sem)
                for i in banks:
                    reader[i], read_at[i] = sem, n

            def drain():
                for i in range(8):
                    pe.wait_ge(reader[i], see.at(reader[i], read_at[i]))
                    reader[i], read_at[i] = q.const, CONSTS

            def input_of(b, i):
                pe.wait_ge(q.normed, see.next(q.normed))
                pe.wait_ge(reader[i], see.at(reader[i], read_at[i]))
                for t in range(TB):
                    ins = turn(bank[i][:, t * P:(t + 1) * P], nx[:, b * TB + t, :], ident[:, :])
                ins.then_inc(q.hT_full, 1)
                lend([i], q.hT_ready)

            def inputs():
                for b in range(B):
                    input_of(b, 6 + b)

            def hT_of(b):
                return hT[:, b * S:(b + 1) * S]

            def hT_tile(t):
                return hT[:, t * P:(t + 1) * P]

            def hT_wait(b):
                pe.wait_ge(q.hT_ready, see.at(q.hT_ready, see.n["hT_ready"] - (B - 1 - b)))

            def pair(w, wrot, j, rhs, n, i=None):
                if i is None:
                    i = 2 + 2 * (see.n.get("roped", 0) % 2)
                for k in (i, i + 1):
                    pe.wait_ge(reader[k], see.at(reader[k], read_at[k]))
                mm(bank[i][:, 0:n], w[:, j * P:(j + 1) * P], rhs, start=True, stop=True)
                mm(bank[i + 1][:, 0:n], wrot[:, j * P:(j + 1) * P], rhs, start=True, stop=True).then_inc(q.proj_full, 1)
                lend([i, i + 1], q.roped)

            def value_tile(src, w, i):
                pe.wait_ge(reader[i], see.at(reader[i], read_at[i]))
                mm(bank[i][:, :], src, w[:, :], start=True, stop=True).then_inc(q.v_full, 1)
                lend([i], q.v_ready)

            def max_self(u, n):
                b, h, t = u // PAIRS, u % PAIRS * 2 + n // TB, n % TB
                i = see.n.get("max_done", 0) % 2
                pe.wait_ge(reader[i], see.at(reader[i], read_at[i]))
                mm(bank[i][:, :], QHL[:, h, b * S + t * P:b * S + (t + 1) * P], KHL[:, h, b * S:(b + 1) * S],
                   start=True, stop=True).then_inc(q.max_full, 1)
                lend([i], q.max_done)

            def max_cross(u, n):
                b, h, t = u // PAIRS, u % PAIRS * 2 + n // 2, n % 2 * 2
                i = see.n.get("max_done", 0) % 2
                pe.wait_ge(reader[i], see.at(reader[i], read_at[i]))
                for k in range(2):
                    ins = mm(bank[i][:, k * C:(k + 1) * C], QHL[:, h, b * S + (t + k) * P:b * S + (t + k + 1) * P],
                             KHLc[:, h, b * C:(b + 1) * C], start=True, stop=True)
                ins.then_inc(q.max_full, 1)
                lend([i], q.max_done)

            def shifts_turn(i, heads, ready, full, done):
                pe.wait_ge(ready, see.next(ready))
                pe.wait_ge(reader[i], see.at(reader[i], read_at[i]))
                for t in range(TB):
                    ins = turn(bank[i][0:2 * heads, t * P // 2:(t + 1) * P // 2].bitcast(BF16), shl[:, t, 0:2 * heads],
                               identb[:, :])
                ins.then_inc(full, 1)
                lend([i], done)

            def scores(b, h, k, kt, per_batch, step):
                i = 2 + h % 2
                keys = kt[:, h, b * per_batch + k * step:b * per_batch + k * step + P]
                pe.wait_ge(reader[i], see.at(reader[i], read_at[i]))
                mm(bank[i][:, :], sel[:, h % 2, :], shiftT[0:4, h // 2 % 2, :], start=True, stop=False)
                mm(bank[i][:, :], keys, QHL[:, h, b * S:(b + 1) * S], start=False, stop=False)
                mm(bank[i][:, :], keys, QSW[:, h % 4, :], start=False, stop=True).then_inc(q.scores_full, 1)
                lend([i], q.probs_ready)

            def weigh(b, j, k, tiles, vals, ready):
                i = 4 + 2 * (j % 2)
                if k == 0:
                    for bk in (i, i + 1):
                        pe.wait_ge(reader[bk], see.at(reader[bk], read_at[bk]))
                pe.wait_ge(q.probs_ready, see.at(q.probs_ready, ready))
                first, last = k == 0, k == tiles - 1
                for ones_too in range(1 + direct(b, j, tiles)):
                    for e in range(2):
                        h = 2 * j + e
                        lhs = vals[:, b * tiles + k, h * DH:(h + 1) * DH]
                        if ones_too:
                            lhs = once64[:, :] if tiles == 2 and k else ones64[:, :]
                        ins = mm(bank[i + ones_too][DH * e:DH * e + DH, :], lhs,
                                 ring[:, 2 * ((j * tiles + k) % 4) + e, :], start=first, stop=last)
                ins.then_inc(q.weighed, 1)
                see.expect(q.weighed)
                if last and direct(b, j, tiles):
                    lend([i, i + 1], q.heads_ready)

            def sum_up(b, j):
                u, i = b * PAIRS + j, 4 + 2 * (j % 2)
                pe.wait_ge(q.summed, see.next(q.summed, TB - 1))
                for e in range(2):
                    ins = mm(bank[i + 1][DH * e:DH * e + DH, :], ones64[:, :], acc[:, u % 2, e, :], start=True, stop=True)
                ins.then_inc(q.den_full, 1)
                see.expect(q.den_full)
                lend([i, i + 1], q.heads_ready)

            def pair_shifts_turn():
                shifts_turn(0, 2, q.shift_ready, q.shiftT_full, q.shiftT_ready)

            def cross_values(t):
                c0 = t // 2 * C + t % 2 * C2
                value_tile(ctxT[:, c0:c0 + P], cv, t % 2)

            def begin_cross(u, k):
                if (u, k) == (6, 0):
                    pe.wait_ge(q.w_cross, see.next(q.w_cross, 80))
                if (u, k) in ((6, 0), (6, 1), (6, 2), (7, 0)):
                    pair(ck, ckr, k if u == 6 else 3, ctxT[:, :], B * C, 0)
                elif u == 7:
                    cross_values(k - 1)

            def attend(maximum, tiles, kt, per_batch, step, vals, w):
                for u in range(UNITS):
                    b, j = u // PAIRS, u % PAIRS
                    pe.wait_ge(q.shiftT_ready, see.now(q.shiftT_ready))
                    swap = (q.swap0, q.swap1)[u % 2]
                    pe.wait_ge(swap, see.next(swap, 32))
                    for k in range(tiles):
                        before = see.n.get("probs_ready", 0)
                        for e in range(2):
                            scores(b, 2 * j + e, k, kt, per_batch, step)
                        if k == TURN[tiles] and u + 1 < UNITS:
                            pair_shifts_turn()
                        if u == 0 and k == 1:
                            pe.wait_ge(q.v_ready, see.now(q.v_ready))
                        if k:
                            weigh(b, j, k - 1, tiles, vals, before)
                        elif u:
                            weigh((u - 1) // PAIRS, (u - 1) % PAIRS, tiles - 1, tiles, vals, before)
                        if u == PAIRS and k == CONTRACT[tiles]:
                            pe.wait_ge(q.heads_ready, see.now(q.heads_ready))
                            contract(0, lambda c, t: AT[:, c, t * P:(t + 1) * P], w, PAIRS)
                        if u + 2 < UNITS:
                            for i in quota(tiles, k):
                                maximum(u + 2, i)
                        if tiles == TB:
                            begin_cross(u, k)
                        if u and k == 1 and not direct((u - 1) // PAIRS, (u - 1) % PAIRS, tiles):
                            sum_up((u - 1) // PAIRS, (u - 1) % PAIRS)
                weigh(B - 1, PAIRS - 1, tiles - 1, tiles, vals, see.n["probs_ready"])

            def contract_heads(w):
                pe.wait_ge(q.heads_ready, see.now(q.heads_ready))
                contract(1, lambda c, t: AT[:, c, t * P:(t + 1) * P], w, PAIRS)

            def by_parts(o, k, cols_, b):
                w = slice(b * S, (b + 1) * S)
                mm(o, wh[k][:, cols_], hTh[:, w], start=True, stop=False)
                mm(o, wh[k][:, cols_], hTl[:, w], start=False, stop=False)
                return mm(o, wl[k][:, cols_], hTh[:, w], start=False, stop=True)

            def contract(b, lhs, w, chunks):
                pe.wait_ge(reader[6 + b], see.at(reader[6 + b], read_at[6 + b]))
                for t in range(TB):
                    for k in range(chunks):
                        ins = mm(bank[6 + b][:, t * P:(t + 1) * P], lhs(k, b * TB + t), w[:, k, :], start=(k == 0),
                                 stop=(k == chunks - 1))
                ins.then_inc(q.out_full, 1)
                lend([6 + b], q.y_ready)

            see.expect(q.const, CONSTS)
            pe.wait_ge(q.const, see.now(q.const))
            pe.wait_ge(q.ctx_in, see.next(q.ctx_in, 16))
            for i in range(2 * B):
                ins = turn(bank[2][:, i * CH:(i + 1) * CH], cin[:, i, :], ident[0:CH, 0:CH])
            ins.then_inc(q.ctx_full, 1)
            lend([2], q.ctx_ready)
            pe.wait_ge(q.mask_ready, see.next(q.mask_ready))
            for k in range(2):
                for t in range(TB):
                    c0 = k * (S // 2) + t * P // 2
                    ins = turn(bank[3][:, c0:c0 + P // 2].bitcast(BF16), maskq[:, t, k * C2:k * C2 + P], identb[:, :])
            ins.then_inc(q.maskT_full, 1)
            lend([3], q.maskT_ready)

            inputs()
            pe.wait_ge(q.w_early, see.next(q.w_early, 32))
            pe.wait_ge(q.small_in, see.next(q.small_in, 144))
            for b in range(B):
                hT_wait(b)
                for k in range(3):
                    i = 3 * b + k
                    pe.wait_ge(reader[i], see.at(reader[i], read_at[i]))
                    mm(bank[i][:, :], wa[:, k, :], hT_of(b), start=True, stop=True).then_inc(q.lin_full, 1)
            for b in range(B):
                pe.wait_ge(q.lin_ready, see.next(q.lin_ready))
                pe.wait_ge(reader[6 + b], see.at(reader[6 + b], read_at[6 + b]))
                for t in range(TB):
                    o = bank[6 + b][:, t * P:(t + 1) * P]
                    mm(o, ones[:, :], rows[:, 0, :], start=True, stop=False)
                    ins = mm(o, o0T[:, b * S + t * P:b * S + (t + 1) * P], wa[:, 3, :], start=False, stop=True)
                ins.then_inc(q.gelu_full, 1)
                lend([6 + b], q.gelu_ready)
            see.expect(q.normed, 2)
            drain()

            with pe.Fori(0, LAYERS) as l:
                see.enter(l, LAYER)
                see.expect(q.w_small, 32)
                pe.wait_ge(q.w_self, see.next(q.w_self, 80))
                inputs()
                for b in range(B):
                    hT_wait(b)
                    low0 = see.n.get("qk_ready", 0)
                    for h in range(HEADS):
                        w, wr_ = (wk, wkr) if h < PAIRS else (wq, wqr)
                        pair(w, wr_, h % PAIRS, hT_of(b), S)
                        if b:
                            pe.wait_ge(q.qk_ready, see.at(q.qk_ready, PAIRS + h // PAIRS + 1 + low0))
                            if h == 6:
                                pair_shifts_turn()
                            for i in (2 * h, 2 * h + 1):
                                max_self(h // PAIRS, i % HEADS)
                            value_tile(hT_tile(h), wv, 6 + h % 2)
                see.expect(q.qk_ready, 4 * PAIRS)
                see.expect(q.rope_ready, 4 * PAIRS)
                pe.wait_ge(q.w_sout, see.next(q.w_sout, 16))
                attend(max_self, TB, KHL, S, P, Vs, wo)

                cross_values(3)
                input_of(0, 0)
                pe.wait_ge(q.hT_ready, see.now(q.hT_ready))
                for j in range(PAIRS):
                    pair(cq, cqr, j, hT_of(0), S)
                    if j == 1:
                        contract_heads(wo)
                queries0 = see.n["qk_ready"] + PAIRS
                input_of(1, 1)
                pe.wait_ge(q.hT_ready, see.now(q.hT_ready))
                for j in range(PAIRS):
                    pair(cq, cqr, j, hT_of(1), S)
                    pe.wait_ge(q.qk_ready, see.at(q.qk_ready, queries0 + j // 2 + 1))
                    if j == PAIRS - 1:
                        pair_shifts_turn()
                    for i in range(2):
                        max_cross(j // 2, j % 2 * 2 + i)
                see.expect(q.qk_ready, 3 * PAIRS)
                see.expect(q.rope_ready, 3 * PAIRS)
                pe.wait_ge(q.w_cout, see.next(q.w_cout, 16))
                attend(max_cross, 2, KHLc, C, C2, Vc, co)
                pe.wait_ge(q.w_ff1, see.next(q.w_ff1, 16))
                pe.wait_ge(q.w_ff2, see.next(q.w_ff2, 16))
                for b in range(B):
                    input_of(b, b)
                    pe.wait_ge(q.hT_ready, see.now(q.hT_ready))
                    for k in range(FCH):
                        pe.wait_ge(reader[2 + k], see.at(reader[2 + k], read_at[2 + k]))
                        mm(bank[2 + k][:, :], f1[:, k * P:(k + 1) * P], hT_of(b), start=True, stop=True)\
                            .then_inc(q.up_full, 1)
                        lend([2 + k], q.up_ready)
                    if b == 0:
                        contract_heads(co)
                    pe.wait_ge(q.up_ready, see.now(q.up_ready))
                    contract(b, lambda k, t: probs[:, b, k, (t % TB) * P:(t % TB + 1) * P], f2, FCH)
                drain()
                see.leave(LAYERS)
            see.expect(q.normed, 2)

            def router(w, bias):
                pe.wait_ge(reader[0], see.at(reader[0], read_at[0]))
                for t in range(TILES):
                    if t % TB == 0:
                        hT_wait(t // TB)
                    o = bank[0][:, t * E:(t + 1) * E]
                    ins = mm(o, hT_tile(t), w, start=True, stop=not bias)
                    if bias:
                        ins = mm(o, ones[:, :], lrow8[:, :], start=False, stop=True)
                ins.then_inc(q.router_full, 1)
                lend([0], q.logits_read)

            inputs()
            router(wr[:, 0, :], True)
            pe.wait_ge(q.gate_ready, see.next(q.gate_ready))
            for b in range(B):
                pe.wait_ge(reader[1 + b], see.at(reader[1 + b], read_at[1 + b]))
                for t in range(TB):
                    ins = turn(bank[1 + b][0:E, t * P:(t + 1) * P], gate0[:, b * TB + t, :], ident[:, :])
                ins.then_inc(q.gateT_full, 1)
                lend([1 + b], q.gateT_ready)
            for b in range(B):
                pe.wait_ge(q.gateT_ready, see.at(q.gateT_ready, b + 1))
                pe.wait_ge(reader[6 + b], see.at(reader[6 + b], read_at[6 + b]))
                for t in range(TB):
                    ins = mm(bank[6 + b][:, t * P:(t + 1) * P], gateT[:, b * S + t * P:b * S + (t + 1) * P], b2e[:, :],
                             start=True, stop=True)
                ins.then_inc(q.bias_full, 1)
                lend([6 + b], q.x_ready)
            drain()
            pe.wait_ge(q.split_ready, see.next(q.split_ready))
            with pe.Fori(0, E // 2) as i:
                see.enter(i, EXPERTS0)
                for k in range(2):
                    w = (q.w_expert0, q.w_expert1)[k]
                    pe.wait_ge(w, see.next(w, 48))
                    pe.wait_ge(q.split_ready, see.next(q.split_ready))
                    for b in range(B):
                        for j in range(F0CH):
                            pe.wait_ge(reader[2 + j], see.at(reader[2 + j], read_at[2 + j]))
                            by_parts(bank[2 + j][:, :], k, slice(j * P, (j + 1) * P), b).then_inc(q.moe_up_full, 1)
                            lend([2 + j], q.moe_up_ready)
                    for b in range(B):
                        pe.wait_ge(q.moe_up_ready, see.at(q.moe_up_ready, see.n["moe_up_ready"] - (B - 1 - b) * F0CH))
                        pe.wait_ge(reader[6 + b], see.at(reader[6 + b], read_at[6 + b]))
                        for t in range(TB):
                            for j in range(F0CH):
                                ins = mm(bank[6 + b][:, t * P:(t + 1) * P], probs[:, b, j, t * P:(t + 1) * P],
                                         ew2[k][:, j * D:(j + 1) * D], start=(j == 0), stop=(j == F0CH - 1))
                        ins.then_inc(q.moe_down_full, 1)
                        lend([6 + b], q.moe_x_ready)
                drain()
                see.leave(E // 2)

            pe.wait_ge(q.w_l1, see.next(q.w_l1, 64))
            inputs()
            for b in range(B):
                hT_wait(b)
                pe.wait_ge(reader[3], see.at(reader[3], read_at[3]))
                mm(bank[3][:, :], w1a[:, 3, :], hT_of(b), start=True, stop=True).then_inc(q.decay_full, 1)
                lend([3], q.log_ready)
                for k in range(2):
                    pe.wait_ge(reader[k], see.at(reader[k], read_at[k]))
                    mm(bank[k][:, :], w1a[:, k, :], hT_of(b), start=True, stop=True).then_inc(q.qkv_full, 1)
                    lend([k], q.qkv_ready)
                pe.wait_ge(reader[2], see.at(reader[2], read_at[2]))
                for t in range(TB):
                    ins = mm(bank[2][:, t * P:(t + 1) * P], hT_tile(b * TB + t), w1a[:, 2, :], start=True, stop=True)
                ins.then_inc(q.qkv_full, 1)
                lend([2], q.qkv_ready)
                pe.wait_ge(q.qkv_ready, see.now(q.qkv_ready))
                for j in range(TB):
                    pe.wait_ge(reader[4 + j % 2], see.at(reader[4 + j % 2], read_at[4 + j % 2]))
                    mm(bank[4 + j % 2][:, j * P:], k1T[:, b * S + j * P:b * S + (j + 1) * P],
                       q1T[:, b * S + j * P:(b + 1) * S], start=True, stop=True).then_inc(q.sc_full, 1)
                    lend([4 + j % 2], q.sc_ready)
                for t in range(TB):
                    pe.wait_ge(q.sc_ready, see.at(q.sc_ready, b * TB + t + 1))
                    pe.wait_ge(reader[6 + t % 2], see.at(reader[6 + t % 2], read_at[6 + t % 2]))
                    for j in range(t + 1):
                        ins = mm(bank[6 + t % 2][:, 0:D + 1], SC[:, j, t * P:(t + 1) * P], V1[:, b * TB + j, 0:D + 1],
                                 start=(j == 0), stop=(j == t))
                    ins.then_inc(q.num_full, 1)
                    lend([6 + t % 2], q.num_ready)

            inputs()
            for k in (0, 1, 2, 3, 4, 5):
                pe.wait_ge(reader[k], see.at(reader[k], read_at[k]))
            mm(bank[0][:, 0:B * C], w1x[:, 1, :], ctxT[:, :], start=True, stop=True).then_inc(q.xkq_full, 1)
            lend([0], q.parts_ready)
            for b in range(B):
                hT_wait(b)
                mm(bank[1 + b][:, :], w1x[:, 0, :], hT_of(b), start=True, stop=True).then_inc(q.xkq_full, 1)
                lend([1 + b], q.parts_ready)
            for i in range(2 * B):
                pe.wait_ge(reader[3 + i], see.at(reader[3 + i], read_at[3 + i]))
                c0 = i // 2 * C + i % 2 * C2
                mm(bank[3 + i][:, 0:D], ctxT[:, c0:c0 + P], w1x[:, 2, :], start=True, stop=True)\
                    .then_inc(q.xv_full, 1)
                lend([3 + i], q.xv_ready)
            pe.wait_ge(q.parts_in, see.next(q.parts_in, 16 * 2 * SPLITS))

            def xmax(b, n):
                t, h = n // (H1 // 2), n % (H1 // 2) * 2
                i = see.n.get("xm_done", 0) % 2
                pe.wait_ge(reader[i], see.at(reader[i], read_at[i]))
                for k in range(2):
                    o = bank[i][:, k * C:(k + 1) * C]
                    mm(o, Qst[:, h + k, b * S + t * P:b * S + (t + 1) * P], Kst[:, h + k, b * C:(b + 1) * C],
                       start=True, stop=False)
                    ins = mm(o, identb[:, :], maskq[:, t, :], start=False, stop=True)
                ins.then_inc(q.xm_full, 1)
                lend([i], q.xm_done)

            def xscores(b, u):
                for e in range(2):
                    for k in range(2):
                        pe.wait_ge(reader[2 + k], see.at(reader[2 + k], read_at[2 + k]))
                        c0 = b * C + k * C2
                        mm(bank[2 + k][:, :], Kst[:, 2 * u + e, c0:c0 + P], Qst[:, 2 * u + e, b * S:(b + 1) * S],
                           start=True, stop=False)
                        mm(bank[2 + k][:, :], identb[:, :], maskT[:, k, :], start=False, stop=True).then_inc(q.xs_full, 1)
                        lend([2 + k], q.xp_ready)

            def xweigh(b, u):
                g = u // 2
                if u % 2 == 0:
                    pe.wait_ge(reader[4 + g % 2], see.at(reader[4 + g % 2], read_at[4 + g % 2]))
                pe.wait_ge(q.xp_ready, 4 * (b * H1 // 2 + u + 1))
                for k in range(2):
                    for e in range(2):
                        j = u % 2 * 2 + e
                        ins = mm(bank[4 + g % 2][32 * j:32 * j + 32, :], Vx[:, 2 * b + k, 2 * u + e, :],
                                 ring[:, u % 2 * 4 + 2 * e + k, :], start=(k == 0), stop=(k == 1))
                ins.then_inc(q.xpv_full, 1)
                if u % 2:
                    lend([4 + g % 2], q.xo_ready)

            def xturn(b, g):
                pe.wait_ge(q.xo_ready, b * H1 // 4 + g + 1)
                pe.wait_ge(reader[6], see.at(reader[6], read_at[6]))
                for t in range(TB):
                    ins = turn(bank[6][:, t * P:(t + 1) * P], O4[g % 2][:, t * P:(t + 1) * P], ident[:, :])
                ins.then_inc(q.xt_full, 1)
                lend([6], q.xn_ready)

            def xgather():
                pe.wait_ge(q.xn_ready, see.now(q.xn_ready))
                for t in range(TB):
                    ins = turn(bank[6][:, t * P:(t + 1) * P], OX[:, t, :], ident[:, :])
                ins.then_inc(q.xo_full, 1)
                lend([6], q.xoT_ready)

            def xproject():
                pe.wait_ge(q.xoT_ready, see.now(q.xoT_ready))
                pe.wait_ge(reader[7], see.at(reader[7], read_at[7]))
                for t in range(TB):
                    o = bank[7][:, t * P:(t + 1) * P]
                    mm(o, ones[:, :], rows[:, 1, :], start=True, stop=False)
                    ins = mm(o, OXT[:, t * P:(t + 1) * P], w1x[:, 3, :], start=False, stop=True)
                ins.then_inc(q.xout_full, 1)
                lend([7], q.x_ready)

            for n in range(TB * H1 // 2):
                xmax(0, n)
            shifts_turn(0, H1, q.xsh_ready, q.xshT_full, q.xshT_ready)
            for b in range(B):
                w = (q.xsh_in0, q.xsh_in1)[b]
                pe.wait_ge(w, see.next(w, 16))
                for u in range(H1 // 2 + 1):
                    if u < H1 // 2:
                        xscores(b, u)
                    if b and u == 0:
                        xturn(0, H1 // 4 - 1)
                    if b and u == 1:
                        xgather()
                    if b and u == 2:
                        xproject()
                    if u >= 3 and u % 2:
                        xturn(b, (u - 3) // 2)
                    if u:
                        xweigh(b, u - 1)
                    if b == 0 and u < len(XQUOTA):
                        for n in range(sum(XQUOTA[:u]), sum(XQUOTA[:u + 1])):
                            xmax(1, n)
                    if b == 0 and u == XTURN:
                        shifts_turn(0, H1, q.xsh_ready, q.xshT_full, q.xshT_ready)
            xturn(1, H1 // 4 - 1)
            xgather()
            xproject()

            inputs()
            router(wr[:, 1, :], False)

            def glu(n, down):
                pe.wait_ge(q.split_ready, see.next(q.split_ready))
                for b in range(B):
                    for k in range(2):
                        pe.wait_ge(reader[2 * k], see.at(reader[2 * k], read_at[2 * k]))
                        by_parts(bank[2 * k][0:HP, :], n, slice(k * HP, (k + 1) * HP), b).then_inc(q.glu_gate_full, 1)
                        lend([2 * k], q.glu_act)
                        pe.wait_ge(reader[2 * k + 1], see.at(reader[2 * k + 1], read_at[2 * k + 1]))
                        by_parts(bank[2 * k + 1][0:HP, :], n, slice(HALF + k * HP, HALF + (k + 1) * HP), b)\
                            .then_inc(q.glu_up_full, 1)
                        lend([2 * k + 1], q.glu_ready)
                for b in range(B):
                    pe.wait_ge(q.glu_ready, see.at(q.glu_ready, see.n["glu_ready"] - (B - 1 - b) * 2))
                    pe.wait_ge(reader[6 + b], see.at(reader[6 + b], read_at[6 + b]))
                    for t in range(TB):
                        for k in range(2):
                            ins = mm(bank[6 + b][:, t * P:(t + 1) * P], GA[:, b, k, t * P:(t + 1) * P], down[:, k, :],
                                     start=(k == 0), stop=(k == 1))
                    ins.then_inc(q.glu_down_full, 1)
                    lend([6 + b], q.glu_x_ready)

            drain()
            pe.wait_ge(q.split_ready, see.next(q.split_ready))
            with pe.Fori(0, E // 2) as i:
                see.enter(i, EXPERTS1)
                for k in range(2):
                    w = (q.w_glu0, q.w_glu1)[k]
                    pe.wait_ge(w, see.next(w, 32))
                    glu(k, gdn[k])
                drain()
                see.leave(E // 2)
            glu(2, gdn[2])


def kernel(**inputs):
    import numpy as np
    import concourse.bacc as bacc
    from concourse.bass_utils import run_bass_kernel_spmd

    def arr(name):
        return np.ascontiguousarray(np.asarray(inputs[name]))

    def half_swapped(w):
        w = w.reshape(LAYERS, D, HEADS, DH)
        return np.concatenate([w[..., 16:32], w[..., 0:16], w[..., 32:]], axis=-1).reshape(LAYERS, D, INNER)

    l0 = {n: arr("L0_xattn_" + n) for n in ("sWq", "sWk", "sWv", "sWo", "cWq", "cWk", "cWv", "cWo", "fW1", "fW2")}
    for n in ("sWq", "sWk", "cWq", "cWk"):
        l0[n + "r"] = half_swapped(l0[n])
    gam = [arr("L0_xattn_" + n)[:, :, None] for n in ("sg", "cg", "fg")]
    fb1 = arr("L0_xattn_fb1").reshape(LAYERS, FCH, P).transpose(0, 2, 1)
    arrays = dict(
        x=arr("x"), ctx=arr("ctx_1024"),
        mask1=arr("mask_BxS_bf1"), mask1c=arr("mask_BxS_bf1").reshape(TILES, P).T, mask2=arr("mask_1x1xSxS2_bk1").reshape(S, C),
        wa=np.stack([arr("L0_attn_" + n) for n in ("wq", "wk", "wv", "wo")]),
        cols=np.stack([arr(n) for n in ("L0_attn_bq", "L0_attn_bk", "L0_attn_bv", "L1_attn_b_q", "L1_attn_b_k",
                                        "L1_attn_b_a", "L1_xattn_bq", "L1_xattn_bk")], axis=1),
        rows=np.stack([arr("L0_attn_bo"), arr("L1_xattn_bo"), arr("L1_xattn_bo")]),
        brow=np.stack([arr("L0_xattn_g_out"), arr("L1_attn_b_v"), arr("L1_xattn_bv")]),
        br=arr("L0_ffn_br"), wr=np.stack([arr("L0_ffn_Wr"), arr("L1_ffn_gate_w").T]),
        lcol=np.concatenate(gam + [fb1], axis=2),
        lrow=np.stack([arr("L0_xattn_" + n) for n in ("sbo", "cbo", "fb2")], axis=1),
        W1=arr("L0_ffn_W1"), W2=arr("L0_ffn_W2"), b2=arr("L0_ffn_b2"),
        b1=arr("L0_ffn_b1").reshape(E, F0CH, P).transpose(0, 2, 1),
        w1a=np.stack([arr("L1_attn_" + n).T for n in ("W_q", "W_k", "W_v", "W_a")]),
        w1x=np.stack([arr("L1_xattn_" + n).T for n in ("Wq", "Wk", "Wv", "Wo")]),
        wup=arr("L1_ffn_w_up").transpose(0, 2, 1), wdn=arr("L1_ffn_w_down").transpose(0, 2, 1),
        sgu=np.concatenate([arr("L1_ffn_sg_gate").T, arr("L1_ffn_sg_up").T], axis=1), sgd=arr("L1_ffn_sg_down").T,
        **l0)

    rotd = 32
    inv = (1.0 / 10000.0 ** (np.arange(0, rotd, 2, dtype=np.float32) / np.float32(rotd))).astype(np.float32)
    ang = (np.arange(S, dtype=np.float32)[:, None] * inv[None, :]).astype(np.float32)
    cos, sin = np.cos(ang).T.astype(np.float32), np.sin(ang).T.astype(np.float32)
    one = np.concatenate([cos, cos, np.ones((DH - rotd, S), np.float32)])
    two = np.concatenate([-sin, sin, np.zeros((DH - rotd, S), np.float32)])
    arrays["cos"], arrays["sin"] = np.concatenate([one, one]), np.concatenate([two, two])
    arrays["tri8"] = np.tril(np.ones((E, E), np.float32))
    sel = np.zeros((2, 2, 2, P), np.float32)
    for h in range(2):
        sel[:, h, h, :] = 1.0
    import ml_dtypes
    arrays["sel"] = sel.reshape(4, 2, P).astype(ml_dtypes.bfloat16)

    nc = bacc.Bacc("TRN2", target_bir_lowering=False, num_devices=1)
    nc.disable_value_cache = True
    feeds, aps = {}, {}
    for name, v in arrays.items():
        v = np.ascontiguousarray(v)
        feeds["in_" + name] = v
        aps[name] = nc.dram_tensor("in_" + name, v.shape, mybir.dt.from_np(v.dtype), kind="ExternalInput").ap()
    out = nc.dram_tensor("out_x", (B, S, D), F32, kind="ExternalOutput").ap()
    decoder(nc, aps, out)
    r = run_bass_kernel_spmd(nc, [feeds], core_ids=[0])
    return r.results[0]["out_x"]
```
